# Optimizing a Trainium2 kernel written in Bass

```python
import numpy as np
import jax
import jax.numpy as jnp

def _softmax(x, axis=-1):
    return jax.nn.softmax(x, axis=axis)

def _gelu(x):
    return jax.nn.gelu(x, approximate=True)

def _silu(x):
    return jax.nn.silu(x)

def _sigmoid(x):
    return jax.nn.sigmoid(x)

def _layernorm(x, axis=-1, eps=1e-05):
    m = jnp.mean(x, axis=axis, keepdims=True)
    v = jnp.var(x, axis=axis, keepdims=True)
    return (x - m) / jnp.sqrt(v + eps)

def _scatter_add(tgt, idx, src, axis=0):
    return tgt.at[idx].add(src)

def _segment_sum(src, seg, n):
    return jax.ops.segment_sum(src, seg, n)
kernel_name = 'mk_early_fusion_d1_tok_img768_r4_623f56'

def setup_inputs(seed: int=0):
    np.random.seed(seed)
    _w = jnp.asarray

    def _rec_inputs():
        import jax
        import jax.numpy as jnp
        _rk = jax.random.key(seed)
        x = 7.57192e-06 + 1.00007 * jax.random.normal(jax.random.fold_in(_rk, 1), (32, 3, 112, 112), jnp.float32)
        txt = -6.31349e-07 + 0.985278 * jax.random.normal(jax.random.fold_in(_rk, 2), (32, 32, 192), jnp.float32)
        return (x, txt)
    x, txt = _rec_inputs()

    def _L0_tok_setup():
        import jax, jax.numpy as jnp
        import numpy as np
        B, IN, IMG = (64, 3, 224)
        PATCH, LEVELS, D = (16, 4, 192)
        ISQ2 = 0.7071067811865476
        DN = ('NCHW', 'OIHW', 'NCHW')

        def conv(x, w, b=None, stride=1, pad=((0, 0), (0, 0)), groups=1):
            y = jax.lax.conv_general_dilated(x, w, (stride, stride), pad, dimension_numbers=DN, feature_group_count=groups)
            return y if b is None else y + b[None, :, None, None]

        def dwconv(x, wd, wp, bp):
            y = conv(x, wd, pad=((1, 1), (1, 1)), groups=x.shape[1])
            return conv(y, wp, bp)

        def haar_dwt2(x):
            xe, xo = (x[..., ::2], x[..., 1::2])
            lo_w, hi_w = ((xe + xo) * ISQ2, (xe - xo) * ISQ2)

            def split_h(t):
                te, to = (t[..., ::2, :], t[..., 1::2, :])
                return ((te + to) * ISQ2, (te - to) * ISQ2)
            ll, lh = split_h(lo_w)
            hl, hh = split_h(hi_w)
            return (ll, lh, hl, hh)

        def wavelet_packet(x):
            f = x
            for _ in range(LEVELS):
                b, k, h, w = f.shape
                ll, lh, hl, hh = haar_dwt2(f)
                bands = jnp.stack([ll, lh, hl, hh], axis=1)
                bands = bands.reshape(b, 4, k // IN, IN, h // 2, w // 2)
                f = jnp.transpose(bands, (0, 2, 1, 3, 4, 5)).reshape(b, 4 * k, h // 2, w // 2)
            return f

        def gelu(x):
            return jax.nn.gelu(x, approximate=False)

        def forward(x, pl_w, pl_b, pl_dw, pl_pw, pl_pwb, pg_w1, pg_b1, pg_dw, pg_pw, pg_pwb, pg_w2, pg_b2, alpha, f1_dw, f1_pw, f1_pwb, f2_dw, f2_pw, f2_pwb, f3_dw, f3_pw, f3_pwb, ln_g, ln_b, cls):
            loc = conv(x, pl_w, pl_b, stride=PATCH)
            loc = dwconv(gelu(loc), pl_dw, pl_pw, pl_pwb)
            g = wavelet_packet(x)
            g = gelu(conv(g, pg_w1, pg_b1))
            g = gelu(dwconv(g, pg_dw, pg_pw, pg_pwb))
            glob = conv(g, pg_w2, pg_b2)
            gate = 0.5 * (jnp.tanh(alpha) + 1.0)
            h = (1.0 - gate) * loc + gate * glob
            h = jax.nn.relu(dwconv(h, f1_dw, f1_pw, f1_pwb))
            h = jax.nn.relu(dwconv(h, f2_dw, f2_pw, f2_pwb))
            h = dwconv(loc + h, f3_dw, f3_pw, f3_pwb)
            t = jnp.transpose(h.reshape(h.shape[0], D, -1), (0, 2, 1))
            mu = jnp.mean(t, -1, keepdims=True)
            var = jnp.mean((t - mu) ** 2, -1, keepdims=True)
            t = (t - mu) / jnp.sqrt(var + 1e-05) * ln_g + ln_b
            cls_tok = jnp.broadcast_to(cls, (t.shape[0], 1, D))
            return jnp.concatenate([cls_tok, t], axis=1)
        key = jax.random.key(seed)
        ks = jax.random.split(key, 32)

        def rn(i, shape, s=0.02):
            return jax.random.normal(ks[i], shape, jnp.float32) * s
        KW = IN * 4 ** LEVELS
        return {'x': jax.random.normal(ks[0], (B, IN, IMG, IMG), jnp.float32), 'pl_w': rn(1, (D, IN, PATCH, PATCH)), 'pl_b': rn(2, (D,)), 'pl_dw': rn(3, (D, 1, 3, 3)), 'pl_pw': rn(4, (D, D, 1, 1)), 'pl_pwb': rn(5, (D,)), 'pg_w1': rn(6, (D, KW, 1, 1)), 'pg_b1': rn(7, (D,)), 'pg_dw': rn(8, (D, 1, 3, 3)), 'pg_pw': rn(9, (D, D, 1, 1)), 'pg_pwb': rn(10, (D,)), 'pg_w2': rn(11, (D, D, 1, 1)), 'pg_b2': rn(12, (D,)), 'alpha': jnp.zeros((1, D, 1, 1), jnp.float32), 'f1_dw': rn(13, (D, 1, 3, 3)), 'f1_pw': rn(14, (D, D, 1, 1)), 'f1_pwb': rn(15, (D,)), 'f2_dw': rn(16, (D, 1, 3, 3)), 'f2_pw': rn(17, (D, D, 1, 1)), 'f2_pwb': rn(18, (D,)), 'f3_dw': rn(19, (D, 1, 3, 3)), 'f3_pw': rn(20, (D, D, 1, 1)), 'f3_pwb': rn(21, (D,)), 'ln_g': jnp.ones((D,), jnp.float32), 'ln_b': jnp.zeros((D,), jnp.float32), 'cls': rn(22, (1, 1, D))}
    _L0_tok_all = _L0_tok_setup()
    _L0_tok_in = {k: v for k, v in _L0_tok_all.items() if k in ('pl_w', 'pl_b', 'pl_dw', 'pl_pw', 'pl_pwb', 'pg_w1', 'pg_b1', 'pg_dw', 'pg_pw', 'pg_pwb', 'pg_w2', 'pg_b2', 'alpha', 'f1_dw', 'f1_pw', 'f1_pwb', 'f2_dw', 'f2_pw', 'f2_pwb', 'f3_dw', 'f3_pw', 'f3_pwb', 'ln_g', 'ln_b', 'cls')}
    del _L0_tok_all

    def _L0_attn_setup():
        import jax, jax.numpy as jnp
        import numpy as np
        D_MODEL = 192
        D_INNER = 384
        D_STATE = 16
        DT_RANK = 96
        H_FFN = 512
        B, L = (1, 512)
        EPS = 1e-06

        def rmsnorm(x, w):
            return x * jax.lax.rsqrt(jnp.mean(x * x, axis=-1, keepdims=True) + EPS) * w

        def selective_scan(z, W_xproj, W_dt, b_dt, A_log, D_skip):
            xdbl = jnp.einsum('bld,kd->blk', z, W_xproj)
            dt_in, Bm, Cm = jnp.split(xdbl, [DT_RANK, DT_RANK + D_STATE], axis=-1)
            dt = jax.nn.softplus(jnp.einsum('blr,dr->bld', dt_in, W_dt) + b_dt)
            A = -jnp.exp(A_log)
            A_bar = jnp.exp(dt[..., None] * A)
            Bx = (dt * z)[..., None] * Bm[:, :, None, :]

            def comb(e1, e2):
                a1, b1 = e1
                a2, b2 = e2
                return (a1 * a2, a2 * b1 + b2)
            _, h = jax.lax.associative_scan(comb, (A_bar, Bx), axis=1)
            y = jnp.einsum('blds,bls->bld', h, Cm) + D_skip * z
            return y
        key = jax.random.key(seed)
        ks = jax.random.split(key, 10)
        s = lambda k, shape, scale=0.02: jax.random.normal(k, shape, dtype=jnp.float32) * scale
        return {'x': jax.random.normal(ks[0], (B, L, D_MODEL), dtype=jnp.float32), 'w_norm1': jnp.ones((D_MODEL,), jnp.float32), 'W_in': s(ks[1], (D_INNER, D_MODEL)), 'W_gate': s(ks[2], (D_INNER, D_MODEL)), 'W_xproj': s(ks[3], (DT_RANK + 2 * D_STATE, D_INNER)), 'W_dt': s(ks[4], (D_INNER, DT_RANK)), 'b_dt': jnp.full((D_INNER,), -4.6, jnp.float32), 'A_log': jnp.log(jnp.tile(jnp.arange(1, D_STATE + 1, dtype=jnp.float32), (D_INNER, 1))), 'D_skip': jnp.ones((D_INNER,), jnp.float32), 'W_out': s(ks[5], (D_MODEL, D_INNER)), 'w_ffn_norm': jnp.ones((D_MODEL,), jnp.float32), 'W_up': s(ks[6], (H_FFN, D_MODEL)), 'W_gate_ffn': s(ks[7], (H_FFN, D_MODEL)), 'W_down': s(ks[8], (D_MODEL, H_FFN))}
    _L0_attn_all = _L0_attn_setup()
    _L0_attn_in = {k: v for k, v in _L0_attn_all.items() if k in ('w_norm1', 'W_in', 'W_gate', 'W_xproj', 'W_dt', 'b_dt', 'A_log', 'D_skip', 'W_out', 'w_ffn_norm', 'W_up', 'W_gate_ffn', 'W_down')}
    del _L0_attn_all

    def _L0_ffn_setup():
        import jax, jax.numpy as jnp
        import numpy as np
        EPS = 1e-05

        def _ln(x, g, b):
            m = jnp.mean(x, axis=-1, keepdims=True)
            v = jnp.mean((x - m) ** 2, axis=-1, keepdims=True)
            return (x - m) / jnp.sqrt(v + EPS) * g + b
        key = jax.random.key(seed)
        ks = jax.random.split(key, 16)
        B, S, D, H, E, K = (32, 128, 192, 12, 8, 2)
        Dff = 4 * D
        s = 0.02
        return {'x': jax.random.normal(ks[0], (B, S, D), dtype=jnp.float32), 'ln1_g': jnp.ones((D,), jnp.float32), 'ln1_b': jnp.zeros((D,), jnp.float32), 'in_proj_w': jax.random.normal(ks[1], (3 * D, D), jnp.float32) * s, 'in_proj_b': jnp.zeros((3 * D,), jnp.float32), 'out_proj_w': jax.random.normal(ks[2], (D, D), jnp.float32) * s, 'out_proj_b': jnp.zeros((D,), jnp.float32), 'ln2_g': jnp.ones((D,), jnp.float32), 'ln2_b': jnp.zeros((D,), jnp.float32), 'router_w': jax.random.normal(ks[3], (E, D), jnp.float32) * s, 'router_b': jnp.zeros((E,), jnp.float32), 'w1': jax.random.normal(ks[4], (E, D, Dff), jnp.float32) * s, 'b1': jnp.zeros((E, Dff), jnp.float32), 'w2': jax.random.normal(ks[5], (E, Dff, D), jnp.float32) * s, 'b2': jnp.zeros((E, D), jnp.float32)}
    _L0_ffn_all = _L0_ffn_setup()
    _L0_ffn_in = {k: v for k, v in _L0_ffn_all.items() if k in ('ln1_g', 'ln1_b', 'in_proj_w', 'in_proj_b', 'out_proj_w', 'out_proj_b', 'ln2_g', 'ln2_b', 'router_w', 'router_b', 'w1', 'b1', 'w2', 'b2')}
    del _L0_ffn_all
    return {'x': x, 'txt': txt, 'L0_tok_pl_w': _L0_tok_in['pl_w'], 'L0_tok_pl_b': _L0_tok_in['pl_b'], 'L0_tok_pl_dw': _L0_tok_in['pl_dw'], 'L0_tok_pl_pw': _L0_tok_in['pl_pw'], 'L0_tok_pl_pwb': _L0_tok_in['pl_pwb'], 'L0_tok_pg_w1': _L0_tok_in['pg_w1'], 'L0_tok_pg_b1': _L0_tok_in['pg_b1'], 'L0_tok_pg_dw': _L0_tok_in['pg_dw'], 'L0_tok_pg_pw': _L0_tok_in['pg_pw'], 'L0_tok_pg_pwb': _L0_tok_in['pg_pwb'], 'L0_tok_pg_w2': _L0_tok_in['pg_w2'], 'L0_tok_pg_b2': _L0_tok_in['pg_b2'], 'L0_tok_alpha': _L0_tok_in['alpha'], 'L0_tok_f1_dw': _L0_tok_in['f1_dw'], 'L0_tok_f1_pw': _L0_tok_in['f1_pw'], 'L0_tok_f1_pwb': _L0_tok_in['f1_pwb'], 'L0_tok_f2_dw': _L0_tok_in['f2_dw'], 'L0_tok_f2_pw': _L0_tok_in['f2_pw'], 'L0_tok_f2_pwb': _L0_tok_in['f2_pwb'], 'L0_tok_f3_dw': _L0_tok_in['f3_dw'], 'L0_tok_f3_pw': _L0_tok_in['f3_pw'], 'L0_tok_f3_pwb': _L0_tok_in['f3_pwb'], 'L0_tok_ln_g': _L0_tok_in['ln_g'], 'L0_tok_ln_b': _L0_tok_in['ln_b'], 'L0_tok_cls': _L0_tok_in['cls'], 'L0_attn_w_norm1': _L0_attn_in['w_norm1'], 'L0_attn_W_in': _L0_attn_in['W_in'], 'L0_attn_W_gate': _L0_attn_in['W_gate'], 'L0_attn_W_xproj': _L0_attn_in['W_xproj'], 'L0_attn_W_dt': _L0_attn_in['W_dt'], 'L0_attn_b_dt': _L0_attn_in['b_dt'], 'L0_attn_A_log': _L0_attn_in['A_log'], 'L0_attn_D_skip': _L0_attn_in['D_skip'], 'L0_attn_W_out': _L0_attn_in['W_out'], 'L0_attn_w_ffn_norm': _L0_attn_in['w_ffn_norm'], 'L0_attn_W_up': _L0_attn_in['W_up'], 'L0_attn_W_gate_ffn': _L0_attn_in['W_gate_ffn'], 'L0_attn_W_down': _L0_attn_in['W_down'], 'L0_ffn_ln1_g': _L0_ffn_in['ln1_g'], 'L0_ffn_ln1_b': _L0_ffn_in['ln1_b'], 'L0_ffn_in_proj_w': _L0_ffn_in['in_proj_w'], 'L0_ffn_in_proj_b': _L0_ffn_in['in_proj_b'], 'L0_ffn_out_proj_w': _L0_ffn_in['out_proj_w'], 'L0_ffn_out_proj_b': _L0_ffn_in['out_proj_b'], 'L0_ffn_ln2_g': _L0_ffn_in['ln2_g'], 'L0_ffn_ln2_b': _L0_ffn_in['ln2_b'], 'L0_ffn_router_w': _L0_ffn_in['router_w'], 'L0_ffn_router_b': _L0_ffn_in['router_b'], 'L0_ffn_w1': _L0_ffn_in['w1'], 'L0_ffn_b1': _L0_ffn_in['b1'], 'L0_ffn_w2': _L0_ffn_in['w2'], 'L0_ffn_b2': _L0_ffn_in['b2']}

def reference(x, txt, L0_tok_pl_w, L0_tok_pl_b, L0_tok_pl_dw, L0_tok_pl_pw, L0_tok_pl_pwb, L0_tok_pg_w1, L0_tok_pg_b1, L0_tok_pg_dw, L0_tok_pg_pw, L0_tok_pg_pwb, L0_tok_pg_w2, L0_tok_pg_b2, L0_tok_alpha, L0_tok_f1_dw, L0_tok_f1_pw, L0_tok_f1_pwb, L0_tok_f2_dw, L0_tok_f2_pw, L0_tok_f2_pwb, L0_tok_f3_dw, L0_tok_f3_pw, L0_tok_f3_pwb, L0_tok_ln_g, L0_tok_ln_b, L0_tok_cls, L0_attn_w_norm1, L0_attn_W_in, L0_attn_W_gate, L0_attn_W_xproj, L0_attn_W_dt, L0_attn_b_dt, L0_attn_A_log, L0_attn_D_skip, L0_attn_W_out, L0_attn_w_ffn_norm, L0_attn_W_up, L0_attn_W_gate_ffn, L0_attn_W_down, L0_ffn_ln1_g, L0_ffn_ln1_b, L0_ffn_in_proj_w, L0_ffn_in_proj_b, L0_ffn_out_proj_w, L0_ffn_out_proj_b, L0_ffn_ln2_g, L0_ffn_ln2_b, L0_ffn_router_w, L0_ffn_router_b, L0_ffn_w1, L0_ffn_b1, L0_ffn_w2, L0_ffn_b2):
    import jax
    import jax.numpy as jnp

    def _L0_tok_ref(x, pl_w, pl_b, pl_dw, pl_pw, pl_pwb, pg_w1, pg_b1, pg_dw, pg_pw, pg_pwb, pg_w2, pg_b2, alpha, f1_dw, f1_pw, f1_pwb, f2_dw, f2_pw, f2_pwb, f3_dw, f3_pw, f3_pwb, ln_g, ln_b, cls):
        import jax, jax.numpy as jnp
        import numpy as np
        B, IN, IMG = (64, 3, 224)
        PATCH, LEVELS, D = (16, 4, 192)
        ISQ2 = 0.7071067811865476
        DN = ('NCHW', 'OIHW', 'NCHW')

        def conv(x, w, b=None, stride=1, pad=((0, 0), (0, 0)), groups=1):
            y = jax.lax.conv_general_dilated(x, w, (stride, stride), pad, dimension_numbers=DN, feature_group_count=groups)
            return y if b is None else y + b[None, :, None, None]

        def dwconv(x, wd, wp, bp):
            y = conv(x, wd, pad=((1, 1), (1, 1)), groups=x.shape[1])
            return conv(y, wp, bp)

        def haar_dwt2(x):
            xe, xo = (x[..., ::2], x[..., 1::2])
            lo_w, hi_w = ((xe + xo) * ISQ2, (xe - xo) * ISQ2)

            def split_h(t):
                te, to = (t[..., ::2, :], t[..., 1::2, :])
                return ((te + to) * ISQ2, (te - to) * ISQ2)
            ll, lh = split_h(lo_w)
            hl, hh = split_h(hi_w)
            return (ll, lh, hl, hh)

        def wavelet_packet(x):
            f = x
            for _ in range(LEVELS):
                b, k, h, w = f.shape
                ll, lh, hl, hh = haar_dwt2(f)
                bands = jnp.stack([ll, lh, hl, hh], axis=1)
                bands = bands.reshape(b, 4, k // IN, IN, h // 2, w // 2)
                f = jnp.transpose(bands, (0, 2, 1, 3, 4, 5)).reshape(b, 4 * k, h // 2, w // 2)
            return f

        def gelu(x):
            return jax.nn.gelu(x, approximate=False)

        def forward(x, pl_w, pl_b, pl_dw, pl_pw, pl_pwb, pg_w1, pg_b1, pg_dw, pg_pw, pg_pwb, pg_w2, pg_b2, alpha, f1_dw, f1_pw, f1_pwb, f2_dw, f2_pw, f2_pwb, f3_dw, f3_pw, f3_pwb, ln_g, ln_b, cls):
            loc = conv(x, pl_w, pl_b, stride=PATCH)
            loc = dwconv(gelu(loc), pl_dw, pl_pw, pl_pwb)
            g = wavelet_packet(x)
            g = gelu(conv(g, pg_w1, pg_b1))
            g = gelu(dwconv(g, pg_dw, pg_pw, pg_pwb))
            glob = conv(g, pg_w2, pg_b2)
            gate = 0.5 * (jnp.tanh(alpha) + 1.0)
            h = (1.0 - gate) * loc + gate * glob
            h = jax.nn.relu(dwconv(h, f1_dw, f1_pw, f1_pwb))
            h = jax.nn.relu(dwconv(h, f2_dw, f2_pw, f2_pwb))
            h = dwconv(loc + h, f3_dw, f3_pw, f3_pwb)
            t = jnp.transpose(h.reshape(h.shape[0], D, -1), (0, 2, 1))
            mu = jnp.mean(t, -1, keepdims=True)
            var = jnp.mean((t - mu) ** 2, -1, keepdims=True)
            t = (t - mu) / jnp.sqrt(var + 1e-05) * ln_g + ln_b
            cls_tok = jnp.broadcast_to(cls, (t.shape[0], 1, D))
            return jnp.concatenate([cls_tok, t], axis=1)
        return forward(x, pl_w, pl_b, pl_dw, pl_pw, pl_pwb, pg_w1, pg_b1, pg_dw, pg_pw, pg_pwb, pg_w2, pg_b2, alpha, f1_dw, f1_pw, f1_pwb, f2_dw, f2_pw, f2_pwb, f3_dw, f3_pw, f3_pwb, ln_g, ln_b, cls)

    def _L0_attn_ref(x, w_norm1, W_in, W_gate, W_xproj, W_dt, b_dt, A_log, D_skip, W_out, w_ffn_norm, W_up, W_gate_ffn, W_down):
        import jax, jax.numpy as jnp
        import numpy as np
        D_MODEL = 192
        D_INNER = 384
        D_STATE = 16
        DT_RANK = 96
        H_FFN = 512
        B, L = (1, 512)
        EPS = 1e-06

        def rmsnorm(x, w):
            return x * jax.lax.rsqrt(jnp.mean(x * x, axis=-1, keepdims=True) + EPS) * w

        def selective_scan(z, W_xproj, W_dt, b_dt, A_log, D_skip):
            xdbl = jnp.einsum('bld,kd->blk', z, W_xproj)
            dt_in, Bm, Cm = jnp.split(xdbl, [DT_RANK, DT_RANK + D_STATE], axis=-1)
            dt = jax.nn.softplus(jnp.einsum('blr,dr->bld', dt_in, W_dt) + b_dt)
            A = -jnp.exp(A_log)
            A_bar = jnp.exp(dt[..., None] * A)
            Bx = (dt * z)[..., None] * Bm[:, :, None, :]

            def comb(e1, e2):
                a1, b1 = e1
                a2, b2 = e2
                return (a1 * a2, a2 * b1 + b2)
            _, h = jax.lax.associative_scan(comb, (A_bar, Bx), axis=1)
            y = jnp.einsum('blds,bls->bld', h, Cm) + D_skip * z
            return y
        residual = x
        h = rmsnorm(x, w_norm1)
        z = h @ W_in.T
        z = z * jax.nn.sigmoid(h @ W_gate.T)
        y = selective_scan(z, W_xproj, W_dt, b_dt, A_log, D_skip)
        x = residual + y @ W_out.T
        hf = rmsnorm(x, w_ffn_norm)
        ffn = jax.nn.silu(hf @ W_gate_ffn.T) * (hf @ W_up.T) @ W_down.T
        return x + ffn

    def _L0_ffn_ref(x, ln1_g, ln1_b, in_proj_w, in_proj_b, out_proj_w, out_proj_b, ln2_g, ln2_b, router_w, router_b, w1, b1, w2, b2):
        import jax, jax.numpy as jnp
        import numpy as np
        EPS = 1e-05

        def _ln(x, g, b):
            m = jnp.mean(x, axis=-1, keepdims=True)
            v = jnp.mean((x - m) ** 2, axis=-1, keepdims=True)
            return (x - m) / jnp.sqrt(v + EPS) * g + b
        B, S, D = x.shape
        H = 12
        Dh = D // H
        E = router_w.shape[0]
        K = 2
        x2 = _ln(x, ln1_g, ln1_b)
        qkv = x2 @ in_proj_w.T + in_proj_b
        q, k, v = jnp.split(qkv, 3, axis=-1)
        q = q.reshape(B, S, H, Dh)
        k = k.reshape(B, S, H, Dh)
        v = v.reshape(B, S, H, Dh)
        scores = jnp.einsum('bqhd,bkhd->bhqk', q, k) / jnp.sqrt(jnp.float32(Dh))
        attn = jax.nn.softmax(scores, axis=-1)
        ao = jnp.einsum('bhqk,bkhd->bqhd', attn, v).reshape(B, S, D)
        ao = ao @ out_proj_w.T + out_proj_b
        x = x + ao
        xm = _ln(x, ln2_g, ln2_b).reshape(B * S, D)
        T = B * S
        logits = xm @ router_w.T + router_b
        probs = jax.nn.softmax(logits, axis=-1)
        topw, topi = jax.lax.top_k(probs, K)
        topw = topw / jnp.sum(topw, axis=-1, keepdims=True)
        combine = jnp.zeros((T, E), xm.dtype).at[jnp.arange(T)[:, None], topi].add(topw)
        out = jnp.zeros_like(xm)
        for e in range(E):
            h = jax.nn.gelu(xm @ w1[e] + b1[e], approximate=False)
            y = h @ w2[e] + b2[e]
            out = out + combine[:, e:e + 1] * y
        x = x + out.reshape(B, S, D)
        return x
    h = _L0_tok_ref(x, L0_tok_pl_w, L0_tok_pl_b, L0_tok_pl_dw, L0_tok_pl_pw, L0_tok_pl_pwb, L0_tok_pg_w1, L0_tok_pg_b1, L0_tok_pg_dw, L0_tok_pg_pw, L0_tok_pg_pwb, L0_tok_pg_w2, L0_tok_pg_b2, L0_tok_alpha, L0_tok_f1_dw, L0_tok_f1_pw, L0_tok_f1_pwb, L0_tok_f2_dw, L0_tok_f2_pw, L0_tok_f2_pwb, L0_tok_f3_dw, L0_tok_f3_pw, L0_tok_f3_pwb, L0_tok_ln_g, L0_tok_ln_b, L0_tok_cls)
    h = jnp.concatenate([h, txt], axis=1)
    h = h + _L0_attn_ref(_layernorm(h, axis=-1), L0_attn_w_norm1, L0_attn_W_in, L0_attn_W_gate, L0_attn_W_xproj, L0_attn_W_dt, L0_attn_b_dt, L0_attn_A_log, L0_attn_D_skip, L0_attn_W_out, L0_attn_w_ffn_norm, L0_attn_W_up, L0_attn_W_gate_ffn, L0_attn_W_down)
    h = h + _L0_ffn_ref(_layernorm(h, axis=-1), L0_ffn_ln1_g, L0_ffn_ln1_b, L0_ffn_in_proj_w, L0_ffn_in_proj_b, L0_ffn_out_proj_w, L0_ffn_out_proj_b, L0_ffn_ln2_g, L0_ffn_ln2_b, L0_ffn_router_w, L0_ffn_router_b, L0_ffn_w1, L0_ffn_b1, L0_ffn_w2, L0_ffn_b2)
    return h

_drawn_inputs = setup_inputs


def setup_inputs(seed=0):
    import zlib

    import numpy as np

    out = dict(_drawn_inputs(seed))
    spreads = {'L0_tok_alpha': (0.0, 0.8),
     'L0_tok_ln_g': (1.0, 0.2),
     'L0_tok_ln_b': (0.0, 0.1),
     'L0_attn_w_norm1': (1.0, 0.6),
     'L0_attn_b_dt': (-4.599999904632568, 0.6),
     'L0_attn_D_skip': (1.0, 0.6),
     'L0_attn_w_ffn_norm': (1.0, 0.6),
     'L0_ffn_ln1_g': (1.0, 0.6),
     'L0_ffn_ln1_b': (0.0, 0.8),
     'L0_ffn_in_proj_b': (0.0, 0.8),
     'L0_ffn_out_proj_b': (0.0, 0.644),
     'L0_ffn_ln2_g': (1.0, 0.6),
     'L0_ffn_ln2_b': (0.0, 2.0),
     'L0_ffn_router_b': (0.0, 0.8),
     'L0_ffn_b1': (0.0, 2.0),
     'L0_ffn_b2': (0.0, 1.076)}
    factors = {'x': 8.0,
     'L0_tok_pl_w': 8.0,
     'L0_tok_pl_b': 64.0,
     'L0_tok_pl_dw': 8.0,
     'L0_tok_pl_pw': 8.0,
     'L0_tok_pl_pwb': 38.88,
     'L0_tok_pg_w1': 8.0,
     'L0_tok_pg_b1': 188.788,
     'L0_tok_pg_dw': 8.0,
     'L0_tok_pg_pw': 8.0,
     'L0_tok_pg_pwb': 64.0,
     'L0_tok_pg_w2': 8.0,
     'L0_tok_pg_b2': 200.0,
     'L0_tok_f1_dw': 8.0,
     'L0_tok_f1_pw': 8.0,
     'L0_tok_f1_pwb': 64.0,
     'L0_tok_f2_dw': 8.0,
     'L0_tok_f2_pw': 8.0,
     'L0_tok_f2_pwb': 64.0,
     'L0_tok_f3_dw': 3.345,
     'L0_tok_f3_pw': 3.923,
     'L0_attn_W_gate': 8.0,
     'L0_attn_W_xproj': 8.0,
     'L0_attn_W_dt': 8.0,
     'L0_attn_A_log': 130.578,
     'L0_attn_W_up': 5.361,
     'L0_attn_W_gate_ffn': 5.73,
     'L0_attn_W_down': 5.503,
     'L0_ffn_in_proj_w': 3.378,
     'L0_ffn_out_proj_w': 3.181,
     'L0_ffn_w1': 2.916,
     'L0_tok_f3_pwb': 8.0,
     'L0_ffn_router_w': 3.73}
    for name, (base, spread) in spreads.items():
        noise = np.random.default_rng([zlib.crc32(name.encode()), seed]).standard_normal(out[name].shape)
        drawn = base * np.exp(spread * noise) if base else spread * noise
        out[name] = jnp.asarray(drawn.astype(out[name].dtype))
    for name, factor in factors.items():
        out[name] = (out[name] * factor).astype(out[name].dtype)
    return out
```

```python
from contextlib import ExitStack

import numpy as np

import concourse.bass as bass
from concourse import mybir

F32 = mybir.dt.float32
BF16 = mybir.dt.bfloat16
I32 = mybir.dt.int32
ALU = mybir.AluOpType
ACT = mybir.ActivationFunctionType
AX = mybir.AxisListType

B = 32
D = 192
HD = D // 2
GRID = 7
PATCHES = GRID * GRID
TXT = 32
S = 1 + PATCHES + TXT
PIX = 256
KW = 3 * PIX
KT = KW // 128
BANK = 512


class Own:

    def __init__(self, eng, sem, base=0):
        self.eng, self.sem, self.base, self.n = eng, sem, base, 0

    def did(self, ins):
        ins.then_inc(self.sem, 1)
        self.n += 1
        return self.n

    def need(self, n):
        self.eng.wait_ge(self.sem, self.base + n)


def retire(nc, sems):
    for s in sems:
        nc.sync.sem_clear(s)
    nc.all_engine_barrier()


V_CONV_B = 0
V_DW = 3
V_F_DW = 30
V_PL_PWB = 84
V_PG_PWB = 86
V_PG_B2 = 88
V_F1_B = 90
V_F2_B = 92
V_ALPHA = 94
V_NORM1 = 96
V_FFN_NORM = 98
V_LN1_G = 100
V_LN1_B = 102
V_LN2_G = 104
V_LN2_B = 106
V_B_DT = 108
V_DSKIP = 111
V_QB = 114
V_KB = 117
V_N = 120


def tokenizer(nc, H, xcol, w_pl, w_pg, had, pw_mix, w96, vecs, pwb_row, lng_row, lnb_row, cls_row, txt):
    CH = 4
    IM = B // CH
    NP = IM * PATCHES
    ROW = GRID + 1
    IMG = ROW * ROW
    PADC = IM * IMG
    EDGE = ROW + 1
    ROWS = IM * ROW - 1
    with ExitStack() as ctx:
        def sb(name, shape, dt=F32):
            return ctx.enter_context(nc.sbuf_tensor(name, shape, dt))

        sems = []

        def sem(name):
            sems.append(ctx.enter_context(nc.semaphore(name)))
            return sems[-1]

        wp = sb("wp", [128, 2, 3, D])
        hd = sb("hd", [128, 2, PIX])
        wc = sb("wc", [128, KT, 2 * D])
        pwm = sb("pwm", [128, 3, D])
        wf = sb("wf", [HD, 4, 2, D])
        vec = sb("vec", [128, V_N])
        gate = sb("gate", [HD, 8])
        xc = sb("xc", [128, 2, KT, NP])
        P1 = sb("P1", [128, 3, CH * PADC + 2 * EDGE])
        PF = [sb(f"PF{k}", [HD, 2, CH * PADC + 2 * EDGE]) for k in range(3)]
        D1 = sb("D1", [128, 3, IM * ROW, GRID])
        DF = [sb(f"DF{k}", [HD, 2, IM * ROW, GRID]) for k in range(3)]
        L2 = sb("L2", [HD, 2, CH, NP])
        LS = sb("LS", [HD, 2, NP])
        G2 = sb("G2", [HD, 2, NP])
        TG = sb("TG", [HD, 2, NP])
        R2 = sb("R2", [HD, 2, NP])
        T0 = P1[0:PATCHES].rearrange("p k n -> p (k n)")[:, 0:B * D].rearrange("p (b c) -> p b c", b=B)
        T1 = sb("T1", [PATCHES, 2, D])
        rows = sb("rows", [PATCHES, 3, D])
        st = sb("st", [PATCHES, 2, 6])
        mv = sb("mv", [PATCHES, B, 2])
        ve = sb("ve", [PATCHES, B])
        rs = sb("rs", [PATCHES, B])
        nh = sb("nh", [PATCHES, B])
        psC = ctx.enter_context(nc.psum_tensor("psC", [128, 3, BANK], F32))
        psA = ctx.enter_context(nc.psum_tensor("psA", [128, 2, BANK], F32))
        psB = ctx.enter_context(nc.psum_tensor("psB", [128, 2, BANK], F32))
        psF = ctx.enter_context(nc.psum_tensor("psF", [128, BANK], F32))

        s_wp = sem("a_wp"); s_small = sem("a_small"); s_wc = sem("a_wc"); s_x = [sem("a_x0"), sem("a_x1")]
        s_pad = sem("a_pad"); s_had = sem("a_had"); s_hadv = sem("a_hadv"); s_rows = sem("a_rows")
        s_conv = sem("a_conv"); s_gelu = sem("a_gelu"); s_dw1 = sem("a_dw1")
        s_loc = sem("a_loc"); s_g = sem("a_g"); s_lev = sem("a_lev"); s_gev = sem("a_gev")
        s_w2 = sem("a_w2"); s_tg = sem("a_tg"); s_h = sem("a_h"); s_gate = sem("a_gate")
        s_dwf = [sem(f"a_dwf{k}") for k in range(3)]
        s_f = [sem(f"a_f{k}") for k in range(3)]
        s_r1 = sem("a_r1"); s_r2 = sem("a_r2"); s_lr = sem("a_lr"); s_t0 = sem("a_t0")
        s_mv = sem("a_mv"); s_rs = sem("a_rs"); s_t1 = sem("a_t1"); s_out = sem("a_out"); s_cls = sem("a_cls")
        s_own = sem("a_own_dve"); s_ownp = sem("a_own_pool"); s_owna = sem("a_own_act")

        def padded(p, k, c):
            v = p[:, k, EDGE + c * PADC:EDGE + (c + 1) * PADC]
            return v.rearrange("p (i r c) -> p i r c", i=IM, r=ROW)[:, :, 0:GRID, 0:GRID]

        def tap(p, k, c, t):
            off = EDGE + c * PADC + (t // 3 - 1) * ROW + t % 3 - 1
            v = p[:, k, off:off + ROWS * ROW]
            return v.rearrange("p (r c) -> p r c", c=ROW)[:, :, 0:GRID]

        def dense(d, k):
            return d[:, k].rearrange("p (i r) c -> p i (r c)", r=ROW)[:, :, 0:PATCHES]

        WAVES = CH + 3
        ctx.callback(retire, nc, sems)
        block = ctx.enter_context(nc.Block())

        @block.sync
        def _(sp):
            sp.dma_start(wp[:], w_pg.rearrange("(t p) c o -> p t c o", p=128)).then_inc(s_wp, 16)
            sp.dma_start(hd[:], had.rearrange("(t p) x -> p t x", p=128)).then_inc(s_wp, 16)
            sp.dma_start(vec[:], vecs).then_inc(s_small, 16)
            for c in range(CH):
                if c >= 2:
                    sp.wait_ge(s_conv, c - 1)
                sp.dma_start(xc[:, c % 2], xcol.rearrange("(t p) n -> p t n", p=128)[:, :, c * NP:(c + 1) * NP]
                             ).then_inc(s_x[c % 2], 16)
            sp.dma_start(H[0:1, :, :], cls_row.rearrange("(a n) c -> a n c", a=1)).then_inc(s_cls, 16)
            sp.dma_start(H[1 + PATCHES:S, :, :], txt.rearrange("b t c -> t b c")).then_inc(s_cls, 16)
            for n in range(B // 2):
                sp.wait_ge(s_t1, n + 1)
                sp.dma_start(H[1:1 + PATCHES, 2 * n:2 * n + 2, :], T1[:]).then_inc(s_out, 16)
            sp.wait_ge(s_out, 16 * (B // 2))
            sp.wait_ge(s_cls, 32)

        @block.tensor
        def _(pe):
            pe.wait_ge(s_wp, 32)
            for ch in range(3):
                for xt in range(2):
                    n = 2 * ch + xt
                    if n >= 3:
                        pe.wait_ge(s_hadv, n - 2)
                    for bt in range(2):
                        mm = pe.matmul(psC[:, n % 3, 0:D], hd[:, bt, xt * 128:(xt + 1) * 128], wp[:, bt, ch, :],
                                       start=bt == 0, stop=bt == 1)
                    mm.then_inc(s_had, 1)
            pe.wait_ge(s_hadv, 6)
            pe.wait_ge(s_wc, 32)

            def conv(c):
                pe.wait_ge(s_x[c % 2], 16 * (c // 2 + 1))
                if c >= 1:
                    pe.wait_ge(s_gelu, c)
                for t in range(3):
                    for k in range(KT):
                        mm = pe.matmul(psC[:, t, 0:NP], wc[:, k, t * 128:(t + 1) * 128], xc[:, c % 2, k, :],
                                       start=k == 0, stop=k == KT - 1)
                mm.then_inc(s_conv, 1)

            def pair(ps, w, d):
                for m in range(2):
                    for k in range(2):
                        mm = pe.matmul(ps[0:HD, m, 0:NP], w[:, k, m * HD:(m + 1) * HD], d(k),
                                       start=k == 0, stop=k == 1)
                return mm

            conv(0)
            for w in range(WAVES):
                if w + 1 < CH:
                    conv(w + 1)
                if w < CH:
                    if w == 0:
                        pe.wait_ge(s_small, 16 * 3)
                    pe.wait_ge(s_dw1, w + 1)
                    if w > 0:
                        pe.wait_ge(s_tg, w)
                    if w > 2:
                        pe.wait_ge(s_r2, w - 2)
                    for m in range(2):
                        pe.matmul(psA[0:HD, m, 0:NP], pwm[:, 0, m * HD:(m + 1) * HD], dense(D1, 0),
                                  start=True, stop=False)
                        mm = pe.matmul(psA[0:HD, m, 0:NP], pwm[0:64, 1, m * HD:(m + 1) * HD], dense(D1, 1)[0:64],
                                       start=False, stop=True)
                    mm.then_inc(s_loc, 1)
                    if w > 1:
                        pe.wait_ge(s_r1, w - 1)
                    for m in range(2):
                        pe.matmul(psB[0:HD, m, 0:NP], pwm[:, 2, m * HD:(m + 1) * HD], dense(D1, 2),
                                  start=True, stop=False)
                        mm = pe.matmul(psB[0:HD, m, 0:NP], pwm[64:128, 1, m * HD:(m + 1) * HD], dense(D1, 1)[64:128],
                                       start=False, stop=True)
                    mm.then_inc(s_g, 1)
                    pe.wait_ge(s_lev, w + 1)
                    pe.wait_ge(s_gev, w + 1)
                    pair(psA, wf[:, 0], lambda k: G2[:, k, :]).then_inc(s_w2, 1)
                if 0 <= w - 1 < CH:
                    c = w - 1
                    pe.wait_ge(s_dwf[0], c + 1)
                    pe.wait_ge(s_gev, min(w + 1, CH))
                    if c > 0:
                        pe.wait_ge(s_r1, c)
                    pair(psB, wf[:, 1], lambda k: dense(DF[0], k)).then_inc(s_f[0], 1)
                if 0 <= w - 2 < CH:
                    c = w - 2
                    pe.wait_ge(s_dwf[1], c + 1)
                    pe.wait_ge(s_tg, min(w + 1, CH))
                    if c > 0:
                        pe.wait_ge(s_r2, c)
                    pair(psA, wf[:, 2], lambda k: dense(DF[1], k)).then_inc(s_f[1], 1)
                if 0 <= w - 3 < CH:
                    c = w - 3
                    pe.wait_ge(s_dwf[2], c + 1)
                    for n in range(IM // 2):
                        if c * IM // 2 + n > 0:
                            pe.wait_ge(s_t0, c * IM // 2 + n)
                        for j in range(2):
                            for k in range(2):
                                mm = pe.matmul(psF[0:PATCHES, j * D:(j + 1) * D], dense(DF[2], k)[:, 2 * n + j, :],
                                               wf[:, 3, k, :], start=k == 0, stop=k == 1)
                        mm.then_inc(s_f[2], 1)

        @block.scalar
        def _(act):
            act.dma_start(wc[:, :, 0:128], w_pl.rearrange("(t p) o -> p t o", p=128)[:, :, 0:128]).then_inc(s_wc, 16)
            act.dma_start(wc[:, :, 128:192], w_pl.rearrange("(t p) o -> p t o", p=128)[:, :, 128:192]).then_inc(s_wc, 16)
            act.dma_start(pwm[:], pw_mix).then_inc(s_small, 16)
            act.dma_start(wf[:], w96).then_inc(s_small, 16)
            for k, row in enumerate((pwb_row, lng_row, lnb_row)):
                act.dma_start(rows[:, k, :], row.rearrange("(a c) -> a c", a=1).broadcast_to([PATCHES, D])).then_inc(s_rows, 16)
            act.wait_ge(s_small, 48)
            own = Own(act, s_owna)
            n = own.did(act.activation(gate[:, 0:2], vec[0:HD, V_ALPHA:V_ALPHA + 2], ACT.Tanh))
            own.need(n)
            own.did(act.activation(gate[:, 2:4], gate[:, 0:2], ACT.Copy, bias=0.5, scale=-0.5))
            n = own.did(act.activation(gate[:, 0:2], gate[:, 0:2], ACT.Copy, bias=0.5, scale=0.5))
            own.need(n)
            for k in range(2):
                own.did(act.activation(gate[:, 4 + k:5 + k], vec[0:HD, V_PG_B2 + k:V_PG_B2 + k + 1], ACT.Copy,
                                       scale=gate[:, k:k + 1]))
                n = own.did(act.activation(gate[:, 6 + k:7 + k], vec[0:HD, V_PL_PWB + k:V_PL_PWB + k + 1], ACT.Copy,
                                           scale=gate[:, 2 + k:3 + k]))
            own.need(n)

            def gelu(c):
                act.wait_ge(s_conv, c + 1)
                if c == 0:
                    act.wait_ge(s_pad, 1)
                for t in range(3):
                    i = act.activation(padded(P1, t, c), psC[:, t, 0:NP].rearrange("p (i r c) -> p i r c", i=IM, r=GRID),
                                       ACT.Gelu, bias=vec[:, V_CONV_B + t:V_CONV_B + t + 1])
                i.then_inc(s_gelu, 1)

            gelu(0)
            for w in range(WAVES):
                if w + 1 < CH:
                    gelu(w + 1)
                if w < CH:
                    act.wait_ge(s_loc, w + 1)
                    if w > 0:
                        act.wait_ge(s_h, w)
                        act.wait_ge(s_w2, w)
                    for k in range(2):
                        act.activation(L2[:, k, w, :], psA[0:HD, k, 0:NP], ACT.Identity,
                                       bias=vec[0:HD, V_PL_PWB + k:V_PL_PWB + k + 1])
                        i = act.activation(LS[:, k, :], psA[0:HD, k, 0:NP], ACT.Identity,
                                           bias=gate[:, 6 + k:7 + k], scale=gate[:, 2 + k:3 + k])
                    i.then_inc(s_lev, 1)
                    act.wait_ge(s_g, w + 1)
                    for k in range(2):
                        i = act.activation(G2[:, k, :], psB[0:HD, k, 0:NP], ACT.Gelu,
                                           bias=vec[0:HD, V_PG_PWB + k:V_PG_PWB + k + 1])
                    i.then_inc(s_gev, 1)
                    act.wait_ge(s_w2, w + 1)
                    for k in range(2):
                        i = act.activation(TG[:, k, :], psA[0:HD, k, 0:NP], ACT.Identity,
                                           bias=gate[:, 4 + k:5 + k], scale=gate[:, k:k + 1])
                    i.then_inc(s_tg, 1)
                if 0 <= w - 1 < CH:
                    c = w - 1
                    act.wait_ge(s_f[0], c + 1)
                    for k in range(2):
                        i = act.activation(padded(PF[1], k, c),
                                           psB[0:HD, k, 0:NP].rearrange("p (i r c) -> p i r c", i=IM, r=GRID),
                                           ACT.Relu, bias=vec[0:HD, V_F1_B + k:V_F1_B + k + 1])
                    i.then_inc(s_r1, 1)
                if 0 <= w - 2 < CH:
                    c = w - 2
                    act.wait_ge(s_f[1], c + 1)
                    if c > 0:
                        act.wait_ge(s_lr, c)
                    for k in range(2):
                        i = act.activation(R2[:, k, :], psA[0:HD, k, 0:NP], ACT.Relu,
                                           bias=vec[0:HD, V_F2_B + k:V_F2_B + k + 1])
                    i.then_inc(s_r2, 1)

        @block.vector
        def _(v):
            own = Own(v, s_own)
            v.memset(P1[:], 0.0)
            for p in PF:
                i = v.memset(p[:], 0.0)
            i.then_inc(s_pad, 1)
            for n in range(6):
                v.wait_ge(s_had, n + 1)
                v.tensor_copy(wc[:, n, 256:384], psC[:, n % 3, 0:128])
                v.tensor_copy(wc[:, n, 192:256], psC[:, n % 3, 128:192]).then_inc(s_hadv, 1)
            v.wait_ge(s_small, 48)
            v.wait_ge(s_rows, 48)

            def dw(src, dst, n, c, col, done):
                last = [0] * n
                for t in range(9):
                    for k in range(n):
                        out, w = dst[:, k, 0:ROWS, :], vec[0:src.shape[0], col + 9 * k + t:col + 9 * k + t + 1]
                        if t == 0:
                            i = v.tensor_scalar(out, tap(src, k, c, t), w, None, ALU.mult)
                        else:
                            own.need(last[k])
                            i = v.scalar_tensor_tensor(out, tap(src, k, c, t), w, out, ALU.mult, ALU.add)
                        last[k] = own.did(i)
                own.need(last[n - 1])
                v.sem_inc(done, 1)

            for w in range(WAVES):
                if w < CH:
                    v.wait_ge(s_gelu, w + 1)
                    if w > 0:
                        v.wait_ge(s_g, w)
                    dw(P1, D1, 3, w, V_DW, s_dw1)
                if 0 <= w - 1 < CH:
                    v.wait_ge(s_h, w)
                    if w > 1:
                        v.wait_ge(s_f[0], w - 1)
                    dw(PF[0], DF[0], 2, w - 1, V_F_DW, s_dwf[0])
                if 0 <= w - 2 < CH:
                    v.wait_ge(s_r1, w - 1)
                    if w > 2:
                        v.wait_ge(s_f[1], w - 2)
                    dw(PF[1], DF[1], 2, w - 2, V_F_DW + 18, s_dwf[1])
                if 0 <= w - 3 < CH:
                    c = w - 3
                    v.wait_ge(s_lr, c + 1)
                    if c > 0:
                        v.wait_ge(s_f[2], c * IM // 2)
                    dw(PF[2], DF[2], 2, c, V_F_DW + 36, s_dwf[2])
                    for n in range(c * IM // 2, (c + 1) * IM // 2):
                        v.wait_ge(s_f[2], n + 1)
                        v.tensor_tensor(T0[:, 2 * n:2 * n + 2, :], psF[0:PATCHES, 0:2 * D].rearrange("p (j c) -> p j c", j=2),
                                        rows[:, 0:0+1, :].broadcast_to([PATCHES, 2, D]), ALU.add).then_inc(s_t0, 1)
                        v.wait_ge(s_t0, n + 1)
                        for j in range(2):
                            b = own.did(v.bn_stats(st[:, j, :], T0[:, 2 * n + j, :]))
                            own.need(b)
                            v.bn_aggr(mv[:, 2 * n + j, :], st[:, j, :]).then_inc(s_mv, 1)
            v.memset(nh[:], -0.5).then_inc(s_mv, 1)
            v.wait_ge(s_rs, 1)
            for n in range(B // 2):
                if n > 0:
                    v.wait_ge(s_out, 16 * n)
                for j in range(2):
                    b = 2 * n + j
                    i = own.did(v.tensor_scalar(T1[:, j, :], T0[:, b, :], mv[:, b, 0:1], rs[:, b:b + 1],
                                                ALU.subtract, ALU.mult))
                own.need(i)
                i = own.did(v.tensor_tensor(T1[:], T1[:], rows[:, 1:1+1, :].broadcast_to([PATCHES, 2, D]), ALU.mult))
                own.need(i)
                v.tensor_tensor(T1[:], T1[:], rows[:, 2:2+1, :].broadcast_to([PATCHES, 2, D]), ALU.add).then_inc(s_t1, 1)

        @block.gpsimd
        def _(g):
            own = Own(g, s_ownp)
            for w in range(WAVES):
                if w < CH:
                    g.wait_ge(s_tg, w + 1)
                    for k in range(2):
                        i = g.tensor_tensor(padded(PF[0], k, w), LS[:, k, :].rearrange("p (i r c) -> p i r c", i=IM, r=GRID),
                                            TG[:, k, :].rearrange("p (i r c) -> p i r c", i=IM, r=GRID), ALU.add)
                    i.then_inc(s_h, 1)
                if 0 <= w - 2 < CH:
                    c = w - 2
                    g.wait_ge(s_r2, c + 1)
                    for k in range(2):
                        i = g.tensor_tensor(padded(PF[2], k, c), L2[:, k, c, :].rearrange("p (i r c) -> p i r c", i=IM, r=GRID),
                                            R2[:, k, :].rearrange("p (i r c) -> p i r c", i=IM, r=GRID), ALU.add)
                    i.then_inc(s_lr, 1)
            g.wait_ge(s_mv, B + 1)
            n = own.did(g.tensor_scalar(ve[:], mv[:, :, 1], 1e-5, None, ALU.add))
            own.need(n)
            g.tensor_tensor(rs[:], ve[:], nh[:], ALU.pow).then_inc(s_rs, 1)


G = 4
N = G * S
ROUNDS = B // G
INNER = 384
NI = INNER // 128
STATE = 16
FFN = 512
NF = FFN // 128


def row_stats(nc, tag, H, eps2, r1, r12, mv):
    with ExitStack() as ctx:
        def sem(name):
            return ctx.enter_context(nc.semaphore(name))

        st = ctx.enter_context(nc.sbuf_tensor(f"{tag}_st_stats", [S, B, 6], F32))
        t = ctx.enter_context(nc.sbuf_tensor(f"{tag}_st_t", [S, B], F32))
        nh = ctx.enter_context(nc.sbuf_tensor(f"{tag}_st_nh", [S, B], F32))
        s_st = sem(f"{tag}_st_bn"); s_mv = sem(f"{tag}_st_mv"); s_p = sem(f"{tag}_st_pool")
        block = ctx.enter_context(nc.Block())

        @block.vector
        def _(v):
            v.memset(nh[:], -0.5)
            for b in range(B):
                v.bn_stats(st[:, b, :], H[:, b, :]).then_inc(s_st, 1)
            v.wait_ge(s_st, B)
            for b in range(B):
                v.bn_aggr(mv[:, b, :], st[:, b, :]).then_inc(s_mv, 1)
            v.wait_ge(s_mv, B)

        @block.gpsimd
        def _(g):
            own = Own(g, s_p)
            g.wait_ge(s_mv, B)
            n = own.did(g.tensor_scalar(t[:], mv[:, :, 1], 1e-5, None, ALU.add))
            own.need(n)
            n = own.did(g.tensor_tensor(r1[:], t[:], nh[:], ALU.pow))
            own.need(n)
            n = own.did(g.tensor_tensor(t[:], r1[:], r1[:], ALU.mult))
            own.need(n)
            n = own.did(g.tensor_tensor(t[:], t[:], mv[:, :, 1], ALU.mult))
            own.need(n)
            n = own.did(g.tensor_scalar(t[:], t[:], eps2, None, ALU.add))
            own.need(n)
            n = own.did(g.tensor_tensor(t[:], t[:], nh[:], ALU.pow))
            own.need(n)
            n = own.did(g.tensor_tensor(r12[:], t[:], r1[:], ALU.mult))
            own.need(n)


def mamba(nc, H, w_zg, w_x, w_dt, a_log, w_o, w_ug, w_dn, vecs, onehot, eye):
    K_V, K_G = 27, 3
    with ExitStack() as ctx:
        def sb(name, shape, dt=F32):
            return ctx.enter_context(nc.sbuf_tensor(name, shape, dt))

        def sem(name):
            return ctx.enter_context(nc.semaphore(name))

        mv = sb("b_mv", [S, B, 2]); r1 = sb("b_r1", [S, B]); r12 = sb("b_r12", [S, B])
        row_stats(nc, "b", H, 1e-6, r1, r12, mv)

        wzg = sb("wzg", [HD, 2, 2, INNER]); wx = sb("wx", [128, NI, 192]); wdt = sb("wdt", [HD, INNER])
        wo = sb("wo", [128, NI, D]); wug = sb("wug", [HD, 2, 2, FFN]); wdn = sb("wdn", [128, NF, D])
        A = sb("A", [128, NI, STATE]); vec = sb("b_vec", [128, V_N])
        oh = sb("oh", [HD, 2 * STATE]); sel = sb("sel", [HD, 2 * STATE, 128], BF16); ident = sb("b_id", [128, 128])
        nh = sb("b_nh", [S, G])
        xl = sb("xl", [S, G, D]); hn = sb("hn", [S, G, D]); hT = sb("hT", [HD, 2, N])
        sg = sb("sg", [128, NI, N]); z = sb("z", [128, NI, N]); dtin = sb("dtin", [HD, N])
        P3 = sb("P3", [HD, N], BF16); Pm = sb("Pm", [HD, N], BF16); R = sb("R", [HD, N])
        xd = sb("xd", [128, NI, N]); ax = sb("ax", [128, NI, N]); u = sb("u", [128, NI, N]); lnw = sb("lnw", [128, NI, N])
        dt = sb("dt", [128, NI, N]); dtz = sb("dtz", [128, NI, N])
        abar = sb("abar", [128, 2, NI, G, S]); Bb = sb("Bb", [128, 2, N]); Bx = sb("Bx", [128, 2, NI, N])
        hs = sb("hs", [128, 3, NI, N]); hC = sb("hC", [128, 2, NI, N]); y = sb("y", [128, NI, N])
        x1 = sb("x1", [S, G, D]); hf = sb("hf", [S, G, D]); hfT = sb("hfT", [HD, 2, N])
        th = sb("th", [128, 2, 2, N]); av = sb("av", [128, NF, N])
        st = sb("b_st", [S, G, 6]); mg = sb("b_mg", [S, G, 2]); ms = sb("b_ms", [S, G]); rr = sb("b_rr", [S, G])
        ps = ctx.enter_context(nc.psum_tensor("b_ps", [128, 8, BANK], F32))

        s_w = sem("b_w"); s_cst = sem("b_cst"); s_A = sem("b_A"); s_A2 = sem("b_A2")
        s_hn = sem("b_hn"); s_tr = sem("b_tr"); s_hT = sem("b_hT"); s_gt = sem("b_gt"); s_zi = sem("b_zi")
        s_sg = sem("b_sg"); s_z = sem("b_z"); s_xp = sem("b_xp"); s_dtin = sem("b_dtin"); s_hi = sem("b_hi")
        s_P3 = sem("b_P3"); s_dtp = sem("b_dtp"); s_u = sem("b_u"); s_ln = sem("b_ln"); s_dt = sem("b_dt")
        s_dtz = sem("b_dtz"); s_pb = sem("b_pb"); s_pc = sem("b_pc"); s_ab = sem("b_ab"); s_bb = sem("b_bb")
        s_bx = sem("b_bx"); s_scan = sem("b_scan"); s_hc = sem("b_hc"); s_ys = sem("b_ys"); s_y = sem("b_y")
        s_o = sem("b_o"); s_st = sem("b_stat"); s_rr = sem("b_rr2"); s_hf = sem("b_hf"); s_tr2 = sem("b_tr2")
        s_hfT = sem("b_hfT"); s_ug = sem("b_ug"); s_th = sem("b_th"); s_av = sem("b_av"); s_dn = sem("b_dn")
        s_x1 = sem("b_x1"); s_own = sem("b_own_dve"); s_ownp = sem("b_own_pool"); s_owna = sem("b_own_act"); s_add = sem("b_add"); s_step = sem("b_step")
        block = ctx.enter_context(nc.Block())

        def f2(t):
            return t.rearrange("p a b -> p (a b)")

        @block.sync
        def _(sp):
            for dst, src in ((wzg, w_zg), (wx, w_x), (wdt, w_dt), (A, a_log), (wo, w_o), (wug, w_ug), (wdn, w_dn),
                             (vec, vecs), (oh, onehot), (ident, eye)):
                sp.dma_start(dst[:], src).then_inc(s_w, 16)

        @block.tensor
        def _(pe):
            pe.wait_ge(s_w, 160)
            pe.wait_ge(s_cst, 3)
            with pe.Fori(0, ROUNDS) as i:
                def turn(src, bank, done):
                    for k in range(2):
                        for q in range(G):
                            mm = pe.transpose(ps[0:HD, bank + k, q * S:(q + 1) * S], src[:, q, k * HD:(k + 1) * HD],
                                              ident[0:S, 0:S])
                    mm.then_inc(done, 1)

                pe.wait_ge(s_hn, i + 1)
                turn(hn, 0, s_tr)
                pe.wait_ge(s_hT, i + 1)
                for j, done in ((1, s_gt), (0, s_zi)):
                    for m in range(NI):
                        for k in range(2):
                            mm = pe.matmul(ps[:, (2 if j else 5) + m, 0:N], wzg[:, k, j, m * 128:(m + 1) * 128], hT[:, k, :],
                                           start=k == 0, stop=k == 1)
                    mm.then_inc(done, 1)
                pe.wait_ge(s_z, i + 1)
                for j in range(2):
                    for k in range(NI):
                        mm = pe.matmul(ps[0:HD, j, 0:N], wx[:, k, j * 96:(j + 1) * 96], z[:, k, :],
                                       start=k == 0, stop=k == NI - 1)
                mm.then_inc(s_xp, 1)
                pe.wait_ge(s_dtin, i + 1)
                for m in range(NI):
                    mm = pe.matmul(ps[:, 2 + m, 0:N], wdt[:, m * 128:(m + 1) * 128], dtin[:], start=True, stop=True)
                mm.then_inc(s_dtp, 1)

                def spread_b(s):
                    if s >= 2:
                        pe.wait_ge(s_bb, i * STATE + (s - 1))
                    pe.matmul(ps[:, s % 2, 0:N], sel[:, s, :], P3[:], start=True, stop=True).then_inc(s_pb, 1)

                def spread_c(s):
                    if s >= 2:
                        pe.wait_ge(s_hc, i * STATE + (s - 1))
                    pe.matmul(ps[:, 2 + s % 2, 0:N], sel[:, STATE + s, :], P3[:], start=True, stop=True).then_inc(s_pc, 1)

                pe.wait_ge(s_P3, i + 1)
                pe.wait_ge(s_u, i + 1)
                for s in range(2):
                    spread_b(s)
                    spread_c(s)
                for s in range(STATE):
                    if s + 2 < STATE:
                        spread_b(s + 2)
                    pe.wait_ge(s_hc, i * STATE + (s + 1))
                    for m in range(NI):
                        mm = pe.matmul(ps[:, 5 + m, 0:N], ident[:], hC[:, s % 2, m, :], start=s == 0, stop=s == STATE - 1)
                    mm.then_inc(s_ys, 1)
                    if s + 2 < STATE:
                        spread_c(s + 2)
                pe.wait_ge(s_y, i + 1)
                for q in range(G):
                    for k in range(NI):
                        mm = pe.matmul(ps[0:S, q // 2, (q % 2) * D:(q % 2 + 1) * D], y[:, k, q * S:(q + 1) * S], wo[:, k, :],
                                       start=k == 0, stop=k == NI - 1)
                mm.then_inc(s_o, 1)
                pe.wait_ge(s_hf, i + 1)
                turn(hf, 2, s_tr2)
                pe.wait_ge(s_hfT, i + 1)
                for h in range(2):
                    for j in range(2):
                        for m in range(2):
                            for k in range(2):
                                c = (2 * h + m) * 128
                                mm = pe.matmul(ps[:, (4, 0)[h] + 2 * j + m, 0:N], wug[:, k, j, c:c + 128], hfT[:, k, :],
                                               start=k == 0, stop=k == 1)
                    mm.then_inc(s_ug, 1)
                pe.wait_ge(s_av, i * 2 + 2)
                for q in range(G):
                    for k in range(NF):
                        mm = pe.matmul(ps[0:S, 4 + q // 2, (q % 2) * D:(q % 2 + 1) * D], av[:, k, q * S:(q + 1) * S], wdn[:, k, :],
                                       start=k == 0, stop=k == NF - 1)
                mm.then_inc(s_dn, 1)

        @block.scalar
        def _(act):
            act.wait_ge(s_A2, 1)
            n = act.activation(f2(A[:]), f2(A[:]), ACT.Exp).then_inc(s_A, 1)
            act.wait_ge(s_A, 1)
            act.activation(f2(A[:]), f2(A[:]), ACT.Copy, scale=-1.0).then_inc(s_A, 1)
            act.wait_ge(s_A, 2)
            act.wait_ge(s_cst, 3)
            with act.Fori(0, ROUNDS) as i:
                own = Own(act, s_owna, i * 2)
                act.wait_ge(s_tr, i + 1)
                for k in range(2):
                    a = act.activation(hT[:, k, :], ps[0:HD, k, 0:N], ACT.Identity, bias=0.0,
                                       scale=vec[0:HD, V_NORM1 + k:V_NORM1 + k + 1])
                a.then_inc(s_hT, 1)
                act.wait_ge(s_gt, i + 1)
                act.activation(sg[:], ps[:, 2:5, 0:N], ACT.Tanh, scale=0.5).then_inc(s_sg, 1)
                act.wait_ge(s_xp, i + 1)
                act.activation(dtin[:], ps[0:HD, 0, 0:N], ACT.Copy).then_inc(s_dtin, 1)
                act.activation(P3[:], ps[0:HD, 1, 0:N], ACT.Copy).then_inc(s_hi, 1)
                act.wait_ge(s_dtp, i + 1)
                for m in range(NI):
                    n = own.did(act.activation(xd[:, m, :], ps[:, 2 + m, 0:N], ACT.Identity,
                                               bias=vec[:, V_B_DT + m:V_B_DT + m + 1])) if m == NI - 1 else \
                        act.activation(xd[:, m, :], ps[:, 2 + m, 0:N], ACT.Identity, bias=vec[:, V_B_DT + m:V_B_DT + m + 1])
                own.need(n)
                n = own.did(act.activation(f2(ax[:]), f2(xd[:]), ACT.Abs))
                own.need(n)
                act.activation(f2(u[:]), f2(ax[:]), ACT.Exp, scale=-1.0).then_inc(s_u, 1)
                act.wait_ge(s_u, i + 1)
                act.activation(f2(lnw[:]), f2(u[:]), ACT.Ln, bias=1.0).then_inc(s_ln, 1)
                act.wait_ge(s_dt, i + 1)
                for s in range(STATE):
                    if s >= 2:
                        act.wait_ge(s_bx, i * STATE + (s - 1))
                    act.wait_ge(s_pb, i * STATE + (s + 1))
                    act.activation(Bb[:, s % 2, :], ps[:, s % 2, 0:N], ACT.Copy).then_inc(s_bb, 1)
                    if s >= 2:
                        act.wait_ge(s_scan, i * STATE + (s - 1))
                    for m in range(NI):
                        a = act.activation(abar[:, s % 2, m, :, 1:S], dt[:, m, :].rearrange("p (g t) -> p g t", g=G)[:, :, 1:S],
                                           ACT.Exp, scale=A[:, m, s:s + 1])
                    a.then_inc(s_ab, 1)
                act.wait_ge(s_tr2, i + 1)
                for k in range(2):
                    a = act.activation(hfT[:, k, :], ps[0:HD, 2 + k, 0:N], ACT.Identity, bias=0.0,
                                       scale=vec[0:HD, V_FFN_NORM + k:V_FFN_NORM + k + 1])
                a.then_inc(s_hfT, 1)
                for h in range(2):
                    act.wait_ge(s_ug, i * 2 + (h + 1))
                    act.activation(th[:, h], ps[:, (4, 0)[h]:(4, 0)[h] + 2, 0:N], ACT.Tanh, scale=0.5).then_inc(s_th, 1)

        @block.vector
        def _(v):
            v.memset(abar[:], 0.0).then_inc(s_cst, 1)
            v.memset(nh[:], -0.5).then_inc(s_cst, 1)
            v.wait_ge(s_w, 160)
            v.tensor_copy(sel[:], oh[:].rearrange("p (s a) -> p s a", a=1).broadcast_to([HD, 2 * STATE, 128])).then_inc(s_cst, 1)
            v.tensor_scalar(f2(A[:]), f2(A[:]), 80.0, None, ALU.min).then_inc(s_A2, 1)
            with v.Fori(0, ROUNDS) as i:
                own = Own(v, s_own, i * K_V)

                def H_(q):
                    return H[:, bass.ds(i * G + q, 1), :].rearrange("p a c -> p (a c)")

                for q in range(G):
                    b = bass.ds(i * G + q, 1)
                    own.did(v.tensor_scalar(xl[:, q, :], H_(q), mv[:, b, 0:1].rearrange("p a c -> p (a c)"), r1[:, b],
                                            ALU.subtract, ALU.mult))
                    n = v.tensor_scalar(hn[:, q, :], H_(q), mv[:, b, 0:1].rearrange("p a c -> p (a c)"), r12[:, b],
                                        ALU.subtract, ALU.mult)
                n.then_inc(s_hn, 1)
                v.wait_ge(s_sg, i + 1)
                n = own.did(v.tensor_scalar(f2(sg[:]), f2(sg[:]), 0.5, 0.5, ALU.mult, ALU.add))
                own.need(n)
                v.wait_ge(s_zi, i + 1)
                v.tensor_tensor(z[:], sg[:], ps[:, 5:8, 0:N], ALU.mult).then_inc(s_z, 1)
                v.wait_ge(s_hi, i + 1)
                own.did(v.tensor_tensor(R[32:64, :], ps[32:64, 1, 0:N], P3[32:64, :], ALU.subtract))
                n = own.did(v.tensor_tensor(R[64:96, :], ps[64:96, 1, 0:N], P3[64:96, :], ALU.subtract))
                own.need(n)
                own.did(v.tensor_copy(P3[32:64, :], R[32:64, :]))
                n = own.did(v.tensor_copy(Pm[64:96, :], R[64:96, :]))
                own.need(n)
                v.tensor_tensor(P3[64:96, :], R[64:96, :], Pm[64:96, :], ALU.subtract).then_inc(s_P3, 1)
                v.wait_ge(s_u, i + 1)
                n = own.did(v.tensor_scalar(f2(ax[:]), f2(u[:]), 1.0, None, ALU.add))
                own.need(n)
                n = own.did(v.scalar_tensor_tensor(f2(ax[:]), f2(ax[:]), -1.0, f2(u[:]), ALU.add, ALU.subtract, reverse1=True))
                own.need(n)
                v.wait_ge(s_ln, i + 1)
                n = own.did(v.tensor_tensor(f2(ax[:]), f2(ax[:]), f2(lnw[:]), ALU.add))
                own.need(n)
                v.scalar_tensor_tensor(f2(dt[:]), f2(xd[:]), 0.0, f2(ax[:]), ALU.max, ALU.add).then_inc(s_dt, 1)

                def scan(s):
                    v.wait_ge(s_ab, i * STATE + (s + 1))
                    v.wait_ge(s_bx, i * STATE + (s + 1))
                    if s >= 3:
                        v.wait_ge(s_hc, i * STATE + (s - 2))
                    v.tensor_tensor_scan(f2(hs[:, s % 3]), abar[:, s % 2].rearrange("p m g t -> p (m g t)"), f2(Bx[:, s % 2]),
                                         0.0, ALU.mult, ALU.add).then_inc(s_scan, 1)

                scan(0)
                for s in range(STATE):
                    if s + 1 < STATE:
                        scan(s + 1)
                    v.wait_ge(s_scan, i * STATE + (s + 1))
                    v.wait_ge(s_pc, i * STATE + (s + 1))
                    if s >= 2:
                        v.wait_ge(s_ys, i * STATE + (s - 1))
                    v.tensor_tensor(hC[:, s % 2], hs[:, s % 3],
                                    ps[:, 2 + s % 2, 0:N].rearrange("p (a n) -> p a n", a=1).broadcast_to([128, NI, N]),
                                    ALU.mult).then_inc(s_hc, 1)
                v.wait_ge(s_ys, i * STATE + STATE)
                for m in range(NI):
                    n = v.scalar_tensor_tensor(y[:, m, :], z[:, m, :], vec[:, V_DSKIP + m:V_DSKIP + m + 1], ps[:, 5 + m, 0:N],
                                               ALU.mult, ALU.add)
                n.then_inc(s_y, 1)
                v.wait_ge(s_o, i + 1)
                for h in range(2):
                    n = own.did(v.tensor_tensor(x1[:, 2 * h:2 * h + 2, :], xl[:, 2 * h:2 * h + 2, :],
                                                ps[0:S, h, 0:2 * D].rearrange("p (j c) -> p j c", j=2), ALU.add))
                own.need(n)
                for q in range(G):
                    n = own.did(v.bn_stats(st[:, q, :], x1[:, q, :]))
                own.need(n)
                v.sem_inc(s_step, 1)
                for q in range(G):
                    n = own.did(v.bn_aggr(mg[:, q, :], st[:, q, :]))
                own.need(n)
                n = own.did(v.tensor_tensor(ms[:], mg[:, :, 0], mg[:, :, 0], ALU.mult))
                own.need(n)
                v.scalar_tensor_tensor(ms[:], ms[:], 1e-6, mg[:, :, 1], ALU.add, ALU.add).then_inc(s_st, 1)
                v.wait_ge(s_rr, i + 1)
                for q in range(G):
                    n = v.tensor_scalar(hf[:, q, :], x1[:, q, :], rr[:, q:q + 1], None, ALU.mult)
                n.then_inc(s_hf, 1)
                for h in range(2):
                    g0 = (4, 0)[h]
                    v.wait_ge(s_th, i * 2 + (h + 1))
                    n = own.did(v.scalar_tensor_tensor(th[:, h], th[:, h], 1.0, ps[:, g0:g0 + 2, 0:N], ALU.add, ALU.mult))
                    own.need(n)
                    v.scalar_tensor_tensor(av[:, 2 * h:2 * h + 2, :], th[:, h], 0.5, ps[:, g0 + 2:g0 + 4, 0:N],
                                           ALU.mult, ALU.mult).then_inc(s_av, 1)
                v.wait_ge(s_dn, i + 1)
                v.wait_ge(s_add, i + 1)
                for h in range(2):
                    b = bass.ds(i * G + 2 * h, 2)
                    n = own.did(v.tensor_tensor(H[:, b, :], x1[:, 2 * h:2 * h + 2, :],
                                                ps[0:S, 4 + h, 0:2 * D].rearrange("p (j c) -> p j c", j=2), ALU.add))
                own.need(n)
                assert own.n == K_V, own.n

        @block.gpsimd
        def _(g):
            g.wait_ge(s_cst, 3)
            with g.Fori(0, ROUNDS) as i:
                own = Own(g, s_ownp, i * K_G)
                g.wait_ge(s_dt, i + 1)
                n = own.did(g.tensor_tensor(f2(dtz[:]), f2(dt[:]), f2(z[:]), ALU.mult))
                own.need(n)
                for s in range(STATE):
                    g.wait_ge(s_bb, i * STATE + (s + 1))
                    if s >= 2:
                        g.wait_ge(s_scan, i * STATE + (s - 1))
                    g.tensor_tensor(Bx[:, s % 2], dtz[:],
                                    Bb[:, s % 2, :].rearrange("p (a n) -> p a n", a=1).broadcast_to([128, NI, N]),
                                    ALU.mult).then_inc(s_bx, 1)
                g.wait_ge(s_st, i + 1)
                g.tensor_tensor(rr[:], ms[:], nh[:], ALU.pow).then_inc(s_rr, 1)
                g.wait_ge(s_hf, i + 1)
                b = bass.ds(i * G, G)
                for k in range(2):
                    n = own.did(g.tensor_tensor(x1[:, 2 * k:2 * k + 2, :], x1[:, 2 * k:2 * k + 2, :],
                                                H[:, bass.ds(i * G + 2 * k, 2), :], ALU.add))
                own.need(n)
                g.sem_inc(s_add, 1)
                assert own.n == K_G, own.n


HEADS = 12
DH = 16
EXPERTS = 8
DFF = 768
KF = DFF // 128
U32 = mybir.dt.uint32


def attention(nc, H, XN, L, xs, w_qk, w_v, w_ao, w_r, rows_c, vecs, eye, W1, W2, w1d, w2d):
    K_V, K_G = 21, 2
    with ExitStack() as ctx:
        def sb(name, shape, dt=F32):
            return ctx.enter_context(nc.sbuf_tensor(name, shape, dt))

        def sem(name):
            return ctx.enter_context(nc.semaphore(name))

        mv = sb("c_mv", [S, B, 2]); r1 = sb("c_r1", [S, B]); r12 = sb("c_r12", [S, B])
        row_stats(nc, "c", H, 1e-5, r1, r12, mv)

        wqk = sb("wqk", [HD, 2, 6, 128]); wv = sb("wv", [HD, 2, D]); wao = sb("wao", [HD, 2, D]); wr = sb("wr", [HD, 2, EXPERTS])
        bro = sb("bro", [S, 2 * D + EXPERTS]); vec = sb("c_vec", [128, V_N]); ident = sb("c_id", [128, 128])
        qb = sb("qb", [128, 3]); nh = sb("c_nh", [S, G]); zero = sb("c_zero", [128, D])
        x = sb("c_x", [S, G, D]); x2 = sb("c_x2", [S, G, D]); x2T = sb("x2T", [HD, 2, N])
        qT = sb("qT", [128, 3, N]); kB = sb("kB", [128, 3, G, 4, S]); V = sb("V", [S, G, HEADS, DH + 1])
        mx = sb("mx", [S, 2, HEADS]); E = sb("E", [S, 2, HEADS, S]); PT = sb("PT", [S, 2, HEADS, S])
        rc = sb("rc", [S, HEADS]); ao = sb("ao", [S, 2, HEADS, DH]); aoT = sb("aoT", [HD, 2, S])
        x3 = sb("x3", [S, G, D]); st = sb("c_st", [S, G, 6]); mg = sb("c_mg", [S, G, 2]); ms = sb("c_ms", [S, G])
        rr = sb("c_rr", [S, G]); xn = sb("c_xn", [S, G, D]); xnT = sb("xnT", [HD, 2, N])
        ps = ctx.enter_context(nc.psum_tensor("c_ps", [128, 8, BANK], F32))

        s_w = sem("c_w"); s_e = sem("c_e"); s_cst = sem("c_cst"); s_qb = sem("c_qb"); s_x2 = sem("c_x2s"); s_tr = sem("c_tr")
        s_x2T = sem("c_x2T"); s_q = sem("c_q"); s_k = sem("c_k"); s_qT = sem("c_qT"); s_kT = sem("c_kT"); s_v = sem("c_v")
        s_V = sem("c_V"); s_s = sem("c_s"); s_E = sem("c_E"); s_P = sem("c_P"); s_pt = sem("c_pt"); s_PTa = sem("c_PTa")
        s_PTv = sem("c_PTv"); s_av = sem("c_av"); s_ao = sem("c_ao"); s_at = sem("c_at"); s_aoT = sem("c_aoT"); s_op = sem("c_op")
        s_xb = sem("c_xb"); s_x3 = sem("c_x3"); s_mg = sem("c_mgs"); s_rr = sem("c_rrs"); s_xn = sem("c_xn2"); s_tr2 = sem("c_tr2")
        s_xnT = sem("c_xnT"); s_lg = sem("c_lg"); s_L = sem("c_L"); s_add = sem("c_add")
        s_own = sem("c_own_dve"); s_ownp = sem("c_own_pool"); s_zero = sem("c_zs"); s_step = sem("c_step")
        block = ctx.enter_context(nc.Block())

        @block.sync
        def _(sp):
            for dst, src in ((wqk, w_qk), (wv, w_v), (wao, w_ao), (wr, w_r), (vec, vecs), (ident, eye)):
                sp.dma_start(dst[:], src).then_inc(s_w, 16)
            sp.dma_start(bro[:], rows_c.rearrange("(a n) -> a n", a=1).broadcast_to([S, 2 * D + EXPERTS])).then_inc(s_w, 16)
            sp.wait_ge(s_zero, 1)
            sp.dma_start(xs.rearrange("(n p) c -> p n c", p=128),
                         zero[:].rearrange("p (a c) -> p a c", a=1).broadcast_to([128, xs.shape[0] // 128, D])).then_inc(s_e, 16)
            for e in range(EXPERTS):
                sp.dma_start(W1[:, :, e, :], w1d[:, :, e, :]).then_inc(s_e, 16)
                sp.dma_start(W2[:, :, e, :], w2d[:, :, e, :]).then_inc(s_e, 16)
            sp.wait_ge(s_e, 16 * (1 + 2 * EXPERTS))

        @block.tensor
        def _(pe):
            pe.wait_ge(s_w, 112)
            pe.wait_ge(s_cst, 2)
            with pe.Fori(0, ROUNDS) as i:
                def turn(src, bank, done):
                    for k in range(2):
                        for q in range(G):
                            mm = pe.transpose(ps[0:HD, bank + k, q * S:(q + 1) * S], src[:, q, k * HD:(k + 1) * HD],
                                              ident[0:S, 0:S])
                    mm.then_inc(done, 1)

                pe.wait_ge(s_x2, i + 1)
                turn(x2, 0, s_tr)
                pe.wait_ge(s_x2T, i + 1)
                for j, done in ((0, s_q), (1, s_k)):
                    for m in range(3):
                        for k in range(2):
                            mm = pe.matmul(ps[:, 2 + 3 * j + m, 0:N], wqk[:, k, 3 * j + m, :], x2T[:, k, :], start=k == 0, stop=k == 1)
                    mm.then_inc(done, 1)
                for q in range(G):
                    for k in range(2):
                        mm = pe.matmul(ps[0:S, q // 2, (q % 2) * D:(q % 2 + 1) * D], x2T[:, k, q * S:(q + 1) * S], wv[:, k, :],
                                       start=k == 0, stop=k == 1)
                mm.then_inc(s_v, 1)
                pe.wait_ge(s_qT, i + 1)
                pe.wait_ge(s_kT, i + 1)

                def scores(q):
                    if q >= 2:
                        pe.wait_ge(s_E, i * G + (q - 1))
                    for h0, h1 in ((0, 4), (4, 6), (6, 8), (8, 12)):
                        m, j = h0 // 4, h0 % 4
                        mm = pe.matmul(ps[0:S, 2 + 2 * (q % 2) + h0 // 6, (h0 % 6) * S:(h0 % 6 + h1 - h0) * S],
                                       qT[:, m, q * S:(q + 1) * S], kB[:, m, q, j:j + h1 - h0, :].rearrange("p h s -> p (h s)"),
                                       start=True, stop=True)
                    mm.then_inc(s_s, 1)

                def flip(q):
                    pe.wait_ge(s_P, i * G + (q + 1))
                    if q >= 1:
                        pe.wait_ge(s_PTa, i * G + q)
                        pe.wait_ge(s_PTv, i * G + q)
                    for h in range(HEADS):
                        mm = pe.transpose(ps[0:S, 6 + h // 6, (h % 6) * S:(h % 6 + 1) * S], E[:, q % 2, h, :], ident[0:S, 0:S])
                    mm.then_inc(s_pt, 1)

                scores(0)
                scores(1)
                flip(0)
                pe.wait_ge(s_V, i + 1)
                for q in range(G):
                    if q + 2 < G:
                        scores(q + 2)
                    if q + 1 < G:
                        flip_next = q + 1
                    pe.wait_ge(s_PTa, i * G + (q + 1))
                    pe.wait_ge(s_PTv, i * G + (q + 1))
                    if q >= 1:
                        pe.wait_ge(s_x3, i * G + q)
                    for h in range(HEADS):
                        mm = pe.matmul(ps[0:S, 0, h * (DH + 1):(h + 1) * (DH + 1)], PT[:, q % 2, h, :], V[:, q, h, :],
                                       start=True, stop=True)
                    mm.then_inc(s_av, 1)
                    if q + 1 < G:
                        flip(flip_next)
                    pe.wait_ge(s_ao, i * G + (q + 1))
                    for k in range(2):
                        mm = pe.transpose(ps[0:HD, 1, k * S:(k + 1) * S],
                                          ao[:, q % 2].rearrange("p h d -> p (h d)")[:, k * HD:(k + 1) * HD], ident[0:S, 0:S])
                    mm.then_inc(s_at, 1)
                    pe.wait_ge(s_aoT, i * G + (q + 1))
                    for k in range(2):
                        mm = pe.matmul(ps[0:S, 0, 256:256 + D], aoT[:, k, :], wao[:, k, :], start=k == 0, stop=k == 1)
                    mm.then_inc(s_op, 1)
                pe.wait_ge(s_xn, i + 1)
                turn(xn, 2, s_tr2)
                pe.wait_ge(s_xnT, i + 1)
                for q in range(G):
                    for k in range(2):
                        mm = pe.matmul(ps[0:S, 4, q * EXPERTS:(q + 1) * EXPERTS], xnT[:, k, q * S:(q + 1) * S], wr[:, k, :],
                                       start=k == 0, stop=k == 1)
                mm.then_inc(s_lg, 1)

        @block.scalar
        def _(act):
            act.wait_ge(s_w, 112)
            act.activation(qb[:], vec[:, V_QB:V_QB + 3], ACT.Copy, scale=0.25).then_inc(s_qb, 1)
            act.wait_ge(s_qb, 1)
            with act.Fori(0, ROUNDS) as i:
                act.wait_ge(s_tr, i + 1)
                for k in range(2):
                    a = act.activation(x2T[:, k, :], ps[0:HD, k, 0:N], ACT.Identity,
                                       bias=vec[0:HD, V_LN1_B + k:V_LN1_B + k + 1], scale=vec[0:HD, V_LN1_G + k:V_LN1_G + k + 1])
                a.then_inc(s_x2T, 1)
                act.wait_ge(s_q, i + 1)
                for m in range(3):
                    a = act.activation(qT[:, m, :], ps[:, 2 + m, 0:N], ACT.Identity, bias=qb[:, m:m + 1], scale=0.25)
                a.then_inc(s_qT, 1)

                def soft(q):
                    act.wait_ge(s_E, i * G + (q + 1))
                    e = E[:, q % 2].rearrange("p h s -> p (h s)")
                    act.activation(e, e, ACT.Exp).then_inc(s_P, 1)

                soft(0)
                for q in range(G):
                    act.wait_ge(s_pt, i * G + (q + 1))
                    act.activation(PT[:, q % 2, 0:6, :].rearrange("p h s -> p (h s)"), ps[0:S, 6, 0:6 * S], ACT.Copy).then_inc(s_PTa, 1)
                    if q + 1 < G:
                        soft(q + 1)
                    act.wait_ge(s_at, i * G + (q + 1))
                    act.activation(aoT[:].rearrange("p k s -> p (k s)"), ps[0:HD, 1, 0:2 * S], ACT.Copy).then_inc(s_aoT, 1)
                act.wait_ge(s_tr2, i + 1)
                for k in range(2):
                    a = act.activation(xnT[:, k, :], ps[0:HD, 2 + k, 0:N], ACT.Identity,
                                       bias=vec[0:HD, V_LN2_B + k:V_LN2_B + k + 1], scale=vec[0:HD, V_LN2_G + k:V_LN2_G + k + 1])
                a.then_inc(s_xnT, 1)

        @block.vector
        def _(v):
            v.memset(zero[:], 0.0).then_inc(s_zero, 1)
            v.memset(V[:], 1.0)
            v.memset(kB[:], 0.0).then_inc(s_cst, 1)
            v.memset(nh[:], -0.5).then_inc(s_cst, 1)
            v.wait_ge(s_w, 112)
            v.wait_ge(s_cst, 2)
            with v.Fori(0, ROUNDS) as i:
                own = Own(v, s_own, i * K_V)
                for q in range(G):
                    b = bass.ds(i * G + q, 1)
                    h_, m_ = H[:, b, :].rearrange("p a c -> p (a c)"), mv[:, b, 0:1].rearrange("p a c -> p (a c)")
                    own.did(v.tensor_scalar(x[:, q, :], h_, m_, r1[:, b], ALU.subtract, ALU.mult))
                    n = v.tensor_scalar(x2[:, q, :], h_, m_, r12[:, b], ALU.subtract, ALU.mult)
                n.then_inc(s_x2, 1)
                v.wait_ge(s_k, i + 1)
                for m in range(3):
                    for j in range(4):
                        c = slice(32 * j, 32 * j + 32)
                        n = v.tensor_scalar(kB[c, m, :, j, :], ps[c, 5 + m, 0:N].rearrange("p (g s) -> p g s", g=G),
                                            vec[c, V_KB + m:V_KB + m + 1], None, ALU.add)
                n.then_inc(s_kT, 1)
                v.wait_ge(s_v, i + 1)
                bv = bro[:, 0:D].rearrange("p (a h d) -> p a h d", a=1, h=HEADS)
                for q in range(G):
                    n = v.tensor_tensor(V[:, q, :, 0:DH], ps[0:S, q // 2, (q % 2) * D:(q % 2 + 1) * D].rearrange("p (h d) -> p h d", h=HEADS),
                                        bv[:, 0], ALU.add)
                n.then_inc(s_V, 1)

                def centre(q):
                    v.wait_ge(s_s, i * G + (q + 1))
                    sc = ps[0:S, 2 + 2 * (q % 2):4 + 2 * (q % 2), 0:6 * S].rearrange("p a (h s) -> p a h s", h=6)
                    n = own.did(v.tensor_reduce(mx[:, q % 2, :].rearrange("p (a h) -> p a h", a=2), sc, AX.X, ALU.max))
                    own.need(n)
                    if q >= 2:
                        v.wait_ge(s_pt, i * G + (q - 1))
                    for a in range(2):
                        n = v.tensor_tensor(E[:, q % 2, 6 * a:6 * a + 6, :], sc[:, a],
                                            mx[:, q % 2, 6 * a:6 * a + 6].rearrange("p (h a) -> p h a", a=1).broadcast_to([S, 6, S]),
                                            ALU.subtract)
                    n.then_inc(s_E, 1)

                centre(0)
                for q in range(G):
                    if q + 1 < G:
                        centre(q + 1)
                    v.wait_ge(s_pt, i * G + (q + 1))
                    v.tensor_copy(PT[:, q % 2, 6:12, :].rearrange("p h s -> p (h s)"), ps[0:S, 7, 0:6 * S]).then_inc(s_PTv, 1)
                    v.wait_ge(s_av, i * G + (q + 1))
                    o = ps[0:S, 0, 0:HEADS * (DH + 1)].rearrange("p (h d) -> p h d", h=HEADS)
                    n = own.did(v.reciprocal(rc[:].rearrange("p (h a) -> p h a", a=1), o[:, :, DH:DH + 1]))
                    own.need(n)
                    v.tensor_tensor(ao[:, q % 2], o[:, :, 0:DH], rc[:].rearrange("p (h a) -> p h a", a=1).broadcast_to([S, HEADS, DH]),
                                    ALU.mult).then_inc(s_ao, 1)
                    v.wait_ge(s_op, i * G + (q + 1))
                    if q == 0:
                        v.wait_ge(s_xb, i + 1)
                    v.tensor_tensor(x3[:, q, :], x[:, q, :], ps[0:S, 0, 256:256 + D], ALU.add).then_inc(s_x3, 1)
                v.wait_ge(s_x3, i * G + G)
                for q in range(G):
                    n = own.did(v.bn_stats(st[:, q, :], x3[:, q, :]))
                own.need(n)
                v.sem_inc(s_step, 1)
                for q in range(G):
                    n = own.did(v.bn_aggr(mg[:, q, :], st[:, q, :]))
                own.need(n)
                v.tensor_scalar(ms[:], mg[:, :, 1], 1e-5, None, ALU.add).then_inc(s_mg, 1)
                v.wait_ge(s_rr, i + 1)
                for q in range(G):
                    n = v.tensor_scalar(xn[:, q, :], x3[:, q, :], mg[:, q, 0:1], rr[:, q:q + 1], ALU.subtract, ALU.mult)
                n.then_inc(s_xn, 1)
                v.wait_ge(s_lg, i + 1)
                v.wait_ge(s_add, i + 1)
                n = own.did(v.tensor_tensor(L[:, bass.ds(i * G, G), :], ps[0:S, 4, 0:G * EXPERTS].rearrange("p (g e) -> p g e", g=G),
                                            bro[:, 2 * D:].rearrange("p (a e) -> p a e", a=1).broadcast_to([S, G, EXPERTS]), ALU.add))
                own.need(n)
                assert own.n == K_V, own.n

        @block.gpsimd
        def _(g):
            g.wait_ge(s_w, 112)
            g.wait_ge(s_cst, 2)
            with g.Fori(0, ROUNDS) as i:
                own = Own(g, s_ownp, i * K_G)
                g.wait_ge(s_x2, i + 1)
                g.tensor_tensor(x[:], x[:], bro[:, D:2 * D].rearrange("p (a c) -> p a c", a=1).broadcast_to([S, G, D]), ALU.add).then_inc(s_xb, 1)
                g.wait_ge(s_mg, i + 1)
                g.tensor_tensor(rr[:], ms[:], nh[:], ALU.pow).then_inc(s_rr, 1)
                hb = H[:, bass.ds(i * G, G), :]
                own.did(g.tensor_tensor(hb, hb, x3[:], ALU.add))
                g.wait_ge(s_xn, i + 1)
                n = own.did(g.tensor_copy(XN[:, bass.ds(i * G, G), :], xn[:]))
                own.need(n)
                g.sem_inc(s_add, 1)
                assert own.n == K_G, own.n


TILES = B * S * 2 // 128 + EXPERTS - 1


def experts(nc, H, XN, L, W1, W2, xs, ys, b2d, cst, vecs, eye, out):
    with ExitStack() as ctx:
        def sb(name, shape, dt=F32):
            return ctx.enter_context(nc.sbuf_tensor(name, shape, dt))

        def sem(name):
            return ctx.enter_context(nc.semaphore(name))

        BE = B * EXPERTS
        W = [S, B, EXPERTS]
        slot = [sb(f"slot{k}", [S, B], U32) for k in range(2)]
        gw = [sb(f"gw{k}", [S, B]) for k in range(2)]
        te = sb("te", [1, TILES + 1], I32)
        ident = sb("d_id", [128, 128]); vec = sb("d_vec", [128, V_N]); b2 = sb("b2", [1, EXPERTS, D]); one = sb("one", [1, 128])
        with ExitStack() as inner:
            def tb(name, shape, dt=F32):
                return inner.enter_context(nc.sbuf_tensor(name, shape, dt))

            c = tb("d_cst", [S, cst.shape[1]])
            m = [tb(f"d_m{k}", [S, B]) for k in range(2)]
            eq = tb("d_eq", W); t = tb("d_t", W); l2 = tb("d_l2", W)
            it = tb("d_it", [S, B]); sel = [tb(f"d_sel{k}", W) for k in range(2)]
            d_ = tb("d_d", [S, B]); e2 = tb("d_e2", [S, B]); M = tb("d_M", W)
            tot = tb("d_tot", [S, EXPERTS, B]); inc = tb("d_inc", [S, EXPERTS, B])
            nf = tb("d_nf", [S, EXPERTS]); ni = tb("d_ni", [S, EXPERTS], I32); nt = tb("d_nt", [S, EXPERTS]); ct = tb("d_ct", [S, EXPERTS])
            sl = tb("d_sl", W); sf = tb("d_sf", [S, B]); le = tb("d_le", [1, TILES + 1, EXPERTS]); tf = tb("d_tf", [1, TILES + 1])
            ps = inner.enter_context(nc.psum_tensor("d_ps", [128, 2, BANK], F32))
            s_w = sem("d_w"); s_own = sem("d_own"); s_d = sem("d_ds"); s_e2 = sem("d_e2s"); s_M = sem("d_Ms"); s_pe = sem("d_pe")
            s_slot = sem("d_slot"); s_sc = sem("d_sc")
            tri, ones, iota_e, keep, iota_t = (c[:, a:b] for a, b in ((0, S), (S, 2 * S), (2 * S, 2 * S + 8),
                                                                      (2 * S + 8, 2 * S + 8 + BE), (2 * S + 8 + BE, 2 * S + 8 + BE + TILES + 1)))
            block = inner.enter_context(nc.Block())

            @block.sync
            def _(sp):
                sp.dma_start(c[:], cst).then_inc(s_w, 16)
                sp.dma_start(ident[:], eye).then_inc(s_w, 16)
                sp.dma_start(vec[:], vecs).then_inc(s_w, 16)
                sp.dma_start(b2[:], b2d.rearrange("(a e) d -> a e d", a=1)).then_inc(s_w, 16)
                sp.wait_ge(s_w, 64)

            @block.tensor
            def _(pe):
                pe.wait_ge(s_w, 64)
                pe.wait_ge(s_M, 1)
                mm_ = M[:].rearrange("p b e -> p (b e)")
                pe.matmul(ps[0:S, 0, 0:BE], tri, mm_, start=True, stop=True)
                pe.matmul(ps[0:S, 1, 0:BE], ones, mm_, start=True, stop=True).then_inc(s_pe, 1)

            @block.scalar
            def _(act):
                act.wait_ge(s_d, 1)
                act.activation(e2[:], d_[:], ACT.Exp).then_inc(s_e2, 1)

            @block.vector
            def _(v):
                own = Own(v, s_own)

                def do(ins):
                    own.need(own.did(ins))

                def col(a):
                    return a.rearrange("p (b a) -> p b a", a=1).broadcast_to(W)

                ie = iota_e.rearrange("p (a e) -> p a e", a=1).broadcast_to(W)
                v.wait_ge(s_w, 64)
                src = L
                for k in range(2):
                    do(v.tensor_reduce(m[k][:], src[:], AX.X, ALU.max))
                    do(v.tensor_tensor(eq[:], src[:], col(m[k][:]), ALU.is_equal))
                    do(v.scalar_tensor_tensor(t[:], eq[:], -float(EXPERTS), ie, ALU.mult, ALU.add))
                    do(v.tensor_reduce(it[:], t[:], AX.X, ALU.min))
                    do(v.tensor_tensor(sel[k][:], t[:], col(it[:]), ALU.is_equal))
                    if k == 0:
                        do(v.scalar_tensor_tensor(l2[:], sel[0][:], -3.0e38, L[:], ALU.mult, ALU.add))
                        src = l2
                do(v.tensor_tensor(M[:], sel[0][:], sel[1][:], ALU.add))
                v.sem_inc(s_M, 1)
                do(v.tensor_tensor(d_[:], m[1][:], m[0][:], ALU.subtract))
                v.sem_inc(s_d, 1)
                v.wait_ge(s_e2, 1)
                do(v.tensor_scalar(d_[:], e2[:], 1.0, None, ALU.add))
                do(v.reciprocal(gw[0][:], d_[:]))
                do(v.tensor_tensor(gw[1][:], e2[:], gw[0][:], ALU.mult))
                v.wait_ge(s_pe, 1)
                do(v.tensor_copy(tot[:], ps[0:S, 1, 0:BE].rearrange("p (b e) -> p e b", e=EXPERTS)))
                do(v.tensor_tensor_scan(inc[:].rearrange("p e b -> p (e b)"), keep, tot[:].rearrange("p e b -> p (e b)"),
                                        0.0, ALU.mult, ALU.add))
                do(v.tensor_scalar(ni[:], inc[:, :, B - 1], 127.0, None, ALU.add))
                do(v.tensor_scalar(ni[:], ni[:], 7, None, ALU.arith_shift_right))
                do(v.tensor_copy(nt[:], ni[:]))
                do(v.tensor_tensor_scan(ct[:], ones[:, 0:EXPERTS], nt[:], 0.0, ALU.mult, ALU.add))
                do(v.tensor_tensor(inc[:], inc[:], tot[:], ALU.subtract))
                do(v.tensor_tensor(nf[:], ct[:], nt[:], ALU.subtract))
                do(v.tensor_scalar(nf[:], nf[:], 128.0, None, ALU.mult))
                do(v.tensor_tensor(inc[:], inc[:], nf[:].rearrange("p (e a) -> p e a", a=1).broadcast_to([S, EXPERTS, B]), ALU.add))
                do(v.tensor_tensor(sl[:], ps[0:S, 0, 0:BE].rearrange("p (b e) -> p b e", e=EXPERTS), inc[:].rearrange("p e b -> p b e"), ALU.add))
                for k in range(2):
                    do(v.tensor_tensor(t[:], sel[k][:], sl[:], ALU.mult))
                    do(v.tensor_reduce(sf[:], t[:], AX.X, ALU.add))
                    do(v.tensor_copy(slot[k][:], sf[:]))
                v.sem_inc(s_slot, 1)
                TW = [1, TILES + 1, EXPERTS]
                do(v.tensor_tensor(le[:], ct[0:1].rearrange("p (a e) -> p a e", a=1).broadcast_to(TW),
                                   iota_t[0:1].rearrange("p (t a) -> p t a", a=1).broadcast_to(TW), ALU.is_le))
                do(v.tensor_reduce(tf[:], le[:], AX.X, ALU.add))
                do(v.tensor_scalar(te[:], tf[:], float(EXPERTS - 1), None, ALU.min))
                do(v.memset(one[:], 1.0))

            @block.gpsimd
            def _(g):
                g.wait_ge(s_slot, 1)
                for b in range(B):
                    for k in range(2):
                        g.indirect_dma_start(out=xs, out_offset=bass.IndirectOffsetOnAxis(ap=slot[k][:, b:b + 1], axis=0),
                                             in_=XN[:, b, :], in_offset=None).then_inc(s_sc, 16)
                g.wait_ge(s_sc, 16 * 2 * B)

        with ExitStack() as inner:
            def tb(name, shape, dt=F32):
                return inner.enter_context(nc.sbuf_tensor(name, shape, dt))

            xg = tb("xg", [128, 2, D]); xT = tb("xT", [HD + 1, 2, 2, 128]); hb = tb("hb", [128, 2, DFF])
            hT = tb("hT_", [128, 2, KF, 128]); yt = tb("yt", [128, 2, D])
            ps = inner.enter_context(nc.psum_tensor("e_ps", [128, 8, BANK], F32))
            s_xg = [sem("e_xg0"), sem("e_xg1")]; s_st = [sem("e_st0"), sem("e_st1")]
            s_cst = sem("e_cst"); s_tx = sem("e_tx"); s_xT = sem("e_xT"); s_h = sem("e_h"); s_ge = sem("e_ge")
            s_ht = sem("e_ht"); s_hT = sem("e_hT"); s_y = sem("e_y"); s_yt = sem("e_yt")
            block = inner.enter_context(nc.Block())

            @block.sync
            def _(sp):
                for p in range(2):
                    sp.sem_inc(s_st[p], 16)
                    sp.dma_start(xg[:, p, :], xs[p * 128:(p + 1) * 128, :]).then_inc(s_xg[p], 16)
                with sp.Fori(0, TILES // 2) as i:
                    for p in range(2):
                        sp.wait_ge(s_tx, i * 2 + (p + 1))
                        sp.dma_start(xg[:, p, :], xs[bass.ds((i * 2 + (p + 2)) * 128, 128), :]).then_inc(s_xg[p], 16)
                        sp.wait_ge(s_yt, i * 2 + (p + 1))
                        sp.dma_start(ys[bass.ds((i * 2 + p) * 128, 128), :], yt[:, p, :]).then_inc(s_st[p], 16)
                for p in range(2):
                    sp.wait_ge(s_st[p], 16 * (TILES // 2 + 1))
                    sp.wait_ge(s_xg[p], 16 * (TILES // 2 + 1))

            @block.tensor
            def _(pe):
                pe.wait_ge(s_cst, 2)

                def expert(j):
                    return pe.value_load(te[0:1, bass.ds(j, 1)] if not isinstance(j, int) else te[0:1, j:j + 1],
                                         min_val=0, max_val=EXPERTS - 1)

                def up(j, p, rounds):
                    pe.wait_ge(s_xg[p], rounds)
                    for k in range(2):
                        mm = pe.transpose(ps[0:HD, 0, k * 128:(k + 1) * 128], xg[:, p, k * HD:(k + 1) * HD], ident[:])
                    mm.then_inc(s_tx, 1)
                    e = expert(j)
                    pe.wait_ge(s_ge, j + 1)
                    pe.wait_ge(s_xT, j + 1)
                    for h in range(2):
                        for k in range(2):
                            c_ = slice(0, HD + k)
                            mm = pe.matmul(ps[:, 1 + 2 * p + h, 0:384], xT[c_, p, k, :],
                                           W1[c_, k, bass.ds(e, 1), h * 384:(h + 1) * 384].rearrange("p a n -> p (a n)"),
                                           start=k == 0, stop=k == 1)
                    mm.then_inc(s_h, 1)

                up(0, 0, 16)
                with pe.Fori(0, TILES // 2) as i:
                    for p in range(2):
                        j = i * 2 + p
                        up(j + 1, 1 - p, i * 16 + (16 if p == 0 else 32))
                        e = expert(j)
                        pe.wait_ge(s_ge, j + 3)
                        for k in range(KF):
                            mm = pe.transpose(ps[:, 5 + k // 3, (k % 3) * 128:(k % 3 + 1) * 128], hb[:, p, k * 128:(k + 1) * 128], ident[:])
                        mm.then_inc(s_ht, 1)
                        pe.wait_ge(s_hT, j + 1)
                        pe.matmul(ps[:, 7, 0:D], one[:], b2[:, bass.ds(e, 1), :].rearrange("p a n -> p (a n)"), start=True, stop=False)
                        for k in range(KF):
                            mm = pe.matmul(ps[:, 7, 0:D], hT[:, p, k, :], W2[:, k, bass.ds(e, 1), :].rearrange("p a n -> p (a n)"),
                                           start=False, stop=k == KF - 1)
                        mm.then_inc(s_y, 1)

            @block.scalar
            def _(act):
                act.sem_inc(s_ge, 2)
                act.wait_ge(s_cst, 2)

                def affine(j, p):
                    act.wait_ge(s_tx, j + 1)
                    for k in range(2):
                        a = act.activation(xT[0:HD, p, k, :], ps[0:HD, 0, k * 128:(k + 1) * 128], ACT.Identity,
                                           bias=vec[0:HD, V_LN2_B + k:V_LN2_B + k + 1], scale=vec[0:HD, V_LN2_G + k:V_LN2_G + k + 1])
                    a.then_inc(s_xT, 1)

                affine(0, 0)
                with act.Fori(0, TILES // 2) as i:
                    for p in range(2):
                        j = i * 2 + p
                        affine(j + 1, 1 - p)
                        act.wait_ge(s_h, j + 1)
                        act.activation(hb[:, p, :].rearrange("p (a n) -> p a n", a=2), ps[:, 1 + 2 * p:3 + 2 * p, 0:384], ACT.Gelu).then_inc(s_ge, 1)

            @block.vector
            def _(v):
                v.memset(xT[HD:HD + 1], 1.0).then_inc(s_cst, 1)
                v.memset(one[:], 1.0).then_inc(s_cst, 1)
                with v.Fori(0, TILES // 2) as i:
                    for p in range(2):
                        j = i * 2 + p
                        v.wait_ge(s_ht, j + 1)
                        v.tensor_copy(hT[:, p].rearrange("p (a k) n -> p a (k n)", a=2), ps[:, 5:7, 0:384]).then_inc(s_hT, 1)
                        v.wait_ge(s_y, j + 1)
                        v.wait_ge(s_st[p], i * 16 + 16)
                        v.tensor_copy(yt[:, p, :], ps[:, 7, 0:D]).then_inc(s_yt, 1)

        with ExitStack() as inner:
            def tb(name, shape, dt=F32):
                return inner.enter_context(nc.sbuf_tensor(name, shape, dt))

            gy = tb("gy", [S, G, 2, D]); o = tb("o_", [S, G, D])
            s_g = [sem(f"g_g{q}") for q in range(G)]; s_acc = sem("g_acc"); s_o = sem("g_o"); s_out = [sem(f"g_out{q}") for q in range(G)]
            block = inner.enter_context(nc.Block())

            @block.gpsimd
            def _(g):
                for b in range(B):
                    q = b % G
                    if b >= G:
                        g.wait_ge(s_o, b - G + 1)
                    for k in range(2):
                        g.indirect_dma_start(out=gy[:, q, k, :], out_offset=None, in_=ys,
                                             in_offset=bass.IndirectOffsetOnAxis(ap=slot[k][:, b:b + 1], axis=0)).then_inc(s_g[q], 16)

            @block.vector
            def _(v):
                for b in range(B):
                    q = b % G
                    v.wait_ge(s_g[q], 32 * (b // G + 1))
                    v.scalar_tensor_tensor(gy[:, q, 0, :], gy[:, q, 0, :], gw[0][:, b:b + 1], H[:, b, :], ALU.mult, ALU.add).then_inc(s_acc, 1)
                    v.wait_ge(s_acc, b + 1)
                    if b >= G:
                        v.wait_ge(s_out[q], 16 * (b // G))
                    v.scalar_tensor_tensor(o[:, q, :], gy[:, q, 1, :], gw[1][:, b:b + 1], gy[:, q, 0, :], ALU.mult, ALU.add).then_inc(s_o, 1)

            @block.sync
            def _(sp):
                for b in range(B):
                    sp.wait_ge(s_o, b + 1)
                    sp.dma_start(out[b], o[:, b % G, :]).then_inc(s_out[b % G], 16)
                for q in range(G):
                    sp.wait_ge(s_out[q], 16 * (B // G))
def _halves(a):
    import numpy as np
    a = np.asarray(a).reshape(192, -1)
    out = np.zeros((128, 2 * a.shape[1]), a.dtype)
    out[0:96, 0:a.shape[1]] = a[0:96]
    out[0:96, a.shape[1]:] = a[96:192]
    return out


def _mixed(loc, g):
    import numpy as np
    loc, g = np.asarray(loc).reshape(192, -1), np.asarray(g).reshape(192, -1)
    return np.stack([loc[0:128], np.concatenate([loc[128:192], g[128:192]]), g[0:128]], axis=1)


def _haar():
    import numpy as np
    bands, pixels = np.arange(256), np.arange(256)
    odd = np.zeros((256, 256), np.int64)
    for level in range(4):
        pair = (bands >> (2 * (3 - level))) & 3
        wide, high = pair >> 1, pair & 1
        row, col = (pixels // 16 >> level) & 1, (pixels % 16 >> level) & 1
        odd = odd + high[:, None] * row[None, :] + wide[:, None] * col[None, :]
    return np.where(odd % 2 == 1, -0.0625, 0.0625).astype(np.float32)


def _heads(a):
    import numpy as np
    a = np.asarray(a).reshape(12, 16, -1)
    out = np.zeros((12, 32, a.shape[2]), a.dtype)
    out[:, 0:16] = a
    return out.reshape(384, -1)


def _layout(x):
    import numpy as np
    t = {k.replace("L0_", ""): np.asarray(v) for k, v in x.items()}
    f32 = np.float32
    a = {}
    a["xcol"] = t["x"].reshape(32, 3, 7, 16, 7, 16).transpose(1, 3, 5, 0, 2, 4).reshape(768, 1568)
    a["w_pl"] = t["tok_pl_w"].reshape(192, 768).T
    a["w_pg"] = t["tok_pg_w1"].reshape(192, 256, 3).transpose(1, 2, 0)
    a["had"] = _haar()
    a["pw_mix"] = _mixed(t["tok_pl_pw"].reshape(192, 192).T, t["tok_pg_pw"].reshape(192, 192).T)
    a["w96"] = np.stack([t[n].reshape(192, 192).T.reshape(2, 96, 192)
                         for n in ("tok_pg_w2", "tok_f1_pw", "tok_f2_pw", "tok_f3_pw")]).transpose(2, 0, 1, 3)
    thirds = lambda v: v.reshape(3, 128).T
    bq, bk, bv = t["ffn_in_proj_b"].reshape(3, 192)
    cols = [_mixed(t["tok_pl_b"], t["tok_pg_b1"])[:, :, 0], _mixed(t["tok_pl_dw"], t["tok_pg_dw"]).reshape(128, 27)]
    cols += [_halves(t[n]) for n in ("tok_f1_dw", "tok_f2_dw", "tok_f3_dw", "tok_pl_pwb", "tok_pg_pwb", "tok_pg_b2",
                                     "tok_f1_pwb", "tok_f2_pwb", "tok_alpha", "attn_w_norm1", "attn_w_ffn_norm",
                                     "ffn_ln1_g", "ffn_ln1_b", "ffn_ln2_g", "ffn_ln2_b")]
    cols += [thirds(t["attn_b_dt"]), thirds(t["attn_D_skip"]), thirds(_heads(bq)), thirds(_heads(bk))]
    a["vecs"] = np.concatenate(cols, axis=1)
    a["pwb_row"], a["lng_row"], a["lnb_row"] = t["tok_f3_pwb"], t["tok_ln_g"], t["tok_ln_b"]
    a["cls_row"] = np.broadcast_to(t["tok_cls"].reshape(1, 192), (32, 192))
    a["txt"] = t["txt"]
    rows = lambda w, p: w.T.reshape(-1, p, w.shape[0]).transpose(1, 0, 2)
    a["w_zg"] = np.stack([rows(t["attn_W_in"], 96), rows(t["attn_W_gate"], 96)], axis=2)
    wx = t["attn_W_xproj"]
    a["w_x"] = rows(np.concatenate([wx[0:96]] + [wx[96:128]] * 3), 128)
    a["w_dt"] = t["attn_W_dt"].T
    a["a_log"] = t["attn_A_log"].reshape(3, 128, 16).transpose(1, 0, 2)
    a["w_o"] = rows(t["attn_W_out"], 128)
    a["w_ug"] = np.stack([rows(t["attn_W_gate_ffn"], 96), rows(t["attn_W_up"], 96)], axis=2)
    a["w_dn"] = rows(t["attn_W_down"], 128)
    a["onehot"] = np.tile(np.eye(32, dtype=f32), (3, 1))
    a["eye"] = np.eye(128, dtype=f32)
    wq, wk, wv = t["ffn_in_proj_w"].reshape(3, 192, 192)
    a["w_qk"] = rows(np.concatenate([_heads(wq), _heads(wk)]), 96).reshape(96, 2, 6, 128)
    a["w_v"], a["w_ao"], a["w_r"] = rows(wv, 96), rows(t["ffn_out_proj_w"], 96), rows(t["ffn_router_w"], 96)
    a["rows_c"] = np.concatenate([bv, t["ffn_out_proj_b"], t["ffn_router_b"]])
    w1 = np.zeros((97, 2, 8, 768), f32)
    w1[0:96] = t["ffn_w1"].reshape(8, 2, 96, 768).transpose(2, 1, 0, 3)
    w1[96, 1] = t["ffn_b1"]
    a["w1d"] = w1
    a["w2d"] = t["ffn_w2"].reshape(8, 6, 128, 192).transpose(2, 1, 0, 3)
    a["b2d"] = t["ffn_b2"]
    s = 82
    before = np.triu(np.ones((s, s), f32), 1)
    first = np.ones((8, 32), f32)
    first[:, 0] = 0
    wide = lambda v: np.broadcast_to(v.reshape(1, -1), (s, v.size))
    a["cst"] = np.concatenate([before, np.ones((s, s), f32), wide(np.arange(8, dtype=f32)), wide(first),
                               wide(np.arange(49, dtype=f32))], axis=1)
    return {k: np.ascontiguousarray(v) for k, v in a.items()}


def program(nc, io):
    xs = nc.dram_tensor("expert_in", ((TILES + 2) * 128, D), F32, kind="Internal").ap()
    ys = nc.dram_tensor("expert_out", (TILES * 128, D), F32, kind="Internal").ap()
    with nc.sbuf_tensor("H", [S, B, D], F32) as H:
        tokenizer(nc, H, io["xcol"], io["w_pl"], io["w_pg"], io["had"], io["pw_mix"], io["w96"], io["vecs"],
                  io["pwb_row"], io["lng_row"], io["lnb_row"], io["cls_row"], io["txt"])
        mamba(nc, H, io["w_zg"], io["w_x"], io["w_dt"], io["a_log"], io["w_o"], io["w_ug"], io["w_dn"], io["vecs"],
              io["onehot"], io["eye"])
        with (nc.sbuf_tensor("XN", [S, B, D], F32) as XN, nc.sbuf_tensor("L", [S, B, EXPERTS], F32) as L,
              nc.sbuf_tensor("W1", [HD + 1, 2, EXPERTS, DFF], F32) as W1,
              nc.sbuf_tensor("W2", [128, KF, EXPERTS, D], F32) as W2):
            attention(nc, H, XN, L, xs, io["w_qk"], io["w_v"], io["w_ao"], io["w_r"], io["rows_c"], io["vecs"], io["eye"],
                      W1, W2, io["w1d"], io["w2d"])
            experts(nc, H, XN, L, W1, W2, xs, ys, io["b2d"], io["cst"], io["vecs"], io["eye"], io["out"])


def kernel(**inputs):
    import concourse.bacc as _bacc
    from concourse.bass_utils import run_bass_kernel_spmd as _run

    nc = _bacc.Bacc("TRN2", target_bir_lowering=False, num_devices=1)
    arrays = _layout(inputs)
    io = {name: nc.dram_tensor(f"in_{name}", a.shape, mybir.dt.from_np(a.dtype), kind="ExternalInput").ap()
          for name, a in arrays.items()}
    io["out"] = nc.dram_tensor("out_0", (B, S, D), F32, kind="ExternalOutput").ap()
    program(nc, io)
    r = _run(nc, [{f"in_{name}": a for name, a in arrays.items()}], core_ids=[0])
    return r.results[0]["out_0"]
```

```python
from contextlib import ExitStack

import numpy as np

import concourse.bass as bass
from concourse import mybir

F32 = mybir.dt.float32
BF16 = mybir.dt.bfloat16
I32 = mybir.dt.int32
ALU = mybir.AluOpType
ACT = mybir.ActivationFunctionType
AX = mybir.AxisListType

B = 32
D = 192
HD = D // 2
GRID = 7
PATCHES = GRID * GRID
TXT = 32
S = 1 + PATCHES + TXT
PIX = 256
KW = 3 * PIX
KT = KW // 128
BANK = 512


class Own:

    def __init__(self, eng, sem, base=0):
        self.eng, self.sem, self.base, self.n = eng, sem, base, 0

    def did(self, ins):
        ins.then_inc(self.sem, 1)
        self.n += 1
        return self.n

    def need(self, n):
        self.eng.wait_ge(self.sem, self.base + n)


def retire(nc, sems):
    for s in sems:
        nc.sync.sem_clear(s)
    nc.all_engine_barrier()


V_CONV_B = 0
V_DW = 3
V_F_DW = 30
V_PL_PWB = 84
V_PG_PWB = 86
V_PG_B2 = 88
V_F1_B = 90
V_F2_B = 92
V_ALPHA = 94
V_NORM1 = 96
V_FFN_NORM = 98
V_LN1_G = 100
V_LN1_B = 102
V_LN2_G = 104
V_LN2_B = 106
V_B_DT = 108
V_DSKIP = 111
V_QB = 114
V_KB = 117
V_N = 120


def tokenizer(nc, H, xcol, w_pl, w_pg, had, pw_mix, w96, vecs, pwb_row, lng_row, lnb_row, cls_row, txt):
    CH = 4
    IM = B // CH
    NP = IM * PATCHES
    ROW = GRID + 1
    IMG = ROW * ROW
    PADC = IM * IMG
    EDGE = ROW + 1
    ROWS = IM * ROW - 1
    with ExitStack() as ctx:
        def sb(name, shape, dt=F32):
            return ctx.enter_context(nc.sbuf_tensor(name, shape, dt))

        sems = []

        def sem(name):
            sems.append(ctx.enter_context(nc.semaphore(name)))
            return sems[-1]

        wp = sb("wp", [128, 2, 3, D])
        hd = sb("hd", [128, 2, PIX])
        wc = sb("wc", [128, KT, 2 * D])
        pwm = sb("pwm", [128, 3, D])
        wf = sb("wf", [HD, 4, 2, D])
        vec = sb("vec", [128, V_N])
        gate = sb("gate", [HD, 8])
        xc = sb("xc", [128, 2, KT, NP])
        P1 = sb("P1", [128, 3, CH * PADC + 2 * EDGE])
        PF = [sb(f"PF{k}", [HD, 2, CH * PADC + 2 * EDGE]) for k in range(3)]
        D1 = sb("D1", [128, 3, IM * ROW, GRID])
        DF = [sb(f"DF{k}", [HD, 2, IM * ROW, GRID]) for k in range(3)]
        L2 = sb("L2", [HD, 2, CH, NP])
        LS = sb("LS", [HD, 2, NP])
        G2 = sb("G2", [HD, 2, NP])
        TG = sb("TG", [HD, 2, NP])
        R2 = sb("R2", [HD, 2, NP])
        T0 = P1[0:PATCHES].rearrange("p k n -> p (k n)")[:, 0:B * D].rearrange("p (b c) -> p b c", b=B)
        T1 = sb("T1", [PATCHES, 2, D])
        rows = sb("rows", [PATCHES, 3, D])
        st = sb("st", [PATCHES, 2, 6])
        mv = sb("mv", [PATCHES, B, 2])
        ve = sb("ve", [PATCHES, B])
        rs = sb("rs", [PATCHES, B])
        nh = sb("nh", [PATCHES, B])
        psC = ctx.enter_context(nc.psum_tensor("psC", [128, 3, BANK], F32))
        psA = ctx.enter_context(nc.psum_tensor("psA", [128, 2, BANK], F32))
        psB = ctx.enter_context(nc.psum_tensor("psB", [128, 2, BANK], F32))
        psF = ctx.enter_context(nc.psum_tensor("psF", [128, BANK], F32))

        s_wp = sem("a_wp"); s_small = sem("a_small"); s_wc = sem("a_wc"); s_x = [sem("a_x0"), sem("a_x1")]
        s_pad = sem("a_pad"); s_had = sem("a_had"); s_hadv = sem("a_hadv"); s_rows = sem("a_rows")
        s_conv = sem("a_conv"); s_gelu = sem("a_gelu"); s_dw1 = sem("a_dw1")
        s_loc = sem("a_loc"); s_g = sem("a_g"); s_lev = sem("a_lev"); s_gev = sem("a_gev")
        s_w2 = sem("a_w2"); s_tg = sem("a_tg"); s_h = sem("a_h"); s_gate = sem("a_gate")
        s_dwf = [sem(f"a_dwf{k}") for k in range(3)]
        s_f = [sem(f"a_f{k}") for k in range(3)]
        s_r1 = sem("a_r1"); s_r2 = sem("a_r2"); s_lr = sem("a_lr"); s_t0 = sem("a_t0")
        s_mv = sem("a_mv"); s_rs = sem("a_rs"); s_t1 = sem("a_t1"); s_out = sem("a_out"); s_cls = sem("a_cls")
        s_own = sem("a_own_dve"); s_ownp = sem("a_own_pool"); s_owna = sem("a_own_act")

        def padded(p, k, c):
            v = p[:, k, EDGE + c * PADC:EDGE + (c + 1) * PADC]
            return v.rearrange("p (i r c) -> p i r c", i=IM, r=ROW)[:, :, 0:GRID, 0:GRID]

        def tap(p, k, c, t):
            off = EDGE + c * PADC + (t // 3 - 1) * ROW + t % 3 - 1
            v = p[:, k, off:off + ROWS * ROW]
            return v.rearrange("p (r c) -> p r c", c=ROW)[:, :, 0:GRID]

        def dense(d, k):
            return d[:, k].rearrange("p (i r) c -> p i (r c)", r=ROW)[:, :, 0:PATCHES]

        WAVES = CH + 3
        ctx.callback(retire, nc, sems)
        block = ctx.enter_context(nc.Block())

        @block.sync
        def _(sp):
            sp.dma_start(wp[:], w_pg.rearrange("(t p) c o -> p t c o", p=128)).then_inc(s_wp, 16)
            sp.dma_start(hd[:], had.rearrange("(t p) x -> p t x", p=128)).then_inc(s_wp, 16)
            sp.dma_start(vec[:], vecs).then_inc(s_small, 16)
            for c in range(CH):
                if c >= 2:
                    sp.wait_ge(s_conv, c - 1)
                sp.dma_start(xc[:, c % 2], xcol.rearrange("(t p) n -> p t n", p=128)[:, :, c * NP:(c + 1) * NP]
                             ).then_inc(s_x[c % 2], 16)
            sp.dma_start(H[0:1, :, :], cls_row.rearrange("(a n) c -> a n c", a=1)).then_inc(s_cls, 16)
            sp.dma_start(H[1 + PATCHES:S, :, :], txt.rearrange("b t c -> t b c")).then_inc(s_cls, 16)
            for n in range(B // 2):
                sp.wait_ge(s_t1, n + 1)
                sp.dma_start(H[1:1 + PATCHES, 2 * n:2 * n + 2, :], T1[:]).then_inc(s_out, 16)
            sp.wait_ge(s_out, 16 * (B // 2))
            sp.wait_ge(s_cls, 32)

        @block.tensor
        def _(pe):
            pe.wait_ge(s_wp, 32)
            for ch in range(3):
                for xt in range(2):
                    n = 2 * ch + xt
                    if n >= 3:
                        pe.wait_ge(s_hadv, n - 2)
                    for bt in range(2):
                        mm = pe.matmul(psC[:, n % 3, 0:D], hd[:, bt, xt * 128:(xt + 1) * 128], wp[:, bt, ch, :],
                                       start=bt == 0, stop=bt == 1)
                    mm.then_inc(s_had, 1)
            pe.wait_ge(s_hadv, 6)
            pe.wait_ge(s_wc, 32)

            def conv(c):
                pe.wait_ge(s_x[c % 2], 16 * (c // 2 + 1))
                if c >= 1:
                    pe.wait_ge(s_gelu, c)
                for t in range(3):
                    for k in range(KT):
                        mm = pe.matmul(psC[:, t, 0:NP], wc[:, k, t * 128:(t + 1) * 128], xc[:, c % 2, k, :],
                                       start=k == 0, stop=k == KT - 1)
                mm.then_inc(s_conv, 1)

            def pair(ps, w, d):
                for m in range(2):
                    for k in range(2):
                        mm = pe.matmul(ps[0:HD, m, 0:NP], w[:, k, m * HD:(m + 1) * HD], d(k),
                                       start=k == 0, stop=k == 1)
                return mm

            conv(0)
            for w in range(WAVES):
                if w + 1 < CH:
                    conv(w + 1)
                if w < CH:
                    if w == 0:
                        pe.wait_ge(s_small, 16 * 3)
                    pe.wait_ge(s_dw1, w + 1)
                    if w > 0:
                        pe.wait_ge(s_tg, w)
                    if w > 2:
                        pe.wait_ge(s_r2, w - 2)
                    for m in range(2):
                        pe.matmul(psA[0:HD, m, 0:NP], pwm[:, 0, m * HD:(m + 1) * HD], dense(D1, 0),
                                  start=True, stop=False)
                        mm = pe.matmul(psA[0:HD, m, 0:NP], pwm[0:64, 1, m * HD:(m + 1) * HD], dense(D1, 1)[0:64],
                                       start=False, stop=True)
                    mm.then_inc(s_loc, 1)
                    if w > 1:
                        pe.wait_ge(s_r1, w - 1)
                    for m in range(2):
                        pe.matmul(psB[0:HD, m, 0:NP], pwm[:, 2, m * HD:(m + 1) * HD], dense(D1, 2),
                                  start=True, stop=False)
                        mm = pe.matmul(psB[0:HD, m, 0:NP], pwm[64:128, 1, m * HD:(m + 1) * HD], dense(D1, 1)[64:128],
                                       start=False, stop=True)
                    mm.then_inc(s_g, 1)
                    pe.wait_ge(s_lev, w + 1)
                    pe.wait_ge(s_gev, w + 1)
                    pair(psA, wf[:, 0], lambda k: G2[:, k, :]).then_inc(s_w2, 1)
                if 0 <= w - 1 < CH:
                    c = w - 1
                    pe.wait_ge(s_dwf[0], c + 1)
                    pe.wait_ge(s_gev, min(w + 1, CH))
                    if c > 0:
                        pe.wait_ge(s_r1, c)
                    pair(psB, wf[:, 1], lambda k: dense(DF[0], k)).then_inc(s_f[0], 1)
                if 0 <= w - 2 < CH:
                    c = w - 2
                    pe.wait_ge(s_dwf[1], c + 1)
                    pe.wait_ge(s_tg, min(w + 1, CH))
                    if c > 0:
                        pe.wait_ge(s_r2, c)
                    pair(psA, wf[:, 2], lambda k: dense(DF[1], k)).then_inc(s_f[1], 1)
                if 0 <= w - 3 < CH:
                    c = w - 3
                    pe.wait_ge(s_dwf[2], c + 1)
                    for n in range(IM // 2):
                        if c * IM // 2 + n > 0:
                            pe.wait_ge(s_t0, c * IM // 2 + n)
                        for j in range(2):
                            for k in range(2):
                                mm = pe.matmul(psF[0:PATCHES, j * D:(j + 1) * D], dense(DF[2], k)[:, 2 * n + j, :],
                                               wf[:, 3, k, :], start=k == 0, stop=k == 1)
                        mm.then_inc(s_f[2], 1)

        @block.scalar
        def _(act):
            act.dma_start(wc[:, :, 0:128], w_pl.rearrange("(t p) o -> p t o", p=128)[:, :, 0:128]).then_inc(s_wc, 16)
            act.dma_start(wc[:, :, 128:192], w_pl.rearrange("(t p) o -> p t o", p=128)[:, :, 128:192]).then_inc(s_wc, 16)
            act.dma_start(pwm[:], pw_mix).then_inc(s_small, 16)
            act.dma_start(wf[:], w96).then_inc(s_small, 16)
            for k, row in enumerate((pwb_row, lng_row, lnb_row)):
                act.dma_start(rows[:, k, :], row.rearrange("(a c) -> a c", a=1).broadcast_to([PATCHES, D])).then_inc(s_rows, 16)
            act.wait_ge(s_small, 48)
            own = Own(act, s_owna)
            n = own.did(act.activation(gate[:, 0:2], vec[0:HD, V_ALPHA:V_ALPHA + 2], ACT.Tanh))
            own.need(n)
            own.did(act.activation(gate[:, 2:4], gate[:, 0:2], ACT.Copy, bias=0.5, scale=-0.5))
            n = own.did(act.activation(gate[:, 0:2], gate[:, 0:2], ACT.Copy, bias=0.5, scale=0.5))
            own.need(n)
            for k in range(2):
                own.did(act.activation(gate[:, 4 + k:5 + k], vec[0:HD, V_PG_B2 + k:V_PG_B2 + k + 1], ACT.Copy,
                                       scale=gate[:, k:k + 1]))
                n = own.did(act.activation(gate[:, 6 + k:7 + k], vec[0:HD, V_PL_PWB + k:V_PL_PWB + k + 1], ACT.Copy,
                                           scale=gate[:, 2 + k:3 + k]))
            own.need(n)

            def gelu(c):
                act.wait_ge(s_conv, c + 1)
                if c == 0:
                    act.wait_ge(s_pad, 1)
                for t in range(3):
                    i = act.activation(padded(P1, t, c), psC[:, t, 0:NP].rearrange("p (i r c) -> p i r c", i=IM, r=GRID),
                                       ACT.Gelu, bias=vec[:, V_CONV_B + t:V_CONV_B + t + 1])
                i.then_inc(s_gelu, 1)

            gelu(0)
            for w in range(WAVES):
                if w + 1 < CH:
                    gelu(w + 1)
                if w < CH:
                    act.wait_ge(s_loc, w + 1)
                    if w > 0:
                        act.wait_ge(s_h, w)
                        act.wait_ge(s_w2, w)
                    for k in range(2):
                        act.activation(L2[:, k, w, :], psA[0:HD, k, 0:NP], ACT.Identity,
                                       bias=vec[0:HD, V_PL_PWB + k:V_PL_PWB + k + 1])
                        i = act.activation(LS[:, k, :], psA[0:HD, k, 0:NP], ACT.Identity,
                                           bias=gate[:, 6 + k:7 + k], scale=gate[:, 2 + k:3 + k])
                    i.then_inc(s_lev, 1)
                    act.wait_ge(s_g, w + 1)
                    for k in range(2):
                        i = act.activation(G2[:, k, :], psB[0:HD, k, 0:NP], ACT.Gelu,
                                           bias=vec[0:HD, V_PG_PWB + k:V_PG_PWB + k + 1])
                    i.then_inc(s_gev, 1)
                    act.wait_ge(s_w2, w + 1)
                    for k in range(2):
                        i = act.activation(TG[:, k, :], psA[0:HD, k, 0:NP], ACT.Identity,
                                           bias=gate[:, 4 + k:5 + k], scale=gate[:, k:k + 1])
                    i.then_inc(s_tg, 1)
                if 0 <= w - 1 < CH:
                    c = w - 1
                    act.wait_ge(s_f[0], c + 1)
                    for k in range(2):
                        i = act.activation(padded(PF[1], k, c),
                                           psB[0:HD, k, 0:NP].rearrange("p (i r c) -> p i r c", i=IM, r=GRID),
                                           ACT.Relu, bias=vec[0:HD, V_F1_B + k:V_F1_B + k + 1])
                    i.then_inc(s_r1, 1)
                if 0 <= w - 2 < CH:
                    c = w - 2
                    act.wait_ge(s_f[1], c + 1)
                    if c > 0:
                        act.wait_ge(s_lr, c)
                    for k in range(2):
                        i = act.activation(R2[:, k, :], psA[0:HD, k, 0:NP], ACT.Relu,
                                           bias=vec[0:HD, V_F2_B + k:V_F2_B + k + 1])
                    i.then_inc(s_r2, 1)

        @block.vector
        def _(v):
            own = Own(v, s_own)
            v.memset(P1[:], 0.0)
            for p in PF:
                i = v.memset(p[:], 0.0)
            i.then_inc(s_pad, 1)
            for n in range(6):
                v.wait_ge(s_had, n + 1)
                v.tensor_copy(wc[:, n, 256:384], psC[:, n % 3, 0:128])
                v.tensor_copy(wc[:, n, 192:256], psC[:, n % 3, 128:192]).then_inc(s_hadv, 1)
            v.wait_ge(s_small, 48)
            v.wait_ge(s_rows, 48)

            def dw(src, dst, n, c, col, done):
                last = [0] * n
                for t in range(9):
                    for k in range(n):
                        out, w = dst[:, k, 0:ROWS, :], vec[0:src.shape[0], col + 9 * k + t:col + 9 * k + t + 1]
                        if t == 0:
                            i = v.tensor_scalar(out, tap(src, k, c, t), w, None, ALU.mult)
                        else:
                            own.need(last[k])
                            i = v.scalar_tensor_tensor(out, tap(src, k, c, t), w, out, ALU.mult, ALU.add)
                        last[k] = own.did(i)
                own.need(last[n - 1])
                v.sem_inc(done, 1)

            for w in range(WAVES):
                if w < CH:
                    v.wait_ge(s_gelu, w + 1)
                    if w > 0:
                        v.wait_ge(s_g, w)
                    dw(P1, D1, 3, w, V_DW, s_dw1)
                if 0 <= w - 1 < CH:
                    v.wait_ge(s_h, w)
                    if w > 1:
                        v.wait_ge(s_f[0], w - 1)
                    dw(PF[0], DF[0], 2, w - 1, V_F_DW, s_dwf[0])
                if 0 <= w - 2 < CH:
                    v.wait_ge(s_r1, w - 1)
                    if w > 2:
                        v.wait_ge(s_f[1], w - 2)
                    dw(PF[1], DF[1], 2, w - 2, V_F_DW + 18, s_dwf[1])
                if 0 <= w - 3 < CH:
                    c = w - 3
                    v.wait_ge(s_lr, c + 1)
                    if c > 0:
                        v.wait_ge(s_f[2], c * IM // 2)
                    dw(PF[2], DF[2], 2, c, V_F_DW + 36, s_dwf[2])
                    for n in range(c * IM // 2, (c + 1) * IM // 2):
                        v.wait_ge(s_f[2], n + 1)
                        v.tensor_tensor(T0[:, 2 * n:2 * n + 2, :], psF[0:PATCHES, 0:2 * D].rearrange("p (j c) -> p j c", j=2),
                                        rows[:, 0:0+1, :].broadcast_to([PATCHES, 2, D]), ALU.add).then_inc(s_t0, 1)
                        v.wait_ge(s_t0, n + 1)
                        for j in range(2):
                            b = own.did(v.bn_stats(st[:, j, :], T0[:, 2 * n + j, :]))
                            own.need(b)
                            v.bn_aggr(mv[:, 2 * n + j, :], st[:, j, :]).then_inc(s_mv, 1)
            v.memset(nh[:], -0.5).then_inc(s_mv, 1)
            v.wait_ge(s_rs, 1)
            for n in range(B // 2):
                if n > 0:
                    v.wait_ge(s_out, 16 * n)
                for j in range(2):
                    b = 2 * n + j
                    i = own.did(v.tensor_scalar(T1[:, j, :], T0[:, b, :], mv[:, b, 0:1], rs[:, b:b + 1],
                                                ALU.subtract, ALU.mult))
                own.need(i)
                i = own.did(v.tensor_tensor(T1[:], T1[:], rows[:, 1:1+1, :].broadcast_to([PATCHES, 2, D]), ALU.mult))
                own.need(i)
                v.tensor_tensor(T1[:], T1[:], rows[:, 2:2+1, :].broadcast_to([PATCHES, 2, D]), ALU.add).then_inc(s_t1, 1)

        @block.gpsimd
        def _(g):
            own = Own(g, s_ownp)
            for w in range(WAVES):
                if w < CH:
                    g.wait_ge(s_tg, w + 1)
                    for k in range(2):
                        i = g.tensor_tensor(padded(PF[0], k, w), LS[:, k, :].rearrange("p (i r c) -> p i r c", i=IM, r=GRID),
                                            TG[:, k, :].rearrange("p (i r c) -> p i r c", i=IM, r=GRID), ALU.add)
                    i.then_inc(s_h, 1)
                if 0 <= w - 2 < CH:
                    c = w - 2
                    g.wait_ge(s_r2, c + 1)
                    for k in range(2):
                        i = g.tensor_tensor(padded(PF[2], k, c), L2[:, k, c, :].rearrange("p (i r c) -> p i r c", i=IM, r=GRID),
                                            R2[:, k, :].rearrange("p (i r c) -> p i r c", i=IM, r=GRID), ALU.add)
                    i.then_inc(s_lr, 1)
            g.wait_ge(s_mv, B + 1)
            n = own.did(g.tensor_scalar(ve[:], mv[:, :, 1], 1e-5, None, ALU.add))
            own.need(n)
            g.tensor_tensor(rs[:], ve[:], nh[:], ALU.pow).then_inc(s_rs, 1)


G = 4
N = G * S
ROUNDS = B // G
INNER = 384
NI = INNER // 128
STATE = 16
FFN = 512
NF = FFN // 128


def row_stats(nc, tag, H, eps2, r1, r12, mv):
    with ExitStack() as ctx:
        def sem(name):
            return ctx.enter_context(nc.semaphore(name))

        st = ctx.enter_context(nc.sbuf_tensor(f"{tag}_st_stats", [S, B, 6], F32))
        t = ctx.enter_context(nc.sbuf_tensor(f"{tag}_st_t", [S, B], F32))
        nh = ctx.enter_context(nc.sbuf_tensor(f"{tag}_st_nh", [S, B], F32))
        s_st = sem(f"{tag}_st_bn"); s_mv = sem(f"{tag}_st_mv"); s_p = sem(f"{tag}_st_pool")
        block = ctx.enter_context(nc.Block())

        @block.vector
        def _(v):
            v.memset(nh[:], -0.5)
            for b in range(B):
                v.bn_stats(st[:, b, :], H[:, b, :]).then_inc(s_st, 1)
            v.wait_ge(s_st, B)
            for b in range(B):
                v.bn_aggr(mv[:, b, :], st[:, b, :]).then_inc(s_mv, 1)
            v.wait_ge(s_mv, B)

        @block.gpsimd
        def _(g):
            own = Own(g, s_p)
            g.wait_ge(s_mv, B)
            n = own.did(g.tensor_scalar(t[:], mv[:, :, 1], 1e-5, None, ALU.add))
            own.need(n)
            n = own.did(g.tensor_tensor(r1[:], t[:], nh[:], ALU.pow))
            own.need(n)
            n = own.did(g.tensor_tensor(t[:], r1[:], r1[:], ALU.mult))
            own.need(n)
            n = own.did(g.tensor_tensor(t[:], t[:], mv[:, :, 1], ALU.mult))
            own.need(n)
            n = own.did(g.tensor_scalar(t[:], t[:], eps2, None, ALU.add))
            own.need(n)
            n = own.did(g.tensor_tensor(t[:], t[:], nh[:], ALU.pow))
            own.need(n)
            n = own.did(g.tensor_tensor(r12[:], t[:], r1[:], ALU.mult))
            own.need(n)


def at_least(eng, sem, value):
    if not isinstance(value, int) or value > 0:
        eng.wait_ge(sem, value)


def mamba(nc, H, w_zg, w_x, w_dt, a_log, w_o, w_ug, w_dn, vecs, onehot, eye):
    K_PRE, K_POST = 14, 13
    with ExitStack() as ctx:
        def sb(name, shape, dt=F32):
            return ctx.enter_context(nc.sbuf_tensor(name, shape, dt))

        def sem(name):
            return ctx.enter_context(nc.semaphore(name))

        mv = sb("b_mv", [S, B, 2]); r1 = sb("b_r1", [S, B]); r12 = sb("b_r12", [S, B])
        row_stats(nc, "b", H, 1e-6, r1, r12, mv)

        wzg = sb("wzg", [HD, 2, 2, INNER]); wx = sb("wx", [128, NI, 192]); wdt = sb("wdt", [HD, INNER])
        wo = sb("wo", [128, NI, D]); wug = sb("wug", [HD, 2, 2, FFN]); wdn = sb("wdn", [128, NF, D])
        A = sb("A", [128, NI, STATE]); vec = sb("b_vec", [128, V_N])
        oh = sb("oh", [HD, 2 * STATE]); sel = sb("sel", [HD, 2 * STATE, 128], BF16); ident = sb("b_id", [128, 128])
        nh = sb("b_nh", [S, G])
        xl = sb("xl", [S, 2, G, D]); hn = sb("hn", [S, G, D]); hT = sb("hT", [HD, 2, N])
        sg = sb("sg", [128, NI, N]); z = sb("z", [128, 2, NI * N]); dtin = sb("dtin", [HD, N])
        P3 = sb("P3", [HD, 2, N], BF16); Pm = sb("Pm", [HD, N], BF16); R = sb("R", [HD, N])
        xd = sb("xd", [128, NI, N]); ax = sb("ax", [128, NI, N]); u = sb("u", [128, NI, N]); lnw = sb("lnw", [128, NI, N])
        dt = sb("dt", [128, 2, NI, N]); dtz = sb("dtz", [128, 2, NI, N])
        RING = 4
        LONG = 8
        AHEAD = 3
        abar = sb("abar", [128, RING, NI, G, S]); Bb = sb("Bb", [128, RING, N]); Bx = sb("Bx", [128, RING, NI, N])
        hs = sb("hs", [128, LONG, NI, N])
        y = sb("y", [128, NI * N]); x1 = sb("x1", [S, G, D]); hf = sb("hf", [S, G, D]); hfT = sb("hfT", [HD, 2, N])
        th = sb("th", [128, 2, N]); av = sb("av", [128, NF, N])
        st = sb("b_st", [S, G, 6]); mg = sb("b_mg", [S, G, 2]); ms = sb("b_ms", [S, G]); rr = sb("b_rr", [S, G])
        ps = ctx.enter_context(nc.psum_tensor("b_ps", [128, 8, BANK], F32))
        GATE_AT, USE_AT = (8, 10, 11, 12), (9, 11, 12, 13)
        PAIRS = STATE // 2
        SIDE, BANK_B, BANK_C, BANK_Y = 4, 4, 5, 6
        HALF = NI * N // 2

        s_w = sem("b_w"); s_cst = sem("b_cst"); s_A = sem("b_A"); s_A2 = sem("b_A2")
        s_hn = sem("b_hn"); s_tr = sem("b_tr"); s_hT = sem("b_hT"); s_gt = sem("b_gt"); s_zi = sem("b_zi")
        s_sg = sem("b_sg"); s_z = sem("b_z"); s_xp = sem("b_xp"); s_dtin = sem("b_dtin"); s_hi = sem("b_hi")
        s_P3 = sem("b_P3"); s_dtp = sem("b_dtp"); s_xd = sem("b_xd"); s_ax = sem("b_ax"); s_u = sem("b_u"); s_ln = sem("b_ln")
        s_dt = sem("b_dt"); s_dtz = sem("b_dtz"); s_pb = sem("b_pb"); s_pc = sem("b_pc"); s_ab = sem("b_ab"); s_bb = sem("b_bb")
        s_bx = sem("b_bx"); s_scan = sem("b_scan"); s_hc = sem("b_hc"); s_ys = sem("b_ys"); s_y = sem("b_y")
        s_o = sem("b_o"); s_x1 = sem("b_x1"); s_st = sem("b_stat"); s_rr = sem("b_rr2"); s_hf = sem("b_hf"); s_tr2 = sem("b_tr2")
        s_hfT = sem("b_hfT"); s_g = sem("b_g"); s_up = sem("b_up"); s_th = sem("b_th"); s_av = sem("b_av"); s_dn = sem("b_dn")
        s_H = sem("b_H"); s_pre = sem("b_own_pre"); s_post = sem("b_own_post"); s_add = sem("b_add"); s_pair = sem("b_pair"); s_step = sem("b_step")
        block = ctx.enter_context(nc.Block())

        def f2(t):
            return t.rearrange("p a b -> p (a b)")

        NONE = (None, 2, None, 0, 0)
        TILES_ = [("RT0", 1, s_hT, 2, 1), ("RT1", 1, s_hT, 2, 2), ("RG1", 1, s_sg, 3, 2), ("RI1", 1, s_z, 3, 2),
                  ("RG0", 1, s_sg, 3, 1), ("RI0", 1, s_z, 3, 1), ("RG2", 1, s_sg, 3, 3), ("RI2", 1, s_z, 3, 3),
                  ("O0", 0, s_x1, 2, 1), ("O1", 0, s_x1, 2, 2), ("X0", 1, s_dtin, 1, 1), ("X1", 1, s_P3, 1, 1),
                  ("PT0", 0, s_hfT, 2, 1), ("PT1", 0, s_hfT, 2, 2), ("D0", 1, s_xd, 3, 1), ("D1", 1, s_xd, 3, 2),
                  ("G0", 0, s_av, 4, 1), ("U0", 0, s_av, 4, 1), ("D2", 1, s_xd, 3, 3), NONE,
                  ("G1", 0, s_av, 4, 2), ("U1", 0, s_av, 4, 2), ("G2", 0, s_av, 4, 3), ("U2", 0, s_av, 4, 3),
                  ("G3", 0, s_av, 4, 4), ("U3", 0, s_av, 4, 4), NONE, NONE,
                  ("N0", 0, s_H, 2, 1), ("N1", 0, s_H, 2, 2), NONE, NONE]
        PLACE = {t[0]: n for n, t in enumerate(TILES_)}

        def bank(name):
            return PLACE[name] % SIDE

        def program(engine, scan_first, step, pre, post, finish=lambda last: None):
            for s in range(STATE):
                pre(0, 0, s, None)
            scan_first()
            for s in range(STATE):
                step(0, 0, s, False)
                pre(1, 1, s, None)
            with engine.Fori(0, (ROUNDS - 2) // 2) as t:
                for par in (1, 0):
                    i = t * 2 + (2 - par)
                    for s in range(STATE):
                        step(i, par, s, False)
                        post(i - 1, 1 - par, s, i + 1)
                        pre(i + 1, 1 - par, s, i - 1)
            last = ROUNDS - 1
            for s in range(STATE):
                step(last, 1, s, True)
                post(last - 1, 0, s, None)
            finish(last)
            for s in range(STATE):
                post(last, 1, s, None)

        @block.sync
        def _(sp):
            for dst, src in ((wzg, w_zg), (wx, w_x), (wdt, w_dt), (A, a_log), (wo, w_o), (wug, w_ug), (wdn, w_dn),
                             (vec, vecs), (oh, onehot), (ident, eye)):
                sp.dma_start(dst[:], src).then_inc(s_w, 16)

        @block.tensor
        def _(pe):
            pe.wait_ge(s_w, 160)
            pe.wait_ge(s_cst, 3)

            def free(name, mine, other):
                n = PLACE[name]
                side = TILES_[n][1]
                for k in range(n - SIDE, -1, -SIDE):
                    _, kind, s_free, per, at = TILES_[k]
                    index = mine if kind == side else other
                    if kind < 2 and index is not None:
                        pe.wait_ge(s_free, index * per + at)
                        return

            def turn(src, names, done, mine, other):
                for k in range(2):
                    free(names[k], mine, other)
                    for q in range(G):
                        mm = pe.transpose(ps[0:HD, bank(names[k]), q * S:(q + 1) * S], src[:, q, k * HD:(k + 1) * HD],
                                          ident[0:S, 0:S])
                    mm.then_inc(done, 1)

            def pre(j, par, s, other):
                if s == 1:
                    pe.wait_ge(s_hn, j + 1)
                    turn(hn, ("RT0", "RT1"), s_tr, j, other)
                if s in (2, 3, 5):
                    m = (2, 3, 5).index(s)
                    if m == 0:
                        pe.wait_ge(s_hT, j * 2 + 2)
                    for w_, name, done in ((1, f"RG{m}", s_gt), (0, f"RI{m}", s_zi)):
                        free(name, j, other)
                        for k in range(2):
                            mm = pe.matmul(ps[:, bank(name), 0:N], wzg[:, k, w_, m * 128:(m + 1) * 128], hT[:, k, :],
                                           start=k == 0, stop=k == 1)
                        mm.then_inc(done, 1)
                if s == 7:
                    pe.wait_ge(s_z, j * 3 + 3)
                    for n in range(2):
                        free(f"X{n}", j, other)
                        for k in range(NI):
                            mm = pe.matmul(ps[0:HD, bank(f"X{n}"), 0:N], wx[:, k, n * 96:(n + 1) * 96], z[:, par, k * N:(k + 1) * N],
                                           start=k == 0, stop=k == NI - 1)
                        mm.then_inc(s_xp, 1)
                if s == 9:
                    pe.wait_ge(s_dtin, j + 1)
                    for m in range(NI):
                        free(f"D{m}", j, other)
                        pe.matmul(ps[:, bank(f"D{m}"), 0:N], wdt[:, m * 128:(m + 1) * 128], dtin[:], start=True, stop=True).then_inc(s_dtp, 1)

            def post(p, par, s, other):
                if s == 4:
                    pe.wait_ge(s_y, p + 1)
                    for h in range(2):
                        free(f"O{h}", p, other)
                        for q in range(2):
                            c = (2 * h + q) * S
                            for k in range(NI):
                                mm = pe.matmul(ps[0:S, bank(f"O{h}"), q * D:(q + 1) * D], y[:, k * N + c:k * N + c + S], wo[:, k, :],
                                               start=k == 0, stop=k == NI - 1)
                        mm.then_inc(s_o, 1)
                if s == 7:
                    pe.wait_ge(s_hf, p + 1)
                    turn(hf, ("PT0", "PT1"), s_tr2, p, other)
                if s in GATE_AT:
                    m = GATE_AT.index(s)
                    if m == 0:
                        pe.wait_ge(s_hfT, p * 2 + 2)
                    for w_, name, done in ((0, f"G{m}", s_g), (1, f"U{m}", s_up)):
                        free(name, p, other)
                        for k in range(2):
                            mm = pe.matmul(ps[:, bank(name), 0:N], wug[:, k, w_, m * 128:(m + 1) * 128], hfT[:, k, :],
                                           start=k == 0, stop=k == 1)
                        mm.then_inc(done, 1)
                if s == 14:
                    pe.wait_ge(s_av, p * 4 + 4)
                    for h in range(2):
                        free(f"N{h}", p, other)
                        for q in range(2):
                            c = (2 * h + q) * S
                            for k in range(NF):
                                mm = pe.matmul(ps[0:S, bank(f"N{h}"), q * D:(q + 1) * D], av[:, k, c:c + S], wdn[:, k, :],
                                               start=k == 0, stop=k == NF - 1)
                        mm.then_inc(s_dn, 1)

            def spread_b(i, par, t):
                at_least(pe, s_bb, i * STATE + t)
                if t % STATE == 0:
                    pe.wait_ge(s_P3, i + t // STATE + 1)
                pe.matmul(ps[:, BANK_B, 0:N], sel[:, t % STATE, :], P3[:, (par + t // STATE) % 2, :], start=True, stop=True).then_inc(s_pb, 1)

            def spread_c(i, par, t):
                at_least(pe, s_hc, i * STATE + t)
                pe.matmul(ps[:, BANK_C, 0:N], sel[:, STATE + t % STATE, :], P3[:, (par + t // STATE) % 2, :],
                          start=True, stop=True).then_inc(s_pc, 1)

            def first():
                spread_b(0, 0, 0)
                spread_c(0, 0, 0)
                spread_b(0, 0, 1)
                spread_b(0, 0, 2)

            def add_y(i, k):
                pe.wait_ge(s_pair, i * PAIRS + (k + 1))
                if k == 0:
                    at_least(pe, s_y, i)
                for h in range(2):
                    mm = pe.matmul(ps[:, BANK_Y + h, 0:HALF], ident[:], f2(hs[:, 2 * k % LONG])[:, h * HALF:(h + 1) * HALF],
                                   start=k == 0, stop=k == PAIRS - 1)
                mm.then_inc(s_ys, 1)

            def step(i, par, s, last):
                if not last or s + AHEAD < STATE:
                    spread_b(i, par, s + AHEAD)
                if s % 2 == 0 and s >= 4:
                    add_y(i, (s - 4) // 2)
                elif s in (0, 2) and (not isinstance(i, int) or i > 0):
                    add_y(i - 1, PAIRS - 2 + s // 2)
                if not last or s + 1 < STATE:
                    spread_c(i, par, s + 1)

            def finish(last):
                add_y(last, PAIRS - 2)
                add_y(last, PAIRS - 1)

            program(pe, first, step, pre, post, finish)

        @block.scalar
        def _(act):
            act.wait_ge(s_A2, 1)
            act.activation(f2(A[:]), f2(A[:]), ACT.Exp).then_inc(s_A, 1)
            act.wait_ge(s_A, 1)
            act.activation(f2(A[:]), f2(A[:]), ACT.Copy, scale=-1.0).then_inc(s_A, 1)
            act.wait_ge(s_A, 2)
            act.wait_ge(s_cst, 3)

            def pre(j, par, s, other):
                if s == 1:
                    for k in range(2):
                        act.wait_ge(s_tr, j * 2 + (k + 1))
                        act.activation(hT[:, k, :], ps[0:HD, bank(f"RT{k}"), 0:N], ACT.Identity, bias=0.0,
                                       scale=vec[0:HD, V_NORM1 + k:V_NORM1 + k + 1]).then_inc(s_hT, 1)
                if s in (2, 3, 5):
                    m = (2, 3, 5).index(s)
                    act.wait_ge(s_gt, j * 3 + (m + 1))
                    act.activation(sg[:, m, :], ps[:, bank(f"RG{m}"), 0:N], ACT.Tanh, scale=0.5).then_inc(s_sg, 1)
                if s == 7:
                    act.wait_ge(s_xp, j * 2 + 1)
                    act.activation(dtin[:], ps[0:HD, bank("X0"), 0:N], ACT.Copy).then_inc(s_dtin, 1)
                    act.wait_ge(s_xp, j * 2 + 2)
                    act.activation(P3[:, par, :], ps[0:HD, bank("X1"), 0:N], ACT.Copy).then_inc(s_hi, 1)
                if s == 9:
                    for m in range(NI):
                        act.wait_ge(s_dtp, j * 3 + (m + 1))
                        act.activation(xd[:, m, :], ps[:, bank(f"D{m}"), 0:N], ACT.Identity,
                                       bias=vec[:, V_B_DT + m:V_B_DT + m + 1]).then_inc(s_xd, 1)
                    act.wait_ge(s_xd, j * 3 + 3)
                    act.activation(f2(ax[:]), f2(xd[:]), ACT.Abs).then_inc(s_ax, 1)
                    act.wait_ge(s_ax, j + 1)
                    act.activation(f2(u[:]), f2(ax[:]), ACT.Exp, scale=-1.0).then_inc(s_u, 1)
                if s == 10:
                    act.wait_ge(s_u, j + 1)
                    act.activation(f2(lnw[:]), f2(u[:]), ACT.Ln, bias=1.0).then_inc(s_ln, 1)

            def post(p, par, s, other):
                if s == 7:
                    for k in range(2):
                        act.wait_ge(s_tr2, p * 2 + (k + 1))
                        act.activation(hfT[:, k, :], ps[0:HD, bank(f"PT{k}"), 0:N], ACT.Identity, bias=0.0,
                                       scale=vec[0:HD, V_FFN_NORM + k:V_FFN_NORM + k + 1]).then_inc(s_hfT, 1)
                if s in GATE_AT:
                    m = GATE_AT.index(s)
                    act.wait_ge(s_g, p * 4 + (m + 1))
                    act.activation(th[:, m % 2, :], ps[:, bank(f"G{m}"), 0:N], ACT.Tanh, scale=0.5).then_inc(s_th, 1)

            def decays(i, par, t):
                at_least(act, s_bx, i * STATE + t - (RING - 1))
                act.wait_ge(s_pb, i * STATE + (t + 1))
                act.activation(Bb[:, t % RING, :], ps[:, BANK_B, 0:N], ACT.Copy).then_inc(s_bb, 1)
                at_least(act, s_scan, i * STATE + t - (RING - 1))
                if t % STATE == 0:
                    act.wait_ge(s_dt, i + t // STATE + 1)
                for m in range(NI):
                    a = act.activation(abar[:, t % RING, m, :, 1:S],
                                       dt[:, (par + t // STATE) % 2, m, :].rearrange("p (g t) -> p g t", g=G)[:, :, 1:S],
                                       ACT.Exp, scale=A[:, m, t % STATE:t % STATE + 1])
                a.then_inc(s_ab, 1)

            def first():
                decays(0, 0, 0)
                decays(0, 0, 1)
                decays(0, 0, 2)

            def step(i, par, s, last):
                if not last or s + AHEAD < STATE:
                    decays(i, par, s + AHEAD)

            program(act, first, step, pre, post)

        @block.vector
        def _(v):
            v.memset(abar[:], 0.0).then_inc(s_cst, 1)
            v.memset(nh[:], -0.5).then_inc(s_cst, 1)
            v.wait_ge(s_w, 160)
            v.tensor_copy(sel[:], oh[:].rearrange("p (s a) -> p s a", a=1).broadcast_to([HD, 2 * STATE, 128])).then_inc(s_cst, 1)
            v.tensor_scalar(f2(A[:]), f2(A[:]), 80.0, None, ALU.min).then_inc(s_A2, 1)
            own_pre, own_post = Own(v, s_pre), Own(v, s_post)

            def rows_of(j, q):
                b = bass.ds(j * G + q, 1)
                return H[:, b, :].rearrange("p a c -> p (a c)"), mv[:, b, 0:1].rearrange("p a c -> p (a c)"), b

            def pre(j, par, s, other):
                own = own_pre
                if s == 0:
                    own.n, own.base = 0, j * K_PRE
                    for q in range(G):
                        h_, m_, b = rows_of(j, q)
                        n = v.tensor_scalar(hn[:, q, :], h_, m_, r12[:, b], ALU.subtract, ALU.mult)
                    n.then_inc(s_hn, 1)
                if s == 7:
                    for q in range(G):
                        h_, m_, b = rows_of(j, q)
                        own.did(v.tensor_scalar(xl[:, par, q, :], h_, m_, r1[:, b], ALU.subtract, ALU.mult))
                if s in (3, 4, 6):
                    m = (3, 4, 6).index(s)
                    v.wait_ge(s_sg, j * 3 + (m + 1))
                    n = own.did(v.tensor_scalar(sg[:, m, :], sg[:, m, :], 0.5, 0.5, ALU.mult, ALU.add))
                    own.need(n)
                    v.wait_ge(s_zi, j * 3 + (m + 1))
                    v.tensor_tensor(z[:, par, m * N:(m + 1) * N], sg[:, m, :], ps[:, bank(f"RI{m}"), 0:N], ALU.mult).then_inc(s_z, 1)
                if s == 8:
                    x_ = ps[:, bank("X1"), 0:N]
                    v.wait_ge(s_hi, j + 1)
                    own.did(v.tensor_tensor(R[32:64, :], x_[32:64], P3[32:64, par, :], ALU.subtract))
                    n = own.did(v.tensor_tensor(R[64:96, :], x_[64:96], P3[64:96, par, :], ALU.subtract))
                    own.need(n)
                    own.did(v.tensor_copy(P3[32:64, par, :], R[32:64, :]))
                    n = own.did(v.tensor_copy(Pm[64:96, :], R[64:96, :]))
                    own.need(n)
                    v.tensor_tensor(P3[64:96, par, :], R[64:96, :], Pm[64:96, :], ALU.subtract).then_inc(s_P3, 1)
                if s == 10:
                    v.wait_ge(s_u, j + 1)
                    n = own.did(v.tensor_scalar(f2(ax[:]), f2(u[:]), 1.0, None, ALU.add))
                    own.need(n)
                    own.did(v.scalar_tensor_tensor(f2(ax[:]), f2(ax[:]), -1.0, f2(u[:]), ALU.add, ALU.subtract, reverse1=True))
                if s == 11:
                    own.need(own.n)
                    v.wait_ge(s_ln, j + 1)
                    n = own.did(v.tensor_tensor(f2(ax[:]), f2(ax[:]), f2(lnw[:]), ALU.add))
                    own.need(n)
                    v.scalar_tensor_tensor(f2(dt[:, par]), f2(xd[:]), 0.0, f2(ax[:]), ALU.max, ALU.add).then_inc(s_dt, 1)
                if s == STATE - 1:
                    assert own.n == K_PRE, own.n

            def post(p, par, s, other):
                own = own_post
                if s == 3:
                    own.n, own.base = 0, p * K_POST
                    v.wait_ge(s_ys, p * PAIRS + PAIRS)
                    for h, m, a, b in ((0, 0, 0, N), (0, 1, N, HALF), (1, 1, HALF, 2 * N), (1, 2, 2 * N, 3 * N)):
                        n = v.scalar_tensor_tensor(y[:, a:b], z[:, par, a:b], vec[:, V_DSKIP + m:V_DSKIP + m + 1],
                                                   ps[:, BANK_Y + h, a - h * HALF:b - h * HALF], ALU.mult, ALU.add)
                    n.then_inc(s_y, 1)
                if s == 5:
                    for h in range(2):
                        v.wait_ge(s_o, p * 2 + (h + 1))
                        v.tensor_tensor(x1[:, 2 * h:2 * h + 2, :], xl[:, par, 2 * h:2 * h + 2, :],
                                        ps[0:S, bank(f"O{h}"), 0:2 * D].rearrange("p (j c) -> p j c", j=2), ALU.add).then_inc(s_x1, 1)
                    v.wait_ge(s_x1, p * 2 + 2)
                    for q in range(G):
                        n = own.did(v.bn_stats(st[:, q, :], x1[:, q, :]))
                    own.need(n)
                    v.sem_inc(s_step, 1)
                    for q in range(G):
                        n = own.did(v.bn_aggr(mg[:, q, :], st[:, q, :]))
                    own.need(n)
                    n = own.did(v.tensor_tensor(ms[:], mg[:, :, 0], mg[:, :, 0], ALU.mult))
                    own.need(n)
                    v.scalar_tensor_tensor(ms[:], ms[:], 1e-6, mg[:, :, 1], ALU.add, ALU.add).then_inc(s_st, 1)
                if s == 6:
                    v.wait_ge(s_rr, p + 1)
                    for q in range(G):
                        n = v.tensor_scalar(hf[:, q, :], x1[:, q, :], rr[:, q:q + 1], None, ALU.mult)
                    n.then_inc(s_hf, 1)
                if s in USE_AT:
                    m = USE_AT.index(s)
                    v.wait_ge(s_th, p * 4 + (m + 1))
                    n = own.did(v.scalar_tensor_tensor(th[:, m % 2, :], th[:, m % 2, :], 1.0, ps[:, bank(f"G{m}"), 0:N], ALU.add, ALU.mult))
                    own.need(n)
                    v.wait_ge(s_up, p * 4 + (m + 1))
                    v.scalar_tensor_tensor(av[:, m, :], th[:, m % 2, :], 0.5, ps[:, bank(f"U{m}"), 0:N], ALU.mult, ALU.mult).then_inc(s_av, 1)
                if s == 15:
                    v.wait_ge(s_add, p + 1)
                    for h in range(2):
                        v.wait_ge(s_dn, p * 2 + (h + 1))
                        v.tensor_tensor(H[:, bass.ds(p * G + 2 * h, 2), :], x1[:, 2 * h:2 * h + 2, :],
                                        ps[0:S, bank(f"N{h}"), 0:2 * D].rearrange("p (j c) -> p j c", j=2), ALU.add).then_inc(s_H, 1)
                if s == STATE - 1:
                    assert own.n == K_POST, own.n

            def scan(i, t):
                v.wait_ge(s_ab, i * STATE + (t + 1))
                v.wait_ge(s_bx, i * STATE + (t + 1))
                if t % 2 == 0:
                    at_least(v, s_ys, i * PAIRS + (t - LONG) // 2 + 1)
                v.tensor_tensor_scan(f2(hs[:, t % LONG]), abar[:, t % RING].rearrange("p m g t -> p (m g t)"), f2(Bx[:, t % RING]),
                                     0.0, ALU.mult, ALU.add).then_inc(s_scan, 1)

            def first():
                scan(0, 0)

            def step(i, par, s, last):
                v.wait_ge(s_scan, i * STATE + (s + 1))
                v.wait_ge(s_pc, i * STATE + (s + 1))
                v.tensor_tensor(hs[:, s % LONG], hs[:, s % LONG],
                                ps[:, BANK_C, 0:N].rearrange("p (a n) -> p a n", a=1).broadcast_to([128, NI, N]),
                                ALU.mult).then_inc(s_hc, 1)
                if not last or s + 1 < STATE:
                    scan(i, s + 1)

            program(v, first, step, pre, post)
            v.wait_ge(s_H, 2 * ROUNDS)

        @block.gpsimd
        def _(g):
            g.wait_ge(s_cst, 3)

            def pre(j, par, s, other):
                if s == 11:
                    g.wait_ge(s_dt, j + 1)
                    g.tensor_tensor(f2(dtz[:, par]), f2(dt[:, par]), z[:, par, :], ALU.mult).then_inc(s_dtz, 1)

            def post(p, par, s, other):
                if s == 5:
                    g.wait_ge(s_st, p + 1)
                    g.tensor_tensor(rr[:], ms[:], nh[:], ALU.pow).then_inc(s_rr, 1)
                if s == 7:
                    g.wait_ge(s_hf, p + 1)
                    for k in range(2):
                        n = g.tensor_tensor(x1[:, 2 * k:2 * k + 2, :], x1[:, 2 * k:2 * k + 2, :],
                                            H[:, bass.ds(p * G + 2 * k, 2), :], ALU.add)
                    n.then_inc(s_add, 1)

            def inputs(i, par, t):
                g.wait_ge(s_bb, i * STATE + (t + 1))
                at_least(g, s_scan, i * STATE + t - (RING - 1))
                if t % STATE == 0:
                    g.wait_ge(s_dtz, i + t // STATE + 1)
                g.tensor_tensor(Bx[:, t % RING], dtz[:, (par + t // STATE) % 2],
                                Bb[:, t % RING, :].rearrange("p (a n) -> p a n", a=1).broadcast_to([128, NI, N]),
                                ALU.mult).then_inc(s_bx, 1)

            def first():
                inputs(0, 0, 0)
                inputs(0, 0, 1)
                inputs(0, 0, 2)

            def add_pair(i, k):
                g.wait_ge(s_hc, i * STATE + (2 * k + 2))
                a = f2(hs[:, 2 * k % LONG])
                g.tensor_tensor(a, a, f2(hs[:, (2 * k + 1) % LONG]), ALU.add).then_inc(s_pair, 1)

            def step(i, par, s, last):
                if s % 2 == 0 and s > 0:
                    add_pair(i, s // 2 - 1)
                elif s == 0 and (not isinstance(i, int) or i > 0):
                    add_pair(i - 1, PAIRS - 1)
                if not last or s + AHEAD < STATE:
                    inputs(i, par, s + AHEAD)

            program(g, first, step, pre, post, lambda last: add_pair(last, PAIRS - 1))


HEADS = 12
DH = 16
EXPERTS = 8
DFF = 768
KF = DFF // 128
U32 = mybir.dt.uint32


def attention(nc, H, XN, L, xs, w_qk, w_v, w_ao, w_r, rows_c, vecs, eye, W1, W2, w1d, w2d):
    K_TAIL = 9
    with ExitStack() as ctx:
        def sb(name, shape, dt=F32):
            return ctx.enter_context(nc.sbuf_tensor(name, shape, dt))

        def sem(name):
            return ctx.enter_context(nc.semaphore(name))

        mv = sb("c_mv", [S, B, 2]); r1 = sb("c_r1", [S, B]); r12 = sb("c_r12", [S, B])
        row_stats(nc, "c", H, 1e-5, r1, r12, mv)

        wqk = sb("wqk", [HD, 2, 6, 128]); wv = sb("wv", [HD, 2, D]); wao = sb("wao", [HD, 2, D]); wr = sb("wr", [HD, 2, EXPERTS])
        bro = sb("bro", [S, 2 * D + EXPERTS]); vec = sb("c_vec", [128, V_N]); ident = sb("c_id", [128, 128])
        qb = sb("qb", [128, 3]); nh = sb("c_nh", [S, G]); zero = sb("c_zero", [128, D])
        x2 = sb("c_x2", [S, G, D]); x2T = sb("x2T", [HD, 2, N])
        qT = sb("qT", [128, 2, 3, N]); kB = sb("kB", [128, 3, G, 4, S]); V = sb("V", [S, 2, G, HEADS, DH + 1])
        x = sb("c_x", [S, 2, D])
        mx = sb("mx", [S, 2, HEADS]); E = sb("E", [S, 2, HEADS, S]); PT = sb("PT", [S, 2, HEADS, S])
        rc = sb("rc", [S, 2, HEADS]); ao = sb("ao", [S, 2, HEADS, DH]); aoT = sb("aoT", [HD, 2, 2, S])
        x3 = sb("x3", [S, G, D]); st = sb("c_st", [S, G, 6]); mg = sb("c_mg", [S, G, 2]); ms = sb("c_ms", [S, G])
        rr = sb("c_rr", [S, G]); xn = x2; xnT = sb("xnT", [HD, 2, N])
        ps = ctx.enter_context(nc.psum_tensor("c_ps", [128, 8, BANK], F32))
        SCORES, FLIP, HEAD_OUT, SIDE0 = 0, 2, 4, 6

        s_w = sem("c_w"); s_e = sem("c_e"); s_cst = sem("c_cst"); s_qb = sem("c_qb"); s_x2 = sem("c_x2s"); s_tr = sem("c_tr")
        s_x2T = sem("c_x2T"); s_q = sem("c_q"); s_k = sem("c_k"); s_qT = sem("c_qT"); s_kT = sem("c_kT"); s_v = sem("c_v")
        s_V = sem("c_V"); s_s = sem("c_s"); s_mx = sem("c_mx"); s_E = sem("c_E"); s_P = sem("c_P"); s_pt = sem("c_pt"); s_PTa = sem("c_PTa")
        s_PTv = sem("c_PTv"); s_av = sem("c_av"); s_rc = sem("c_rc"); s_ao = sem("c_ao"); s_at = sem("c_at"); s_aoT = sem("c_aoT"); s_op = sem("c_op")
        s_x = sem("c_xs"); s_xb = sem("c_xb"); s_x3 = sem("c_x3"); s_mg = sem("c_mgs"); s_rr = sem("c_rrs"); s_xn = sem("c_xn2"); s_tr2 = sem("c_tr2")
        s_xnT = sem("c_xnT"); s_lg = sem("c_lg"); s_L = sem("c_L"); s_add = sem("c_add")
        s_own = sem("c_own_dve"); s_zero = sem("c_zs"); s_step = sem("c_step")
        block = ctx.enter_context(nc.Block())

        SIDE_TILES = [("RT0", 1, s_x2T, 2, 1), ("RT1", 1, s_x2T, 2, 2), ("Q0", 1, s_qT, 3, 1), ("Q1", 1, s_qT, 3, 2),
                      ("Q2", 1, s_qT, 3, 3), ("V0", 1, s_V, 2, 1), ("V1", 1, s_V, 2, 2), ("K0", 1, s_kT, 3, 1),
                      ("K1", 1, s_kT, 3, 2), ("K2", 1, s_kT, 3, 3), ("T0", 0, s_xnT, 2, 1), ("T1", 0, s_xnT, 2, 2),
                      ("LG", 0, s_L, 1, 1)]
        PLACE = {t[0]: n for n, t in enumerate(SIDE_TILES)}

        def bank(name):
            return SIDE0 + PLACE[name] % 2

        def flat(a):
            return a.rearrange("p h s -> p (h s)")

        def behind(i, q, d):
            r, at = (i, q - d) if q >= d else (i - 1, q - d + G)
            return None if isinstance(r, int) and not 0 <= r < ROUNDS else (r, at)

        def program(engine, step, front, tail):
            for q in range(G):
                front(0, 0, q)

            def round_(i, par, has_front, has_tail):
                for q in range(G):
                    step(i, par, q)
                    if has_front:
                        front(i + 1, 1 - par, q)
                    if has_tail:
                        tail(i - 1, 1 - par, q, has_front)

            round_(0, 0, True, False)
            with engine.Fori(0, (ROUNDS - 2) // 2) as t:
                for par in (1, 0):
                    round_(t * 2 + (2 - par), par, True, True)
            round_(ROUNDS - 1, 1, False, True)
            round_(ROUNDS, 0, False, True)

        @block.sync
        def _(sp):
            for dst, src in ((wqk, w_qk), (wv, w_v), (wao, w_ao), (wr, w_r), (vec, vecs), (ident, eye)):
                sp.dma_start(dst[:], src).then_inc(s_w, 16)
            sp.dma_start(bro[:], rows_c.rearrange("(a n) -> a n", a=1).broadcast_to([S, 2 * D + EXPERTS])).then_inc(s_w, 16)
            sp.wait_ge(s_zero, 1)
            sp.dma_start(xs.rearrange("(n p) c -> p n c", p=128),
                         zero[:].rearrange("p (a c) -> p a c", a=1).broadcast_to([128, xs.shape[0] // 128, D])).then_inc(s_e, 16)
            for e in range(EXPERTS):
                sp.dma_start(W1[:, :, e, :], w1d[:, :, e, :]).then_inc(s_e, 16)
                sp.dma_start(W2[:, :, e, :], w2d[:, :, e, :]).then_inc(s_e, 16)
            sp.wait_ge(s_e, 16 * (1 + 2 * EXPERTS))

        @block.tensor
        def _(pe):
            pe.wait_ge(s_w, 112)
            pe.wait_ge(s_cst, 2)

            def free(name, front_round, tail_round):
                for k in range(PLACE[name] - 2, -1, -2):
                    _, kind, s_free, per, at = SIDE_TILES[k]
                    index = front_round if kind == 1 else tail_round
                    if index is not None:
                        pe.wait_ge(s_free, index * per + at)
                        return

            def turn(src, names, done, front_round, tail_round):
                for k in range(2):
                    free(names[k], front_round, tail_round)
                    for q in range(G):
                        mm = pe.transpose(ps[0:HD, bank(names[k]), q * S:(q + 1) * S], src[:, q, k * HD:(k + 1) * HD],
                                          ident[0:S, 0:S])
                    mm.then_inc(done, 1)

            def project(name, m, done, j):
                free(name, j, None)
                for k in range(2):
                    mm = pe.matmul(ps[:, bank(name), 0:N], wqk[:, k, m, :], x2T[:, k, :], start=k == 0, stop=k == 1)
                mm.then_inc(done, 1)

            def front(j, par, q):
                if q == 0:
                    pe.wait_ge(s_x2, j + 1)
                    turn(x2, ("RT0", "RT1"), s_tr, j, None)
                if q == 1:
                    pe.wait_ge(s_x2T, j * 2 + 2)
                    for m in range(3):
                        project(f"Q{m}", m, s_q, j)
                if q == 2:
                    for h in range(2):
                        free(f"V{h}", j, None)
                        for c in range(2):
                            for k in range(2):
                                mm = pe.matmul(ps[0:S, bank(f"V{h}"), c * D:(c + 1) * D], x2T[:, k, (2 * h + c) * S:(2 * h + c + 1) * S],
                                               wv[:, k, :], start=k == 0, stop=k == 1)
                        mm.then_inc(s_v, 1)
                    project("K0", 3, s_k, j)
                    project("K1", 4, s_k, j)
                if q == 3:
                    project("K2", 5, s_k, j)

            def tail(p, par, q, has_front):
                if q == 3:
                    pe.wait_ge(s_xn, p + 1)
                    turn(xn, ("T0", "T1"), s_tr2, p + 2 if has_front else None, p)
                    pe.wait_ge(s_xnT, p * 2 + 2)
                    free("LG", None, p)
                    for q in range(G):
                        for k in range(2):
                            mm = pe.matmul(ps[0:S, bank("LG"), q * EXPERTS:(q + 1) * EXPERTS], xnT[:, k, q * S:(q + 1) * S], wr[:, k, :],
                                           start=k == 0, stop=k == 1)
                    mm.then_inc(s_lg, 1)

            def step(i, par, q):
                g = i * G + q
                if behind(i, q, 0):
                    if q == 0:
                        pe.wait_ge(s_qT, i * 3 + 3)
                        pe.wait_ge(s_kT, i * 3 + 3)
                    at_least(pe, s_E, g)
                    for h0, h1 in ((0, 4), (4, 6), (6, 8), (8, 12)):
                        m, j = h0 // 4, h0 % 4
                        mm = pe.matmul(ps[0:S, SCORES + h0 // 6, (h0 % 6) * S:(h0 % 6 + h1 - h0) * S],
                                       qT[:, par, m, q * S:(q + 1) * S], kB[:, m, q, j:j + h1 - h0, :].rearrange("p h s -> p (h s)"),
                                       start=True, stop=True)
                    mm.then_inc(s_s, 1)
                if behind(i, q, 2):
                    r, c = behind(i, q, 2)
                    vpar = par if q >= 2 else 1 - par
                    pe.wait_ge(s_PTa, r * G + (c + 1))
                    pe.wait_ge(s_PTv, r * G + (c + 1))
                    if c == 0:
                        pe.wait_ge(s_V, r * 2 + 2)
                    at_least(pe, s_x3, i * G + (q - 3))
                    for h in range(HEADS):
                        mm = pe.matmul(ps[0:S, HEAD_OUT + c % 2, h * (DH + 1):(h + 1) * (DH + 1)], PT[:, c % 2, h, :], V[:, vpar, c, h, :],
                                       start=True, stop=True)
                    mm.then_inc(s_av, 1)
                if behind(i, q, 3):
                    r, c = behind(i, q, 3)
                    pe.wait_ge(s_ao, r * G + (c + 1))
                    for k in range(2):
                        mm = pe.transpose(ps[0:HD, HEAD_OUT + c % 2, 256 + k * S:256 + (k + 1) * S],
                                          ao[:, c % 2].rearrange("p h d -> p (h d)")[:, k * HD:(k + 1) * HD], ident[0:S, 0:S])
                    mm.then_inc(s_at, 1)
                if behind(i, q, 1):
                    r, c = behind(i, q, 1)
                    pe.wait_ge(s_P, r * G + (c + 1))
                    for h in range(HEADS):
                        mm = pe.transpose(ps[0:S, FLIP + h // 6, (h % 6) * S:(h % 6 + 1) * S], E[:, c % 2, h, :], ident[0:S, 0:S])
                    mm.then_inc(s_pt, 1)
                if behind(i, q, 3):
                    r, c = behind(i, q, 3)
                    pe.wait_ge(s_aoT, r * G + (c + 1))
                    for k in range(2):
                        mm = pe.matmul(ps[0:S, HEAD_OUT + c % 2, 0:D], aoT[:, c % 2, k, :], wao[:, k, :], start=k == 0, stop=k == 1)
                    mm.then_inc(s_op, 1)

            program(pe, step, front, tail)

        @block.scalar
        def _(act):
            act.wait_ge(s_w, 112)
            act.wait_ge(s_cst, 2)
            act.activation(qb[:], vec[:, V_QB:V_QB + 3], ACT.Copy, scale=0.25).then_inc(s_qb, 1)
            act.wait_ge(s_qb, 1)

            def front(j, par, q):
                if q == 0:
                    for k in range(2):
                        act.wait_ge(s_tr, j * 2 + (k + 1))
                        act.activation(x2T[:, k, :], ps[0:HD, bank(f"RT{k}"), 0:N], ACT.Identity,
                                       bias=vec[0:HD, V_LN1_B + k:V_LN1_B + k + 1],
                                       scale=vec[0:HD, V_LN1_G + k:V_LN1_G + k + 1]).then_inc(s_x2T, 1)
                if q == 1:
                    for m in range(3):
                        act.wait_ge(s_q, j * 3 + (m + 1))
                        act.activation(qT[:, par, m, :], ps[:, bank(f"Q{m}"), 0:N], ACT.Identity, bias=qb[:, m:m + 1],
                                       scale=0.25).then_inc(s_qT, 1)
                if q == 3:
                    if not isinstance(j, int) or j > 0:
                        act.wait_ge(s_s, j * G)
                    for m in range(3):
                        act.wait_ge(s_k, j * 3 + (m + 1))
                        for h in range(4):
                            c = slice(32 * h, 32 * h + 32)
                            a = act.activation(kB[c, m, :, h, :], ps[c, bank(f"K{m}"), 0:N].rearrange("p (g s) -> p g s", g=G),
                                               ACT.Identity, bias=vec[c, V_KB + m:V_KB + m + 1])
                        a.then_inc(s_kT, 1)

            def tail(p, par, q, has_front):
                if q == 3:
                    for k in range(2):
                        act.wait_ge(s_tr2, p * 2 + (k + 1))
                        act.activation(xnT[:, k, :], ps[0:HD, bank(f"T{k}"), 0:N], ACT.Identity,
                                       bias=vec[0:HD, V_LN2_B + k:V_LN2_B + k + 1],
                                       scale=vec[0:HD, V_LN2_G + k:V_LN2_G + k + 1]).then_inc(s_xnT, 1)

            def step(i, par, q):
                if behind(i, q, 3):
                    r, c = behind(i, q, 3)
                    act.wait_ge(s_at, r * G + (c + 1))
                    act.activation(aoT[:, c % 2].rearrange("p k s -> p (k s)"), ps[0:HD, HEAD_OUT + c % 2, 256:256 + 2 * S],
                                   ACT.Copy).then_inc(s_aoT, 1)
                if behind(i, q, 1):
                    r, c = behind(i, q, 1)
                    act.wait_ge(s_pt, r * G + (c + 1))
                    act.activation(flat(PT[:, c % 2, 0:6, :]), ps[0:S, FLIP, 0:6 * S], ACT.Copy).then_inc(s_PTa, 1)
                if behind(i, q, 0):
                    act.wait_ge(s_E, i * G + (q + 1))
                    act.activation(flat(E[:, q % 2]), flat(E[:, q % 2]), ACT.Exp).then_inc(s_P, 1)

            program(act, step, front, tail)

        @block.vector
        def _(v):
            v.memset(zero[:], 0.0).then_inc(s_zero, 1)
            v.memset(V[:], 1.0)
            v.memset(kB[:], 0.0).then_inc(s_cst, 1)
            v.memset(nh[:], -0.5).then_inc(s_cst, 1)
            v.wait_ge(s_w, 112)
            v.wait_ge(s_cst, 2)

            def rows_of(j, q):
                b = bass.ds(j * G + q, 1)
                return H[:, b, :].rearrange("p a c -> p (a c)"), mv[:, b, 0:1].rearrange("p a c -> p (a c)"), b

            bv = bro[:, 0:D].rearrange("p (a h d) -> p a h d", a=1, h=HEADS)

            def front(j, par, q):
                if q == 2:
                    for h in range(2):
                        v.wait_ge(s_v, j * 2 + (h + 1))
                        for c in range(2):
                            n = v.tensor_tensor(V[:, par, 2 * h + c, :, 0:DH],
                                                ps[0:S, bank(f"V{h}"), c * D:(c + 1) * D].rearrange("p (h d) -> p h d", h=HEADS),
                                                bv[:, 0], ALU.add)
                        n.then_inc(s_V, 1)

            def rows_in(j):
                for c in range(G):
                    h_, m_, b = rows_of(j, c)
                    n = v.tensor_scalar(x2[:, c, :], h_, m_, r12[:, b], ALU.subtract, ALU.mult)
                n.then_inc(s_x2, 1)

            def tail(p, par, q, has_front):
                own = Own(v, s_own, p * K_TAIL)
                if q == 2:
                    v.wait_ge(s_x3, p * G + G)
                    for c in range(G):
                        n = own.did(v.bn_stats(st[:, c, :], x3[:, c, :]))
                    own.need(n)
                    v.sem_inc(s_step, 1)
                    for c in range(G):
                        n = own.did(v.bn_aggr(mg[:, c, :], st[:, c, :]))
                    own.need(n)
                    v.tensor_scalar(ms[:], mg[:, :, 1], 1e-5, None, ALU.add).then_inc(s_mg, 1)
                if q == 3:
                    own.n = 2 * G
                    v.wait_ge(s_lg, p + 1)
                    n = own.did(v.tensor_tensor(L[:, bass.ds(p * G, G), :], ps[0:S, bank("LG"), 0:G * EXPERTS].rearrange("p (g e) -> p g e", g=G),
                                                bro[:, 2 * D:].rearrange("p (a e) -> p a e", a=1).broadcast_to([S, G, EXPERTS]), ALU.add))
                    n_ = own.n
                    assert n_ == K_TAIL, n_
                    own.need(n)
                    v.sem_inc(s_L, 1)
                    v.wait_ge(s_add, p * 2 + 2)

            def tail_rows(p, par):
                v.wait_ge(s_rr, p + 1)
                for c in range(G):
                    n = v.tensor_scalar(xn[:, c, :], x3[:, c, :], mg[:, c, 0:1], rr[:, c:c + 1], ALU.subtract, ALU.mult)
                n.then_inc(s_xn, 1)

            def step(i, par, q):
                if q == 0 and (not isinstance(i, int) or i + 1 < ROUNDS):
                    rows_in(i + 1)
                if q == 3 and (not isinstance(i, int) or i > 0):
                    tail_rows(i - 1, 1 - par)
                if behind(i, q, 0):
                    v.wait_ge(s_s, i * G + (q + 1))
                    sc = ps[0:S, SCORES:SCORES + 2, 0:6 * S].rearrange("p a (h s) -> p a h s", h=6)
                    v.tensor_reduce(mx[:, q % 2, :].rearrange("p (a h) -> p a h", a=2), sc, AX.X, ALU.max).then_inc(s_mx, 1)
                    v.wait_ge(s_mx, i * G + (q + 1))
                    at_least(v, s_pt, i * G + (q - 1))
                    for a in range(2):
                        n = v.tensor_tensor(E[:, q % 2, 6 * a:6 * a + 6, :], sc[:, a],
                                            mx[:, q % 2, 6 * a:6 * a + 6].rearrange("p (h a) -> p h a", a=1).broadcast_to([S, 6, S]),
                                            ALU.subtract)
                    n.then_inc(s_E, 1)
                if behind(i, q, 2):
                    r, c = behind(i, q, 2)
                    v.wait_ge(s_av, r * G + (c + 1))
                    o = ps[0:S, HEAD_OUT + c % 2, 0:HEADS * (DH + 1)].rearrange("p (h d) -> p h d", h=HEADS)
                    v.reciprocal(rc[:, c % 2].rearrange("p (h a) -> p h a", a=1), o[:, :, DH:DH + 1]).then_inc(s_rc, 1)
                    v.wait_ge(s_rc, r * G + (c + 1))
                    v.tensor_tensor(ao[:, c % 2], o[:, :, 0:DH], rc[:, c % 2].rearrange("p (h a) -> p h a", a=1).broadcast_to([S, HEADS, DH]),
                                    ALU.mult).then_inc(s_ao, 1)
                if behind(i, q, 1):
                    r, c = behind(i, q, 1)
                    v.wait_ge(s_pt, r * G + (c + 1))
                    v.tensor_copy(flat(PT[:, c % 2, 6:12, :]), ps[0:S, FLIP + 1, 0:6 * S]).then_inc(s_PTv, 1)
                if behind(i, q, 3):
                    r, c = behind(i, q, 3)
                    v.wait_ge(s_op, r * G + (c + 1))
                    v.wait_ge(s_xb, r * G + (c + 1))
                    if c == 0 and (not isinstance(r, int) or r > 0):
                        v.wait_ge(s_add, r * 2 - 1)
                    v.tensor_tensor(x3[:, c, :], x[:, c % 2, :], ps[0:S, HEAD_OUT + c % 2, 0:D], ALU.add).then_inc(s_x3, 1)
                if behind(i, q, 2):
                    r, c = behind(i, q, 2)
                    h_, m_, b = rows_of(r, c)
                    v.tensor_scalar(x[:, c % 2, :], h_, m_, r1[:, b], ALU.subtract, ALU.mult).then_inc(s_x, 1)

            rows_in(0)
            program(v, step, front, tail)

        @block.gpsimd
        def _(g):
            g.wait_ge(s_w, 112)
            g.wait_ge(s_cst, 2)

            def front(j, par, q):
                pass

            def tail(p, par, q, has_front):
                if q == 2:
                    g.wait_ge(s_mg, p + 1)
                    g.tensor_tensor(rr[:], ms[:], nh[:], ALU.pow).then_inc(s_rr, 1)
                    hb = H[:, bass.ds(p * G, G), :]
                    g.tensor_tensor(hb, hb, x3[:], ALU.add).then_inc(s_add, 1)
                if q == 3:
                    g.wait_ge(s_xn, p + 1)
                    g.tensor_copy(XN[:, bass.ds(p * G, G), :], xn[:]).then_inc(s_add, 1)

            def step(i, par, q):
                if behind(i, q, 2):
                    r, c = behind(i, q, 2)
                    g.wait_ge(s_x, r * G + (c + 1))
                    g.tensor_tensor(x[:, c % 2, :], x[:, c % 2, :], bro[:, D:2 * D], ALU.add).then_inc(s_xb, 1)

            program(g, step, front, tail)
            g.wait_ge(s_add, 2 * ROUNDS)


TILES = B * S * 2 // 128 + EXPERTS - 1


def experts(nc, H, XN, L, W1, W2, xs, ys, b2d, cst, vecs, eye, out):
    with ExitStack() as ctx:
        def sb(name, shape, dt=F32):
            return ctx.enter_context(nc.sbuf_tensor(name, shape, dt))

        def sem(name):
            return ctx.enter_context(nc.semaphore(name))

        BE = B * EXPERTS
        W = [S, B, EXPERTS]
        slot = [sb(f"slot{k}", [S, B], U32) for k in range(2)]
        gw = [sb(f"gw{k}", [S, B]) for k in range(2)]
        te = sb("te", [1, TILES + 1], I32)
        ident = sb("d_id", [128, 128]); vec = sb("d_vec", [128, V_N]); b2 = sb("b2", [1, EXPERTS, D]); one = sb("one", [1, 128])
        with ExitStack() as inner:
            def tb(name, shape, dt=F32):
                return inner.enter_context(nc.sbuf_tensor(name, shape, dt))

            c = tb("d_cst", [S, cst.shape[1]])
            m = [tb(f"d_m{k}", [S, B]) for k in range(2)]
            eq = tb("d_eq", W); t = tb("d_t", W); l2 = tb("d_l2", W)
            it = tb("d_it", [S, B]); sel = [tb(f"d_sel{k}", W) for k in range(2)]
            d_ = tb("d_d", [S, B]); e2 = tb("d_e2", [S, B]); M = tb("d_M", W)
            tot = tb("d_tot", [S, EXPERTS, B]); inc = tb("d_inc", [S, EXPERTS, B])
            nf = tb("d_nf", [S, EXPERTS]); ni = tb("d_ni", [S, EXPERTS], I32); nt = tb("d_nt", [S, EXPERTS]); ct = tb("d_ct", [S, EXPERTS])
            sl = tb("d_sl", W); sf = tb("d_sf", [S, B]); le = tb("d_le", [1, TILES + 1, EXPERTS]); tf = tb("d_tf", [1, TILES + 1])
            ps = inner.enter_context(nc.psum_tensor("d_ps", [128, 2, BANK], F32))
            s_w = sem("d_w"); s_own = sem("d_own"); s_d = sem("d_ds"); s_e2 = sem("d_e2s"); s_M = sem("d_Ms"); s_pe = sem("d_pe")
            s_slot = sem("d_slot"); s_sc = sem("d_sc")
            tri, ones, iota_e, keep, iota_t = (c[:, a:b] for a, b in ((0, S), (S, 2 * S), (2 * S, 2 * S + 8),
                                                                      (2 * S + 8, 2 * S + 8 + BE), (2 * S + 8 + BE, 2 * S + 8 + BE + TILES + 1)))
            block = inner.enter_context(nc.Block())

            @block.sync
            def _(sp):
                sp.dma_start(c[:], cst).then_inc(s_w, 16)
                sp.dma_start(ident[:], eye).then_inc(s_w, 16)
                sp.dma_start(vec[:], vecs).then_inc(s_w, 16)
                sp.dma_start(b2[:], b2d.rearrange("(a e) d -> a e d", a=1)).then_inc(s_w, 16)
                sp.wait_ge(s_w, 64)

            @block.tensor
            def _(pe):
                pe.wait_ge(s_w, 64)
                pe.wait_ge(s_M, 1)
                mm_ = M[:].rearrange("p b e -> p (b e)")
                pe.matmul(ps[0:S, 0, 0:BE], tri, mm_, start=True, stop=True)
                pe.matmul(ps[0:S, 1, 0:BE], ones, mm_, start=True, stop=True).then_inc(s_pe, 1)

            @block.scalar
            def _(act):
                act.wait_ge(s_d, 1)
                act.activation(e2[:], d_[:], ACT.Exp).then_inc(s_e2, 1)

            @block.vector
            def _(v):
                own = Own(v, s_own)

                def do(ins):
                    own.need(own.did(ins))

                def col(a):
                    return a.rearrange("p (b a) -> p b a", a=1).broadcast_to(W)

                ie = iota_e.rearrange("p (a e) -> p a e", a=1).broadcast_to(W)
                v.wait_ge(s_w, 64)
                src = L
                for k in range(2):
                    do(v.tensor_reduce(m[k][:], src[:], AX.X, ALU.max))
                    do(v.tensor_tensor(eq[:], src[:], col(m[k][:]), ALU.is_equal))
                    do(v.scalar_tensor_tensor(t[:], eq[:], -float(EXPERTS), ie, ALU.mult, ALU.add))
                    do(v.tensor_reduce(it[:], t[:], AX.X, ALU.min))
                    do(v.tensor_tensor(sel[k][:], t[:], col(it[:]), ALU.is_equal))
                    if k == 0:
                        do(v.scalar_tensor_tensor(l2[:], sel[0][:], -3.0e38, L[:], ALU.mult, ALU.add))
                        src = l2
                do(v.tensor_tensor(M[:], sel[0][:], sel[1][:], ALU.add))
                v.sem_inc(s_M, 1)
                do(v.tensor_tensor(d_[:], m[1][:], m[0][:], ALU.subtract))
                v.sem_inc(s_d, 1)
                v.wait_ge(s_e2, 1)
                do(v.tensor_scalar(d_[:], e2[:], 1.0, None, ALU.add))
                do(v.reciprocal(gw[0][:], d_[:]))
                do(v.tensor_tensor(gw[1][:], e2[:], gw[0][:], ALU.mult))
                v.wait_ge(s_pe, 1)
                do(v.tensor_copy(tot[:], ps[0:S, 1, 0:BE].rearrange("p (b e) -> p e b", e=EXPERTS)))
                do(v.tensor_tensor_scan(inc[:].rearrange("p e b -> p (e b)"), keep, tot[:].rearrange("p e b -> p (e b)"),
                                        0.0, ALU.mult, ALU.add))
                do(v.tensor_scalar(ni[:], inc[:, :, B - 1], 127.0, None, ALU.add))
                do(v.tensor_scalar(ni[:], ni[:], 7, None, ALU.arith_shift_right))
                do(v.tensor_copy(nt[:], ni[:]))
                do(v.tensor_tensor_scan(ct[:], ones[:, 0:EXPERTS], nt[:], 0.0, ALU.mult, ALU.add))
                do(v.tensor_tensor(inc[:], inc[:], tot[:], ALU.subtract))
                do(v.tensor_tensor(nf[:], ct[:], nt[:], ALU.subtract))
                do(v.tensor_scalar(nf[:], nf[:], 128.0, None, ALU.mult))
                do(v.tensor_tensor(inc[:], inc[:], nf[:].rearrange("p (e a) -> p e a", a=1).broadcast_to([S, EXPERTS, B]), ALU.add))
                do(v.tensor_tensor(sl[:], ps[0:S, 0, 0:BE].rearrange("p (b e) -> p b e", e=EXPERTS), inc[:].rearrange("p e b -> p b e"), ALU.add))
                for k in range(2):
                    do(v.tensor_tensor(t[:], sel[k][:], sl[:], ALU.mult))
                    do(v.tensor_reduce(sf[:], t[:], AX.X, ALU.add))
                    do(v.tensor_copy(slot[k][:], sf[:]))
                v.sem_inc(s_slot, 1)
                TW = [1, TILES + 1, EXPERTS]
                do(v.tensor_tensor(le[:], ct[0:1].rearrange("p (a e) -> p a e", a=1).broadcast_to(TW),
                                   iota_t[0:1].rearrange("p (t a) -> p t a", a=1).broadcast_to(TW), ALU.is_le))
                do(v.tensor_reduce(tf[:], le[:], AX.X, ALU.add))
                do(v.tensor_scalar(te[:], tf[:], float(EXPERTS - 1), None, ALU.min))
                do(v.memset(one[:], 1.0))

            @block.gpsimd
            def _(g):
                g.wait_ge(s_slot, 1)
                for b in range(B):
                    for k in range(2):
                        g.indirect_dma_start(out=xs, out_offset=bass.IndirectOffsetOnAxis(ap=slot[k][:, b:b + 1], axis=0),
                                             in_=XN[:, b, :], in_offset=None).then_inc(s_sc, 16)
                g.wait_ge(s_sc, 16 * 2 * B)

        with ExitStack() as inner:
            def tb(name, shape, dt=F32):
                return inner.enter_context(nc.sbuf_tensor(name, shape, dt))

            xg = tb("xg", [128, 2, D]); xT = tb("xT", [HD + 1, 2, 2, 128]); hb = tb("hb", [128, 2, DFF])
            hT = tb("hT_", [128, 2, KF, 128]); yt = tb("yt", [128, 2, D])
            ps = inner.enter_context(nc.psum_tensor("e_ps", [128, 8, BANK], F32))
            s_xg = [sem("e_xg0"), sem("e_xg1")]; s_st = [sem("e_st0"), sem("e_st1")]
            s_cst = sem("e_cst"); s_tx = sem("e_tx"); s_xT = sem("e_xT"); s_h = sem("e_h"); s_ge = sem("e_ge")
            s_ht = sem("e_ht"); s_hT = sem("e_hT"); s_y = sem("e_y"); s_yt = sem("e_yt")
            block = inner.enter_context(nc.Block())

            @block.sync
            def _(sp):
                for p in range(2):
                    sp.sem_inc(s_st[p], 16)
                    sp.dma_start(xg[:, p, :], xs[p * 128:(p + 1) * 128, :]).then_inc(s_xg[p], 16)
                with sp.Fori(0, TILES // 2) as i:
                    for p in range(2):
                        sp.wait_ge(s_tx, i * 2 + (p + 1))
                        sp.dma_start(xg[:, p, :], xs[bass.ds((i * 2 + (p + 2)) * 128, 128), :]).then_inc(s_xg[p], 16)
                        sp.wait_ge(s_yt, i * 2 + (p + 1))
                        sp.dma_start(ys[bass.ds((i * 2 + p) * 128, 128), :], yt[:, p, :]).then_inc(s_st[p], 16)
                for p in range(2):
                    sp.wait_ge(s_st[p], 16 * (TILES // 2 + 1))
                    sp.wait_ge(s_xg[p], 16 * (TILES // 2 + 1))

            @block.tensor
            def _(pe):
                pe.wait_ge(s_cst, 2)

                def expert(j):
                    return pe.value_load(te[0:1, bass.ds(j, 1)] if not isinstance(j, int) else te[0:1, j:j + 1],
                                         min_val=0, max_val=EXPERTS - 1)

                def up(j, p, rounds):
                    pe.wait_ge(s_xg[p], rounds)
                    for k in range(2):
                        mm = pe.transpose(ps[0:HD, 0, k * 128:(k + 1) * 128], xg[:, p, k * HD:(k + 1) * HD], ident[:])
                    mm.then_inc(s_tx, 1)
                    e = expert(j)
                    pe.wait_ge(s_ge, j + 1)
                    pe.wait_ge(s_xT, j + 1)
                    for h in range(2):
                        for k in range(2):
                            c_ = slice(0, HD + k)
                            mm = pe.matmul(ps[:, 1 + 2 * p + h, 0:384], xT[c_, p, k, :],
                                           W1[c_, k, bass.ds(e, 1), h * 384:(h + 1) * 384].rearrange("p a n -> p (a n)"),
                                           start=k == 0, stop=k == 1)
                    mm.then_inc(s_h, 1)

                up(0, 0, 16)
                with pe.Fori(0, TILES // 2) as i:
                    for p in range(2):
                        j = i * 2 + p
                        up(j + 1, 1 - p, i * 16 + (16 if p == 0 else 32))
                        e = expert(j)
                        pe.wait_ge(s_ge, j + 3)
                        for k in range(KF):
                            mm = pe.transpose(ps[:, 5 + k // 3, (k % 3) * 128:(k % 3 + 1) * 128], hb[:, p, k * 128:(k + 1) * 128], ident[:])
                        mm.then_inc(s_ht, 1)
                        pe.wait_ge(s_hT, j + 1)
                        pe.matmul(ps[:, 7, 0:D], one[:], b2[:, bass.ds(e, 1), :].rearrange("p a n -> p (a n)"), start=True, stop=False)
                        for k in range(KF):
                            mm = pe.matmul(ps[:, 7, 0:D], hT[:, p, k, :], W2[:, k, bass.ds(e, 1), :].rearrange("p a n -> p (a n)"),
                                           start=False, stop=k == KF - 1)
                        mm.then_inc(s_y, 1)

            @block.scalar
            def _(act):
                act.sem_inc(s_ge, 2)
                act.wait_ge(s_cst, 2)

                def affine(j, p):
                    act.wait_ge(s_tx, j + 1)
                    for k in range(2):
                        a = act.activation(xT[0:HD, p, k, :], ps[0:HD, 0, k * 128:(k + 1) * 128], ACT.Identity,
                                           bias=vec[0:HD, V_LN2_B + k:V_LN2_B + k + 1], scale=vec[0:HD, V_LN2_G + k:V_LN2_G + k + 1])
                    a.then_inc(s_xT, 1)

                affine(0, 0)
                with act.Fori(0, TILES // 2) as i:
                    for p in range(2):
                        j = i * 2 + p
                        affine(j + 1, 1 - p)
                        act.wait_ge(s_h, j + 1)
                        act.activation(hb[:, p, :].rearrange("p (a n) -> p a n", a=2), ps[:, 1 + 2 * p:3 + 2 * p, 0:384], ACT.Gelu).then_inc(s_ge, 1)

            @block.vector
            def _(v):
                v.memset(xT[HD:HD + 1], 1.0).then_inc(s_cst, 1)
                v.memset(one[:], 1.0).then_inc(s_cst, 1)
                with v.Fori(0, TILES // 2) as i:
                    for p in range(2):
                        j = i * 2 + p
                        v.wait_ge(s_ht, j + 1)
                        v.tensor_copy(hT[:, p].rearrange("p (a k) n -> p a (k n)", a=2), ps[:, 5:7, 0:384]).then_inc(s_hT, 1)
                        v.wait_ge(s_y, j + 1)
                        v.wait_ge(s_st[p], i * 16 + 16)
                        v.tensor_copy(yt[:, p, :], ps[:, 7, 0:D]).then_inc(s_yt, 1)

        with ExitStack() as inner:
            def tb(name, shape, dt=F32):
                return inner.enter_context(nc.sbuf_tensor(name, shape, dt))

            gy = tb("gy", [S, G, 2, D]); o = tb("o_", [S, G, D])
            s_g = [sem(f"g_g{q}") for q in range(G)]; s_acc = sem("g_acc"); s_o = sem("g_o"); s_out = [sem(f"g_out{q}") for q in range(G)]
            block = inner.enter_context(nc.Block())

            @block.gpsimd
            def _(g):
                for b in range(B):
                    q = b % G
                    if b >= G:
                        g.wait_ge(s_o, b - G + 1)
                    for k in range(2):
                        g.indirect_dma_start(out=gy[:, q, k, :], out_offset=None, in_=ys,
                                             in_offset=bass.IndirectOffsetOnAxis(ap=slot[k][:, b:b + 1], axis=0)).then_inc(s_g[q], 16)

            @block.vector
            def _(v):
                for b in range(B):
                    q = b % G
                    v.wait_ge(s_g[q], 32 * (b // G + 1))
                    v.scalar_tensor_tensor(gy[:, q, 0, :], gy[:, q, 0, :], gw[0][:, b:b + 1], H[:, b, :], ALU.mult, ALU.add).then_inc(s_acc, 1)
                    v.wait_ge(s_acc, b + 1)
                    if b >= G:
                        v.wait_ge(s_out[q], 16 * (b // G))
                    v.scalar_tensor_tensor(o[:, q, :], gy[:, q, 1, :], gw[1][:, b:b + 1], gy[:, q, 0, :], ALU.mult, ALU.add).then_inc(s_o, 1)

            @block.sync
            def _(sp):
                for b in range(B):
                    sp.wait_ge(s_o, b + 1)
                    sp.dma_start(out[b], o[:, b % G, :]).then_inc(s_out[b % G], 16)
                for q in range(G):
                    sp.wait_ge(s_out[q], 16 * (B // G))
def _halves(a):
    import numpy as np
    a = np.asarray(a).reshape(192, -1)
    out = np.zeros((128, 2 * a.shape[1]), a.dtype)
    out[0:96, 0:a.shape[1]] = a[0:96]
    out[0:96, a.shape[1]:] = a[96:192]
    return out


def _mixed(loc, g):
    import numpy as np
    loc, g = np.asarray(loc).reshape(192, -1), np.asarray(g).reshape(192, -1)
    return np.stack([loc[0:128], np.concatenate([loc[128:192], g[128:192]]), g[0:128]], axis=1)


def _haar():
    import numpy as np
    bands, pixels = np.arange(256), np.arange(256)
    odd = np.zeros((256, 256), np.int64)
    for level in range(4):
        pair = (bands >> (2 * (3 - level))) & 3
        wide, high = pair >> 1, pair & 1
        row, col = (pixels // 16 >> level) & 1, (pixels % 16 >> level) & 1
        odd = odd + high[:, None] * row[None, :] + wide[:, None] * col[None, :]
    return np.where(odd % 2 == 1, -0.0625, 0.0625).astype(np.float32)


def _heads(a):
    import numpy as np
    a = np.asarray(a).reshape(12, 16, -1)
    out = np.zeros((12, 32, a.shape[2]), a.dtype)
    out[:, 0:16] = a
    return out.reshape(384, -1)


def _layout(x):
    import numpy as np
    t = {k.replace("L0_", ""): np.asarray(v) for k, v in x.items()}
    f32 = np.float32
    a = {}
    a["xcol"] = t["x"].reshape(32, 3, 7, 16, 7, 16).transpose(1, 3, 5, 0, 2, 4).reshape(768, 1568)
    a["w_pl"] = t["tok_pl_w"].reshape(192, 768).T
    a["w_pg"] = t["tok_pg_w1"].reshape(192, 256, 3).transpose(1, 2, 0)
    a["had"] = _haar()
    a["pw_mix"] = _mixed(t["tok_pl_pw"].reshape(192, 192).T, t["tok_pg_pw"].reshape(192, 192).T)
    a["w96"] = np.stack([t[n].reshape(192, 192).T.reshape(2, 96, 192)
                         for n in ("tok_pg_w2", "tok_f1_pw", "tok_f2_pw", "tok_f3_pw")]).transpose(2, 0, 1, 3)
    thirds = lambda v: v.reshape(3, 128).T
    bq, bk, bv = t["ffn_in_proj_b"].reshape(3, 192)
    cols = [_mixed(t["tok_pl_b"], t["tok_pg_b1"])[:, :, 0], _mixed(t["tok_pl_dw"], t["tok_pg_dw"]).reshape(128, 27)]
    cols += [_halves(t[n]) for n in ("tok_f1_dw", "tok_f2_dw", "tok_f3_dw", "tok_pl_pwb", "tok_pg_pwb", "tok_pg_b2",
                                     "tok_f1_pwb", "tok_f2_pwb", "tok_alpha", "attn_w_norm1", "attn_w_ffn_norm",
                                     "ffn_ln1_g", "ffn_ln1_b", "ffn_ln2_g", "ffn_ln2_b")]
    cols += [thirds(t["attn_b_dt"]), thirds(t["attn_D_skip"]), thirds(_heads(bq)), thirds(_heads(bk))]
    a["vecs"] = np.concatenate(cols, axis=1)
    a["pwb_row"], a["lng_row"], a["lnb_row"] = t["tok_f3_pwb"], t["tok_ln_g"], t["tok_ln_b"]
    a["cls_row"] = np.broadcast_to(t["tok_cls"].reshape(1, 192), (32, 192))
    a["txt"] = t["txt"]
    rows = lambda w, p: w.T.reshape(-1, p, w.shape[0]).transpose(1, 0, 2)
    a["w_zg"] = np.stack([rows(t["attn_W_in"], 96), rows(t["attn_W_gate"], 96)], axis=2)
    wx = t["attn_W_xproj"]
    a["w_x"] = rows(np.concatenate([wx[0:96]] + [wx[96:128]] * 3), 128)
    a["w_dt"] = t["attn_W_dt"].T
    a["a_log"] = t["attn_A_log"].reshape(3, 128, 16).transpose(1, 0, 2)
    a["w_o"] = rows(t["attn_W_out"], 128)
    a["w_ug"] = np.stack([rows(t["attn_W_gate_ffn"], 96), rows(t["attn_W_up"], 96)], axis=2)
    a["w_dn"] = rows(t["attn_W_down"], 128)
    a["onehot"] = np.tile(np.eye(32, dtype=f32), (3, 1))
    a["eye"] = np.eye(128, dtype=f32)
    wq, wk, wv = t["ffn_in_proj_w"].reshape(3, 192, 192)
    a["w_qk"] = rows(np.concatenate([_heads(wq), _heads(wk)]), 96).reshape(96, 2, 6, 128)
    a["w_v"], a["w_ao"], a["w_r"] = rows(wv, 96), rows(t["ffn_out_proj_w"], 96), rows(t["ffn_router_w"], 96)
    a["rows_c"] = np.concatenate([bv, t["ffn_out_proj_b"], t["ffn_router_b"]])
    w1 = np.zeros((97, 2, 8, 768), f32)
    w1[0:96] = t["ffn_w1"].reshape(8, 2, 96, 768).transpose(2, 1, 0, 3)
    w1[96, 1] = t["ffn_b1"]
    a["w1d"] = w1
    a["w2d"] = t["ffn_w2"].reshape(8, 6, 128, 192).transpose(2, 1, 0, 3)
    a["b2d"] = t["ffn_b2"]
    s = 82
    before = np.triu(np.ones((s, s), f32), 1)
    first = np.ones((8, 32), f32)
    first[:, 0] = 0
    wide = lambda v: np.broadcast_to(v.reshape(1, -1), (s, v.size))
    a["cst"] = np.concatenate([before, np.ones((s, s), f32), wide(np.arange(8, dtype=f32)), wide(first),
                               wide(np.arange(49, dtype=f32))], axis=1)
    return {k: np.ascontiguousarray(v) for k, v in a.items()}


def program(nc, io):
    xs = nc.dram_tensor("expert_in", ((TILES + 2) * 128, D), F32, kind="Internal").ap()
    ys = nc.dram_tensor("expert_out", (TILES * 128, D), F32, kind="Internal").ap()
    with nc.sbuf_tensor("H", [S, B, D], F32) as H:
        tokenizer(nc, H, io["xcol"], io["w_pl"], io["w_pg"], io["had"], io["pw_mix"], io["w96"], io["vecs"],
                  io["pwb_row"], io["lng_row"], io["lnb_row"], io["cls_row"], io["txt"])
        mamba(nc, H, io["w_zg"], io["w_x"], io["w_dt"], io["a_log"], io["w_o"], io["w_ug"], io["w_dn"], io["vecs"],
              io["onehot"], io["eye"])
        with (nc.sbuf_tensor("XN", [S, B, D], F32) as XN, nc.sbuf_tensor("L", [S, B, EXPERTS], F32) as L,
              nc.sbuf_tensor("W1", [HD + 1, 2, EXPERTS, DFF], F32) as W1,
              nc.sbuf_tensor("W2", [128, KF, EXPERTS, D], F32) as W2):
            attention(nc, H, XN, L, xs, io["w_qk"], io["w_v"], io["w_ao"], io["w_r"], io["rows_c"], io["vecs"], io["eye"],
                      W1, W2, io["w1d"], io["w2d"])
            experts(nc, H, XN, L, W1, W2, xs, ys, io["b2d"], io["cst"], io["vecs"], io["eye"], io["out"])


def kernel(**inputs):
    import concourse.bacc as _bacc
    from concourse.bass_utils import run_bass_kernel_spmd as _run

    nc = _bacc.Bacc("TRN2", target_bir_lowering=False, num_devices=1)
    arrays = _layout(inputs)
    io = {name: nc.dram_tensor(f"in_{name}", a.shape, mybir.dt.from_np(a.dtype), kind="ExternalInput").ap()
          for name, a in arrays.items()}
    io["out"] = nc.dram_tensor("out_0", (B, S, D), F32, kind="ExternalOutput").ap()
    program(nc, io)
    r = _run(nc, [{f"in_{name}": a for name, a in arrays.items()}], core_ids=[0])
    return r.results[0]["out_0"]
```

```python
from contextlib import ExitStack

import numpy as np

import concourse.bass as bass
from concourse import mybir

F32 = mybir.dt.float32
BF16 = mybir.dt.bfloat16
I32 = mybir.dt.int32
ALU = mybir.AluOpType
ACT = mybir.ActivationFunctionType
AX = mybir.AxisListType

B = 32
D = 192
HD = D // 2
GRID = 7
PATCHES = GRID * GRID
TXT = 32
S = 1 + PATCHES + TXT
PIX = 256
KW = 3 * PIX
KT = KW // 128
BANK = 512


class Own:

    def __init__(self, eng, sem, base=0):
        self.eng, self.sem, self.base, self.n = eng, sem, base, 0

    def did(self, ins):
        ins.then_inc(self.sem, 1)
        self.n += 1
        return self.n

    def need(self, n):
        self.eng.wait_ge(self.sem, self.base + n)


def retire(nc, sems):
    for s in sems:
        nc.sync.sem_clear(s)
    nc.all_engine_barrier()


V_CONV_B = 0
V_DW = 3
V_F_DW = 30
V_PL_PWB = 84
V_PG_PWB = 86
V_PG_B2 = 88
V_F1_B = 90
V_F2_B = 92
V_ALPHA = 94
V_NORM1 = 96
V_FFN_NORM = 98
V_LN1_G = 100
V_LN1_B = 102
V_LN2_G = 104
V_LN2_B = 106
V_B_DT = 108
V_DSKIP = 111
V_QB = 114
V_KB = 117
V_N = 120


def tokenizer(nc, H, xcol, w_pl, w_pg, had, pw_mix, w96, vecs, pwb_row, lng_row, lnb_row, cls_row, txt):
    CH = 4
    IM = B // CH
    NP = IM * PATCHES
    ROW = GRID + 1
    IMG = ROW * ROW
    PADC = IM * IMG
    EDGE = ROW + 1
    ROWS = IM * ROW - 1
    with ExitStack() as ctx:
        def sb(name, shape, dt=F32):
            return ctx.enter_context(nc.sbuf_tensor(name, shape, dt))

        sems = []

        def sem(name):
            sems.append(ctx.enter_context(nc.semaphore(name)))
            return sems[-1]

        wp = sb("wp", [128, 2, 3, D])
        hd = sb("hd", [128, 2, PIX])
        wc = sb("wc", [128, KT, 2 * D])
        pwm = sb("pwm", [128, 3, D])
        wf = sb("wf", [HD, 4, 2, D])
        vec = sb("vec", [128, V_N])
        gate = sb("gate", [HD, 8])
        xc = sb("xc", [128, 2, KT, NP])
        P1 = sb("P1", [128, 3, CH * PADC + 2 * EDGE])
        PF = [sb(f"PF{k}", [HD, 2, CH * PADC + 2 * EDGE]) for k in range(3)]
        D1 = sb("D1", [128, 3, IM * ROW, GRID])
        DF = [sb(f"DF{k}", [HD, 2, IM * ROW, GRID]) for k in range(3)]
        PRODUCTS = 14
        prod = sb("prod", [HD, PRODUCTS, ROWS, GRID])
        L2 = sb("L2", [HD, 2, CH, NP])
        LS = sb("LS", [HD, 2, NP])
        G2 = sb("G2", [HD, 2, NP])
        TG = sb("TG", [HD, 2, NP])
        R2 = sb("R2", [HD, 2, NP])
        T0 = P1[0:PATCHES].rearrange("p k n -> p (k n)")[:, 0:B * D].rearrange("p (b c) -> p b c", b=B)
        rows = sb("rows", [PATCHES, 3, D])
        st = sb("st", [PATCHES, IM, 6])
        mv = sb("mv", [PATCHES, B, 2])
        ve = sb("ve", [PATCHES, B])
        rs = sb("rs", [PATCHES, B])
        nh = sb("nh", [PATCHES, B])
        psC = ctx.enter_context(nc.psum_tensor("psC", [128, 3, BANK], F32))
        psA = ctx.enter_context(nc.psum_tensor("psA", [128, 2, BANK], F32))
        psB = ctx.enter_context(nc.psum_tensor("psB", [128, 2, BANK], F32))
        psF = ctx.enter_context(nc.psum_tensor("psF", [128, BANK], F32))

        f3_bank = [psC[0:PATCHES, 0, 0:2 * D], psC[0:PATCHES, 1, 0:2 * D], psC[0:PATCHES, 2, 0:2 * D], psF[0:PATCHES, 0:2 * D]]

        s_wp = sem("a_wp"); s_small = sem("a_small"); s_wc = sem("a_wc"); s_x = [sem("a_x0"), sem("a_x1")]
        s_pad = sem("a_pad"); s_had = sem("a_had"); s_hadv = sem("a_hadv"); s_rows = sem("a_rows")
        s_conv = sem("a_conv"); s_gelu = sem("a_gelu"); s_dw1 = sem("a_dw1")
        s_loc = sem("a_loc"); s_g = sem("a_g"); s_lev = sem("a_lev"); s_gev = sem("a_gev")
        s_w2 = sem("a_w2"); s_tg = sem("a_tg"); s_h = sem("a_h")
        s_dwf = [sem(f"a_dwf{k}") for k in range(3)]
        s_prod = sem("a_prod"); s_sum = sem("a_sum")
        s_f = [sem(f"a_f{k}") for k in range(3)]
        s_r1 = sem("a_r1"); s_r2 = sem("a_r2"); s_lr = sem("a_lr"); s_t0 = sem("a_t0")
        s_mv = sem("a_mv"); s_rs = sem("a_rs"); s_t1 = sem("a_t1"); s_padp = sem("a_padp"); s_nh = sem("a_nh"); s_out = sem("a_out"); s_cls = sem("a_cls")
        s_own = sem("a_own_dve"); s_ownp = sem("a_own_pool"); s_owna = sem("a_own_act")

        def padded(p, k, c):
            v = p[:, k, EDGE + c * PADC:EDGE + (c + 1) * PADC]
            return v.rearrange("p (i r c) -> p i r c", i=IM, r=ROW)[:, :, 0:GRID, 0:GRID]

        def tap(p, k, c, t):
            off = EDGE + c * PADC + (t // 3 - 1) * ROW + t % 3 - 1
            v = p[:, k, off:off + ROWS * ROW]
            return v.rearrange("p (r c) -> p r c", c=ROW)[:, :, 0:GRID]

        def dense(d, k):
            return d[:, k].rearrange("p (i r) c -> p i (r c)", r=ROW)[:, :, 0:PATCHES]

        def dw(eng, own, src, dst, tiles, c, col, done):
            last = {}
            for t in range(9):
                for k in tiles:
                    out, w = dst[:, k, 0:ROWS, :], vec[0:src.shape[0], col + 9 * k + t:col + 9 * k + t + 1]
                    if t == 0:
                        i = eng.tensor_scalar(out, tap(src, k, c, t), w, None, ALU.mult)
                    else:
                        own.need(last[k])
                        i = eng.scalar_tensor_tensor(out, tap(src, k, c, t), w, out, ALU.mult, ALU.add)
                    last[k] = own.did(i)
            own.need(own.n)
            eng.sem_inc(done, 1)

        def tiles_before(w, k):
            return sum(0 <= w_ - k_ - 1 < CH for w_ in range(w + 1) for k_ in range(3) if (w_, k_) < (w, k))

        WAVES = CH + 3
        ctx.callback(retire, nc, sems)
        block = ctx.enter_context(nc.Block())

        @block.sync
        def _(sp):
            sp.dma_start(wp[:], w_pg.rearrange("(t p) c o -> p t c o", p=128)).then_inc(s_wp, 16)
            sp.dma_start(hd[:], had.rearrange("(t p) x -> p t x", p=128)).then_inc(s_wp, 16)
            sp.dma_start(vec[:], vecs).then_inc(s_small, 16)
            for c in range(CH):
                if c >= 2:
                    sp.wait_ge(s_conv, c - 1)
                sp.dma_start(xc[:, c % 2], xcol.rearrange("(t p) n -> p t n", p=128)[:, :, c * NP:(c + 1) * NP]
                             ).then_inc(s_x[c % 2], 16)
            sp.dma_start(H[0:1, :, :], cls_row.rearrange("(a n) c -> a n c", a=1)).then_inc(s_cls, 16)
            sp.dma_start(H[1 + PATCHES:S, :, :], txt.rearrange("b t c -> t b c")).then_inc(s_cls, 16)
            for c in range(CH):
                sp.wait_ge(s_t1, c + 1)
                sp.dma_start(H[1:1 + PATCHES, c * IM:(c + 1) * IM, :], T0[:, c * IM:(c + 1) * IM, :]).then_inc(s_out, 16)
            sp.wait_ge(s_out, 16 * CH)
            sp.wait_ge(s_cls, 32)

        @block.tensor
        def _(pe):
            pe.wait_ge(s_wp, 32)
            for ch in range(3):
                for xt in range(2):
                    n = 2 * ch + xt
                    if n >= 3:
                        pe.wait_ge(s_hadv, n - 2)
                    for bt in range(2):
                        mm = pe.matmul(psC[:, n % 3, 0:D], hd[:, bt, xt * 128:(xt + 1) * 128], wp[:, bt, ch, :],
                                       start=bt == 0, stop=bt == 1)
                    mm.then_inc(s_had, 1)
            pe.wait_ge(s_hadv, 6)
            pe.wait_ge(s_wc, 32)

            def conv(c):
                pe.wait_ge(s_x[c % 2], 16 * (c // 2 + 1))
                if c >= 1:
                    pe.wait_ge(s_gelu, c)
                for t in range(3):
                    for k in range(KT):
                        mm = pe.matmul(psC[:, t, 0:NP], wc[:, k, t * 128:(t + 1) * 128], xc[:, c % 2, k, :],
                                       start=k == 0, stop=k == KT - 1)
                mm.then_inc(s_conv, 1)

            def pair(ps, w, d):
                for m in range(2):
                    for k in range(2):
                        mm = pe.matmul(ps[0:HD, m, 0:NP], w[:, k, m * HD:(m + 1) * HD], d(k),
                                       start=k == 0, stop=k == 1)
                return mm

            conv(0)
            for w in range(WAVES):
                if w + 1 < CH:
                    conv(w + 1)
                if w < CH:
                    if w == 0:
                        pe.wait_ge(s_small, 16 * 3)
                    pe.wait_ge(s_dw1, w + 1)
                    if w > 0:
                        pe.wait_ge(s_tg, w)
                    if w > 2:
                        pe.wait_ge(s_r2, w - 2)
                    for m in range(2):
                        pe.matmul(psA[0:HD, m, 0:NP], pwm[:, 0, m * HD:(m + 1) * HD], dense(D1, 0),
                                  start=True, stop=False)
                        mm = pe.matmul(psA[0:HD, m, 0:NP], pwm[0:64, 1, m * HD:(m + 1) * HD], dense(D1, 1)[0:64],
                                       start=False, stop=True)
                    mm.then_inc(s_loc, 1)
                    if w > 1:
                        pe.wait_ge(s_r1, w - 1)
                    for m in range(2):
                        pe.matmul(psB[0:HD, m, 0:NP], pwm[:, 2, m * HD:(m + 1) * HD], dense(D1, 2),
                                  start=True, stop=False)
                        mm = pe.matmul(psB[0:HD, m, 0:NP], pwm[64:128, 1, m * HD:(m + 1) * HD], dense(D1, 1)[64:128],
                                       start=False, stop=True)
                    mm.then_inc(s_g, 1)
                    pe.wait_ge(s_lev, w + 1)
                    pe.wait_ge(s_gev, w + 1)
                    pair(psA, wf[:, 0], lambda k: G2[:, k, :]).then_inc(s_w2, 1)
                if 0 <= w - 1 < CH:
                    c = w - 1
                    pe.wait_ge(s_dwf[0], c + 1)
                    pe.wait_ge(s_sum, 8 * (tiles_before(w, 0) + 1))
                    pe.wait_ge(s_gev, min(w + 1, CH))
                    if c > 0:
                        pe.wait_ge(s_r1, c)
                    pair(psB, wf[:, 1], lambda k: dense(DF[0], k)).then_inc(s_f[0], 1)
                if 0 <= w - 2 < CH:
                    c = w - 2
                    pe.wait_ge(s_dwf[1], c + 1)
                    pe.wait_ge(s_sum, 8 * (tiles_before(w, 1) + 1))
                    pe.wait_ge(s_tg, min(w + 1, CH))
                    if c > 0:
                        pe.wait_ge(s_r2, c)
                    pair(psA, wf[:, 2], lambda k: dense(DF[1], k)).then_inc(s_f[1], 1)
                if 0 <= w - 3 < CH:
                    c = w - 3
                    pe.wait_ge(s_dwf[2], c + 1)
                    pe.wait_ge(s_sum, 8 * (tiles_before(w, 2) + 1))
                    if c == 0:
                        pe.wait_ge(s_gelu, CH)
                    for n in range(c * IM // 2, (c + 1) * IM // 2):
                        if n >= 4:
                            pe.wait_ge(s_t0, n - 3)
                        for j in range(2):
                            for k in range(2):
                                mm = pe.matmul(f3_bank[n % 4][:, j * D:(j + 1) * D], dense(DF[2], k)[:, 2 * n + j - c * IM, :],
                                               wf[:, 3, k, :], start=k == 0, stop=k == 1)
                        mm.then_inc(s_f[2], 1)

        @block.scalar
        def _(act):
            act.dma_start(wc[:, :, 0:128], w_pl.rearrange("(t p) o -> p t o", p=128)[:, :, 0:128]).then_inc(s_wc, 16)
            act.dma_start(wc[:, :, 128:192], w_pl.rearrange("(t p) o -> p t o", p=128)[:, :, 128:192]).then_inc(s_wc, 16)
            act.dma_start(pwm[:], pw_mix).then_inc(s_small, 16)
            act.dma_start(wf[:], w96).then_inc(s_small, 16)
            for k, row in enumerate((pwb_row, lng_row, lnb_row)):
                act.dma_start(rows[:, k, :], row.rearrange("(a c) -> a c", a=1).broadcast_to([PATCHES, D])).then_inc(s_rows, 16)
            act.wait_ge(s_small, 48)
            own = Own(act, s_owna)
            n = own.did(act.activation(gate[:, 0:2], vec[0:HD, V_ALPHA:V_ALPHA + 2], ACT.Tanh))
            own.need(n)
            own.did(act.activation(gate[:, 2:4], gate[:, 0:2], ACT.Copy, bias=0.5, scale=-0.5))
            n = own.did(act.activation(gate[:, 0:2], gate[:, 0:2], ACT.Copy, bias=0.5, scale=0.5))
            own.need(n)
            for k in range(2):
                own.did(act.activation(gate[:, 4 + k:5 + k], vec[0:HD, V_PG_B2 + k:V_PG_B2 + k + 1], ACT.Copy,
                                       scale=gate[:, k:k + 1]))
                n = own.did(act.activation(gate[:, 6 + k:7 + k], vec[0:HD, V_PL_PWB + k:V_PL_PWB + k + 1], ACT.Copy,
                                           scale=gate[:, 2 + k:3 + k]))
            own.need(n)

            def gelu(c):
                act.wait_ge(s_conv, c + 1)
                if c == 0:
                    act.wait_ge(s_pad, 1)
                    act.wait_ge(s_padp, 1)
                for t in range(3):
                    i = act.activation(padded(P1, t, c), psC[:, t, 0:NP].rearrange("p (i r c) -> p i r c", i=IM, r=GRID),
                                       ACT.Gelu, bias=vec[:, V_CONV_B + t:V_CONV_B + t + 1])
                i.then_inc(s_gelu, 1)

            def weigh(k, w):
                c, n = w - k - 1, tiles_before(w, k)
                for t in range(9):
                    q = 9 * n + t
                    if q >= PRODUCTS:
                        n_, t_ = divmod(q - PRODUCTS, 9)
                        act.wait_ge(s_sum, 8 * n_ + max(t_, 1))
                    col = V_F_DW + 18 * k + 9 + t
                    act.activation(prod[:, q % PRODUCTS], tap(PF[k], 1, c, t), ACT.Copy, scale=vec[0:HD, col:col + 1]).then_inc(s_prod, 1)

            gelu(0)
            for w in range(WAVES):
                if w + 1 < CH:
                    gelu(w + 1)
                if 0 <= w - 1 < CH:
                    act.wait_ge(s_h, w)
                    weigh(0, w)
                if 0 <= w - 2 < CH:
                    act.wait_ge(s_r1, w - 1)
                    weigh(1, w)
                if 0 <= w - 3 < CH:
                    act.wait_ge(s_lr, w - 2)
                    weigh(2, w)
                if w < CH:
                    act.wait_ge(s_loc, w + 1)
                    if w > 0:
                        act.wait_ge(s_h, w)
                        act.wait_ge(s_w2, w)
                    for k in range(2):
                        act.activation(L2[:, k, w, :], psA[0:HD, k, 0:NP], ACT.Identity,
                                       bias=vec[0:HD, V_PL_PWB + k:V_PL_PWB + k + 1])
                        i = act.activation(LS[:, k, :], psA[0:HD, k, 0:NP], ACT.Identity,
                                           bias=gate[:, 6 + k:7 + k], scale=gate[:, 2 + k:3 + k])
                    i.then_inc(s_lev, 1)
                    act.wait_ge(s_g, w + 1)
                    for k in range(2):
                        i = act.activation(G2[:, k, :], psB[0:HD, k, 0:NP], ACT.Gelu,
                                           bias=vec[0:HD, V_PG_PWB + k:V_PG_PWB + k + 1])
                    i.then_inc(s_gev, 1)
                    act.wait_ge(s_w2, w + 1)
                    for k in range(2):
                        i = act.activation(TG[:, k, :], psA[0:HD, k, 0:NP], ACT.Identity,
                                           bias=gate[:, 4 + k:5 + k], scale=gate[:, k:k + 1])
                    i.then_inc(s_tg, 1)
                if 0 <= w - 1 < CH:
                    c = w - 1
                    act.wait_ge(s_f[0], c + 1)
                    for k in range(2):
                        i = act.activation(padded(PF[1], k, c),
                                           psB[0:HD, k, 0:NP].rearrange("p (i r c) -> p i r c", i=IM, r=GRID),
                                           ACT.Relu, bias=vec[0:HD, V_F1_B + k:V_F1_B + k + 1])
                    i.then_inc(s_r1, 1)
                if 0 <= w - 2 < CH:
                    c = w - 2
                    act.wait_ge(s_f[1], c + 1)
                    if c > 0:
                        act.wait_ge(s_lr, c)
                    for k in range(2):
                        i = act.activation(R2[:, k, :], psA[0:HD, k, 0:NP], ACT.Relu,
                                           bias=vec[0:HD, V_F2_B + k:V_F2_B + k + 1])
                    i.then_inc(s_r2, 1)

        @block.vector
        def _(v):
            own = Own(v, s_own)
            v.memset(P1[:], 0.0).then_inc(s_pad, 1)
            for n in range(6):
                v.wait_ge(s_had, n + 1)
                v.tensor_copy(wc[:, n, 256:384], psC[:, n % 3, 0:128])
                v.tensor_copy(wc[:, n, 192:256], psC[:, n % 3, 128:192]).then_inc(s_hadv, 1)
            v.wait_ge(s_small, 48)
            v.wait_ge(s_rows, 48)

            def take_rows(c):
                for n in range(c * IM // 2, (c + 1) * IM // 2):
                    v.wait_ge(s_f[2], n + 1)
                    v.tensor_tensor(T0[:, 2 * n:2 * n + 2, :], f3_bank[n % 4].rearrange("p (j c) -> p j c", j=2),
                                    rows[:, 0:1, :].broadcast_to([PATCHES, 2, D]), ALU.add).then_inc(s_t0, 1)
                v.wait_ge(s_t0, (c + 1) * IM // 2)
                for b in range(c * IM, (c + 1) * IM):
                    i = own.did(v.bn_stats(st[:, b % IM, :], T0[:, b, :]))
                own.need(i)
                for b in range(c * IM, (c + 1) * IM):
                    v.bn_aggr(mv[:, b, :], st[:, b % IM, :]).then_inc(s_mv, 1)

            def norm_rows(c):
                v.wait_ge(s_rs, c + 1)
                for b in range(c * IM, (c + 1) * IM):
                    i = own.did(v.tensor_scalar(T0[:, b, :], T0[:, b, :], mv[:, b, 0:1], rs[:, b:b + 1], ALU.subtract, ALU.mult))
                own.need(i)
                t = T0[:, c * IM:(c + 1) * IM, :]
                i = own.did(v.tensor_tensor(t, t, rows[:, 1:2, :].broadcast_to([PATCHES, IM, D]), ALU.mult))
                own.need(i)
                v.tensor_tensor(t, t, rows[:, 2:3, :].broadcast_to([PATCHES, IM, D]), ALU.add).then_inc(s_t1, 1)

            v.memset(nh[:], -0.5).then_inc(s_nh, 1)
            for w in range(WAVES):
                if w < CH:
                    v.wait_ge(s_gelu, w + 1)
                    if w > 0:
                        v.wait_ge(s_g, w)
                    dw(v, own, P1, D1, range(3), w, V_DW, s_dw1)
                if 0 <= w - 1 < CH:
                    v.wait_ge(s_h, w)
                    if w > 1:
                        v.wait_ge(s_f[0], w - 1)
                    dw(v, own, PF[0], DF[0], (0,), w - 1, V_F_DW, s_dwf[0])
                if 0 <= w - 4:
                    take_rows(w - 4)
                if 0 <= w - 2 < CH:
                    v.wait_ge(s_r1, w - 1)
                    if w > 2:
                        v.wait_ge(s_f[1], w - 2)
                    dw(v, own, PF[1], DF[1], (0,), w - 2, V_F_DW + 18, s_dwf[1])
                if 0 <= w - 3 < CH:
                    c = w - 3
                    v.wait_ge(s_lr, c + 1)
                    if c > 0:
                        v.wait_ge(s_f[2], c * IM // 2)
                    dw(v, own, PF[2], DF[2], (0,), c, V_F_DW + 36, s_dwf[2])
                if 0 <= w - 5:
                    norm_rows(w - 5)
            take_rows(CH - 1)
            norm_rows(CH - 2)
            norm_rows(CH - 1)

        @block.gpsimd
        def _(g):
            own = Own(g, s_ownp)

            def roots(c):
                g.wait_ge(s_mv, (c + 1) * IM)
                a = slice(c * IM, (c + 1) * IM)
                n = own.did(g.tensor_scalar(ve[:, a], mv[:, a, 1], 1e-5, None, ALU.add))
                own.need(n)
                g.tensor_tensor(rs[:, a], ve[:, a], nh[:, a], ALU.pow).then_inc(s_rs, 1)

            def add_up(k, w):
                n = tiles_before(w, k)
                out = DF[k][:, 1, 0:ROWS, :]
                for t in range(1, 9):
                    if t > 1:
                        g.wait_ge(s_sum, 8 * n + t - 1)
                    g.wait_ge(s_prod, 9 * n + t + 1)
                    a = prod[:, 9 * n % PRODUCTS] if t == 1 else out
                    g.tensor_tensor(out, a, prod[:, (9 * n + t) % PRODUCTS], ALU.add).then_inc(s_sum, 1)

            for p in PF:
                i = g.memset(p[:], 0.0)
            i.then_inc(s_padp, 1)
            g.wait_ge(s_padp, 1)
            g.wait_ge(s_small, 48)
            g.wait_ge(s_nh, 1)
            for w in range(WAVES):
                for k in range(3):
                    if 0 <= w - k - 1 < CH:
                        if w - k - 1 > 0:
                            g.wait_ge(s_f[k], (w - k - 1) * (IM // 2 if k == 2 else 1))
                        add_up(k, w)
                if 0 <= w - 4:
                    roots(w - 4)
                if w < CH:
                    g.wait_ge(s_tg, w + 1)
                    for k in range(2):
                        i = g.tensor_tensor(padded(PF[0], k, w), LS[:, k, :].rearrange("p (i r c) -> p i r c", i=IM, r=GRID),
                                            TG[:, k, :].rearrange("p (i r c) -> p i r c", i=IM, r=GRID), ALU.add)
                    i.then_inc(s_h, 1)
                if 0 <= w - 2 < CH:
                    c = w - 2
                    g.wait_ge(s_r2, c + 1)
                    for k in range(2):
                        i = g.tensor_tensor(padded(PF[2], k, c), L2[:, k, c, :].rearrange("p (i r c) -> p i r c", i=IM, r=GRID),
                                            R2[:, k, :].rearrange("p (i r c) -> p i r c", i=IM, r=GRID), ALU.add)
                    i.then_inc(s_lr, 1)
            roots(CH - 1)


G = 4
N = G * S
ROUNDS = B // G
INNER = 384
NI = INNER // 128
STATE = 16
FFN = 512
NF = FFN // 128


def row_stats(nc, tag, H, eps2, r1, r12, mv, nh, loads, fills):
    with ExitStack() as ctx:
        def sem(name):
            return ctx.enter_context(nc.semaphore(name))

        st = ctx.enter_context(nc.sbuf_tensor(f"{tag}_st_stats", [S, B, 6], F32))
        s_st = sem(f"{tag}_st_bn"); s_mv = sem(f"{tag}_st_mv"); s_p = sem(f"{tag}_st_pool"); s_nh = sem(f"{tag}_st_nh")
        block = ctx.enter_context(nc.Block())

        @block.sync
        def _(sp):
            loads(sp)

        @block.vector
        def _(v):
            v.memset(nh[:], -0.5).then_inc(s_nh, 1)
            for b in range(B):
                v.bn_stats(st[:, b, :], H[:, b, :]).then_inc(s_st, 1)
            v.wait_ge(s_st, B)
            for b in range(B):
                v.bn_aggr(mv[:, b, :], st[:, b, :]).then_inc(s_mv, 1)
            v.wait_ge(s_mv, B)

        @block.gpsimd
        def _(g):
            own = Own(g, s_p)
            fills(g)
            g.wait_ge(s_mv, B)
            n = own.did(g.tensor_scalar(r1[:], mv[:, :, 1], 1e-5, None, ALU.add))
            n = own.did(g.tensor_scalar(r12[:], mv[:, :, 1], 1.0 + eps2, 1e-5 * eps2, ALU.mult, ALU.add))
            own.need(n)
            g.wait_ge(s_nh, 1)
            a = slice(0, 2 * G)
            n = own.did(g.tensor_tensor(r12[:, a], r12[:, a], nh[:, a], ALU.pow))
            own.need(n)


def late_roots(g, r1, r12, nh, done):
    a = slice(2 * G, B)
    g.tensor_tensor(r12[:, a], r12[:, a], nh[:, a], ALU.pow)
    g.tensor_tensor(r1[:], r1[:], nh[:], ALU.pow).then_inc(done, 1)


def at_least(eng, sem, value):
    if not isinstance(value, int) or value > 0:
        eng.wait_ge(sem, value)


def mamba(nc, H, w_zg, w_x, w_dt, a_log, w_o, w_ug, w_dn, vecs, onehot, eye):
    K_PRE, K_POST = 14, 13
    with ExitStack() as ctx:
        def sb(name, shape, dt=F32):
            return ctx.enter_context(nc.sbuf_tensor(name, shape, dt))

        def sem(name):
            return ctx.enter_context(nc.semaphore(name))

        mv = sb("b_mv", [S, B, 2]); r1 = sb("b_r1", [S, B]); r12 = sb("b_r12", [S, B])
        wzg = sb("wzg", [HD, 2, 2, INNER]); wx = sb("wx", [128, NI, 192]); wdt = sb("wdt", [HD, INNER])
        wo = sb("wo", [128, NI, D]); wug = sb("wug", [HD, 2, 2, FFN]); wdn = sb("wdn", [128, NF, D])
        A = sb("A", [128, NI, STATE]); vec = sb("b_vec", [128, V_N])
        oh = sb("oh", [HD, 2 * STATE]); sel = sb("sel", [HD, 2 * STATE, 128], BF16); ident = sb("b_id", [128, 128])
        nh = sb("b_nh", [S, B])
        RING = 4
        abar = sb("abar", [128, RING, NI, G, S])
        s_w = sem("b_w"); s_cst = sem("b_cst")

        def loads(sp):
            for dst, src in ((wzg, w_zg), (wx, w_x), (wdt, w_dt), (A, a_log), (wo, w_o), (wug, w_ug), (wdn, w_dn),
                             (vec, vecs), (oh, onehot), (ident, eye)):
                sp.dma_start(dst[:], src).then_inc(s_w, 16)

        def fills(g):
            g.memset(abar[:], 0.0).then_inc(s_cst, 1)

        row_stats(nc, "b", H, 1e-6, r1, r12, mv, nh, loads, fills)
        xl = sb("xl", [S, 2, G, D]); hn = sb("hn", [S, G, D]); hT = sb("hT", [HD, 2, N])
        sg = sb("sg", [128, NI, N]); z = sb("z", [128, 2, NI * N]); dtin = sb("dtin", [HD, N])
        P3 = sb("P3", [HD, 2, N], BF16); Pm = sb("Pm", [HD, N], BF16); R = sb("R", [HD, N])
        xd = sb("xd", [128, NI, N]); ax = sb("ax", [128, NI, N]); u = sb("u", [128, NI, N]); lnw = sb("lnw", [128, NI, N])
        dt = sb("dt", [128, 2, NI, N]); dtz = sb("dtz", [128, 2, NI, N])
        LONG = 8
        AHEAD = 3
        Bb = sb("Bb", [128, RING, N]); Cb = sb("Cb", [128, RING, N]); Bx = sb("Bx", [128, RING, NI, N])
        hs = sb("hs", [128, LONG, NI, N])
        y = sb("y", [128, NI * N]); x1 = sb("x1", [S, G, D]); hf = sb("hf", [S, G, D]); hfT = sb("hfT", [HD, 2, N])
        th = sb("th", [128, 2, N]); av = sb("av", [128, NF, N])
        st = sb("b_st", [S, G, 6]); mg = sb("b_mg", [S, G, 2]); ms = sb("b_ms", [S, G]); rr = sb("b_rr", [S, G])
        ps = ctx.enter_context(nc.psum_tensor("b_ps", [128, 8, BANK], F32))
        GATE_AT, USE_AT = (8, 9, 10, 11), (9, 10, 11, 12)
        PAIRS = STATE // 2
        SIDE, BANK_B, BANK_C, BANK_Y = 4, 4, 5, 6
        HALF = NI * N // 2

        s_A = sem("b_A"); s_A2 = sem("b_A2")
        s_hn = sem("b_hn"); s_tr = sem("b_tr"); s_hT = sem("b_hT"); s_gt = sem("b_gt"); s_zi = sem("b_zi")
        s_sg = sem("b_sg"); s_z = sem("b_z"); s_xp = sem("b_xp"); s_dtin = sem("b_dtin"); s_hi = sem("b_hi")
        s_P3 = sem("b_P3"); s_dtp = sem("b_dtp"); s_xd = sem("b_xd"); s_ax = sem("b_ax"); s_u = sem("b_u"); s_ln = sem("b_ln")
        s_dt = sem("b_dt"); s_dtz = sem("b_dtz"); s_pb = sem("b_pb"); s_pc = sem("b_pc"); s_cb = sem("b_cb"); s_ab = sem("b_ab"); s_bb = sem("b_bb")
        s_bx = sem("b_bx"); s_scan = sem("b_scan"); s_hc = sem("b_hc"); s_ys = sem("b_ys"); s_y = sem("b_y")
        s_o = sem("b_o"); s_x1 = sem("b_x1"); s_st = sem("b_stat"); s_rr = sem("b_rr2"); s_hf = sem("b_hf"); s_tr2 = sem("b_tr2")
        s_hfT = sem("b_hfT"); s_g = sem("b_g"); s_up = sem("b_up"); s_th = sem("b_th"); s_av = sem("b_av"); s_dn = sem("b_dn")
        s_H = sem("b_H"); s_pre = sem("b_own_pre"); s_post = sem("b_own_post"); s_add = sem("b_add"); s_pair = sem("b_pair"); s_step = sem("b_step"); s_r1 = sem("b_r1s")
        block = ctx.enter_context(nc.Block())

        def f2(t):
            return t.rearrange("p a b -> p (a b)")

        NONE = (None, 2, None, 0, 0)
        SIDE_TILES = [("RT0", 1, s_hT, 2, 1), ("RT1", 1, s_hT, 2, 2), ("RG1", 1, s_sg, 3, 2), ("RI1", 1, s_z, 3, 2),
                  ("RG0", 1, s_sg, 3, 1), ("RI0", 1, s_z, 3, 1), ("RG2", 1, s_sg, 3, 3), ("RI2", 1, s_z, 3, 3),
                  ("O0", 0, s_x1, 2, 1), ("O1", 0, s_x1, 2, 2), ("X0", 1, s_dtin, 1, 1), ("X1", 1, s_P3, 1, 1),
                  ("PT0", 0, s_hfT, 2, 1), ("PT1", 0, s_hfT, 2, 2), ("D0", 1, s_xd, 3, 1), NONE,
                  ("G0", 0, s_av, 4, 1), ("U0", 0, s_av, 4, 1), ("D1", 1, s_xd, 3, 2), NONE,
                  ("G2", 0, s_av, 4, 3), ("U2", 0, s_av, 4, 3), ("D2", 1, s_xd, 3, 3), NONE,
                  ("N0", 0, s_H, 2, 1), ("N1", 0, s_H, 2, 2), ("G1", 0, s_av, 4, 2), ("U1", 0, s_av, 4, 2),
                  NONE, NONE, ("G3", 0, s_av, 4, 4), ("U3", 0, s_av, 4, 4)]
        PLACE = {t[0]: n for n, t in enumerate(SIDE_TILES)}

        def bank(name):
            return PLACE[name] % SIDE

        def program(engine, scan_first, step, pre, post, finish=lambda last: None):
            for s in range(STATE):
                pre(0, 0, s, None)
            scan_first()
            for s in range(STATE):
                step(0, 0, s, False)
                pre(1, 1, s, None)
            with engine.Fori(0, (ROUNDS - 2) // 2) as t:
                for par in (1, 0):
                    i = t * 2 + (2 - par)
                    for s in range(STATE):
                        step(i, par, s, False)
                        post(i - 1, 1 - par, s, i + 1)
                        pre(i + 1, 1 - par, s, i - 1)
            last = ROUNDS - 1
            for s in range(STATE):
                step(last, 1, s, True)
                post(last - 1, 0, s, None)
            finish(last)
            for s in range(STATE):
                post(last, 1, s, None)

        @block.tensor
        def _(pe):
            pe.wait_ge(s_w, 160)
            pe.wait_ge(s_cst, 2)

            def free(name, mine, other):
                n = PLACE[name]
                side = SIDE_TILES[n][1]
                for k in range(n - SIDE, -1, -SIDE):
                    _, kind, s_free, per, at = SIDE_TILES[k]
                    index = mine if kind == side else other
                    if kind < 2 and index is not None:
                        pe.wait_ge(s_free, index * per + at)
                        return

            def turn(src, names, done, mine, other):
                for k in range(2):
                    free(names[k], mine, other)
                    for q in range(G):
                        mm = pe.transpose(ps[0:HD, bank(names[k]), q * S:(q + 1) * S], src[:, q, k * HD:(k + 1) * HD],
                                          ident[0:S, 0:S])
                    mm.then_inc(done, 1)

            def pre(j, par, s, other):
                if s == 1:
                    pe.wait_ge(s_hn, j + 1)
                    turn(hn, ("RT0", "RT1"), s_tr, j, other)
                if s in (2, 3, 5):
                    m = (2, 3, 5).index(s)
                    if m == 0:
                        pe.wait_ge(s_hT, j * 2 + 2)
                    for w_, name, done in ((1, f"RG{m}", s_gt), (0, f"RI{m}", s_zi)):
                        free(name, j, other)
                        for k in range(2):
                            mm = pe.matmul(ps[:, bank(name), 0:N], wzg[:, k, w_, m * 128:(m + 1) * 128], hT[:, k, :],
                                           start=k == 0, stop=k == 1)
                        mm.then_inc(done, 1)
                if s == 7:
                    pe.wait_ge(s_z, j * 3 + 3)
                    for n in range(2):
                        free(f"X{n}", j, other)
                        for k in range(NI):
                            mm = pe.matmul(ps[0:HD, bank(f"X{n}"), 0:N], wx[:, k, n * 96:(n + 1) * 96], z[:, par, k * N:(k + 1) * N],
                                           start=k == 0, stop=k == NI - 1)
                        mm.then_inc(s_xp, 1)
                if s == 8:
                    pe.wait_ge(s_dtin, j + 1)
                    for m in range(NI):
                        free(f"D{m}", j, other)
                        pe.matmul(ps[:, bank(f"D{m}"), 0:N], wdt[:, m * 128:(m + 1) * 128], dtin[:], start=True, stop=True).then_inc(s_dtp, 1)

            def post(p, par, s, other):
                if s == 4:
                    pe.wait_ge(s_y, p + 1)
                    for h in range(2):
                        free(f"O{h}", p, other)
                        for q in range(2):
                            c = (2 * h + q) * S
                            for k in range(NI):
                                mm = pe.matmul(ps[0:S, bank(f"O{h}"), q * D:(q + 1) * D], y[:, k * N + c:k * N + c + S], wo[:, k, :],
                                               start=k == 0, stop=k == NI - 1)
                        mm.then_inc(s_o, 1)
                if s == 7:
                    pe.wait_ge(s_hf, p + 1)
                    turn(hf, ("PT0", "PT1"), s_tr2, p, other)
                if s in GATE_AT:
                    m = GATE_AT.index(s)
                    if m == 0:
                        pe.wait_ge(s_hfT, p * 2 + 2)
                    for w_, name, done in ((0, f"G{m}", s_g), (1, f"U{m}", s_up)):
                        free(name, p, other)
                        for k in range(2):
                            mm = pe.matmul(ps[:, bank(name), 0:N], wug[:, k, w_, m * 128:(m + 1) * 128], hfT[:, k, :],
                                           start=k == 0, stop=k == 1)
                        mm.then_inc(done, 1)
                if s == 13:
                    pe.wait_ge(s_av, p * 4 + 4)
                    for h in range(2):
                        free(f"N{h}", p, other)
                        for q in range(2):
                            c = (2 * h + q) * S
                            for k in range(NF):
                                mm = pe.matmul(ps[0:S, bank(f"N{h}"), q * D:(q + 1) * D], av[:, k, c:c + S], wdn[:, k, :],
                                               start=k == 0, stop=k == NF - 1)
                        mm.then_inc(s_dn, 1)

            def spread_b(i, par, t):
                at_least(pe, s_bb, i * STATE + t)
                if t % STATE == 0:
                    pe.wait_ge(s_P3, i + t // STATE + 1)
                pe.matmul(ps[:, BANK_B, 0:N], sel[:, t % STATE, :], P3[:, (par + t // STATE) % 2, :], start=True, stop=True).then_inc(s_pb, 1)

            def spread_c(i, par, t):
                at_least(pe, s_cb, i * STATE + t)
                pe.matmul(ps[:, BANK_C, 0:N], sel[:, STATE + t % STATE, :], P3[:, (par + t // STATE) % 2, :],
                          start=True, stop=True).then_inc(s_pc, 1)

            def first():
                for t in range(AHEAD):
                    spread_b(0, 0, t)
                    spread_c(0, 0, t)

            def add_y(i, k):
                pe.wait_ge(s_pair, i * PAIRS + (k + 1))
                if k == 0:
                    at_least(pe, s_y, i)
                for h in range(2):
                    mm = pe.matmul(ps[:, BANK_Y + h, 0:HALF], ident[:], f2(hs[:, 2 * k % LONG])[:, h * HALF:(h + 1) * HALF],
                                   start=k == 0, stop=k == PAIRS - 1)
                mm.then_inc(s_ys, 1)

            def step(i, par, s, last):
                if not last or s + AHEAD < STATE:
                    spread_b(i, par, s + AHEAD)
                    spread_c(i, par, s + AHEAD)
                if s % 2 == 0 and s >= 4:
                    add_y(i, (s - 4) // 2)
                elif s in (0, 2) and (not isinstance(i, int) or i > 0):
                    add_y(i - 1, PAIRS - 2 + s // 2)

            def finish(last):
                add_y(last, PAIRS - 2)
                add_y(last, PAIRS - 1)

            program(pe, first, step, pre, post, finish)

        @block.scalar
        def _(act):
            act.wait_ge(s_A2, 1)
            act.activation(f2(A[:]), f2(A[:]), ACT.Exp).then_inc(s_A, 1)
            act.wait_ge(s_A, 1)
            act.activation(f2(A[:]), f2(A[:]), ACT.Copy, scale=-1.0).then_inc(s_A, 1)
            act.wait_ge(s_A, 2)
            act.wait_ge(s_cst, 2)

            def pre(j, par, s, other):
                if s == 1:
                    for k in range(2):
                        act.wait_ge(s_tr, j * 2 + (k + 1))
                        act.activation(hT[:, k, :], ps[0:HD, bank(f"RT{k}"), 0:N], ACT.Identity, bias=0.0,
                                       scale=vec[0:HD, V_NORM1 + k:V_NORM1 + k + 1]).then_inc(s_hT, 1)
                if s in (2, 3, 5):
                    m = (2, 3, 5).index(s)
                    act.wait_ge(s_gt, j * 3 + (m + 1))
                    act.activation(sg[:, m, :], ps[:, bank(f"RG{m}"), 0:N], ACT.Tanh, scale=0.5).then_inc(s_sg, 1)
                if s == 7:
                    act.wait_ge(s_xp, j * 2 + 1)
                    act.activation(dtin[:], ps[0:HD, bank("X0"), 0:N], ACT.Copy).then_inc(s_dtin, 1)
                    act.wait_ge(s_xp, j * 2 + 2)
                    act.activation(P3[:, par, :], ps[0:HD, bank("X1"), 0:N], ACT.Copy).then_inc(s_hi, 1)
                if s == 8:
                    for m in range(NI):
                        act.wait_ge(s_dtp, j * 3 + (m + 1))
                        act.activation(xd[:, m, :], ps[:, bank(f"D{m}"), 0:N], ACT.Identity,
                                       bias=vec[:, V_B_DT + m:V_B_DT + m + 1]).then_inc(s_xd, 1)
                    act.wait_ge(s_xd, j * 3 + 3)
                    act.activation(f2(ax[:]), f2(xd[:]), ACT.Abs).then_inc(s_ax, 1)
                    act.wait_ge(s_ax, j + 1)
                    act.activation(f2(u[:]), f2(ax[:]), ACT.Exp, scale=-1.0).then_inc(s_u, 1)
                if s == 9:
                    act.wait_ge(s_u, j + 1)
                    act.activation(f2(lnw[:]), f2(u[:]), ACT.Ln, bias=1.0).then_inc(s_ln, 1)

            def post(p, par, s, other):
                if s == 7:
                    for k in range(2):
                        act.wait_ge(s_tr2, p * 2 + (k + 1))
                        act.activation(hfT[:, k, :], ps[0:HD, bank(f"PT{k}"), 0:N], ACT.Identity, bias=0.0,
                                       scale=vec[0:HD, V_FFN_NORM + k:V_FFN_NORM + k + 1]).then_inc(s_hfT, 1)
                if s in GATE_AT:
                    m = GATE_AT.index(s)
                    act.wait_ge(s_g, p * 4 + (m + 1))
                    act.activation(th[:, m % 2, :], ps[:, bank(f"G{m}"), 0:N], ACT.Tanh, scale=0.5).then_inc(s_th, 1)

            def decays(i, par, t):
                at_least(act, s_bx, i * STATE + t - (RING - 1))
                act.wait_ge(s_pb, i * STATE + (t + 1))
                act.activation(Bb[:, t % RING, :], ps[:, BANK_B, 0:N], ACT.Copy).then_inc(s_bb, 1)
                at_least(act, s_scan, i * STATE + t - (RING - 1))
                if t % STATE == 0:
                    act.wait_ge(s_dt, i + t // STATE + 1)
                for m in range(NI):
                    a = act.activation(abar[:, t % RING, m, :, 1:S],
                                       dt[:, (par + t // STATE) % 2, m, :].rearrange("p (g t) -> p g t", g=G)[:, :, 1:S],
                                       ACT.Exp, scale=A[:, m, t % STATE:t % STATE + 1])
                a.then_inc(s_ab, 1)
                at_least(act, s_hc, i * STATE + t - (RING - 1))
                act.wait_ge(s_pc, i * STATE + (t + 1))
                act.activation(Cb[:, t % RING, :], ps[:, BANK_C, 0:N], ACT.Copy).then_inc(s_cb, 1)

            def first():
                decays(0, 0, 0)
                decays(0, 0, 1)
                decays(0, 0, 2)

            def step(i, par, s, last):
                if not last or s + AHEAD < STATE:
                    decays(i, par, s + AHEAD)

            program(act, first, step, pre, post)

        @block.vector
        def _(v):
            v.wait_ge(s_w, 160)
            v.tensor_copy(sel[:], oh[:].rearrange("p (s a) -> p s a", a=1).broadcast_to([HD, 2 * STATE, 128])).then_inc(s_cst, 1)
            v.tensor_scalar(f2(A[:]), f2(A[:]), 80.0, None, ALU.min).then_inc(s_A2, 1)
            own_pre, own_post = Own(v, s_pre), Own(v, s_post)

            def rows_of(j, q):
                b = bass.ds(j * G + q, 1)
                return H[:, b, :].rearrange("p a c -> p (a c)"), mv[:, b, 0:1].rearrange("p a c -> p (a c)"), b

            def pre(j, par, s, other):
                own = own_pre
                if s == 0:
                    own.n, own.base = 0, j * K_PRE
                    for q in range(G):
                        h_, m_, b = rows_of(j, q)
                        n = v.tensor_scalar(hn[:, q, :], h_, m_, r12[:, b], ALU.subtract, ALU.mult)
                    n.then_inc(s_hn, 1)
                if s == 7:
                    if isinstance(j, int) and j == 0:
                        v.wait_ge(s_r1, 1)
                    for q in range(G):
                        h_, m_, b = rows_of(j, q)
                        own.did(v.tensor_scalar(xl[:, par, q, :], h_, m_, r1[:, b], ALU.subtract, ALU.mult))
                if s in (3, 4, 6):
                    m = (3, 4, 6).index(s)
                    v.wait_ge(s_sg, j * 3 + (m + 1))
                    n = own.did(v.tensor_scalar(sg[:, m, :], sg[:, m, :], 0.5, 0.5, ALU.mult, ALU.add))
                    own.need(n)
                    v.wait_ge(s_zi, j * 3 + (m + 1))
                    v.tensor_tensor(z[:, par, m * N:(m + 1) * N], sg[:, m, :], ps[:, bank(f"RI{m}"), 0:N], ALU.mult).then_inc(s_z, 1)
                if s == 8:
                    x_ = ps[:, bank("X1"), 0:N]
                    v.wait_ge(s_hi, j + 1)
                    own.did(v.tensor_tensor(R[32:64, :], x_[32:64], P3[32:64, par, :], ALU.subtract))
                    n = own.did(v.tensor_tensor(R[64:96, :], x_[64:96], P3[64:96, par, :], ALU.subtract))
                    own.need(n)
                    own.did(v.tensor_copy(P3[32:64, par, :], R[32:64, :]))
                    n = own.did(v.tensor_copy(Pm[64:96, :], R[64:96, :]))
                    own.need(n)
                    v.tensor_tensor(P3[64:96, par, :], R[64:96, :], Pm[64:96, :], ALU.subtract).then_inc(s_P3, 1)
                if s == 9:
                    v.wait_ge(s_u, j + 1)
                    n = own.did(v.tensor_scalar(f2(ax[:]), f2(u[:]), 1.0, None, ALU.add))
                    own.need(n)
                    own.did(v.scalar_tensor_tensor(f2(ax[:]), f2(ax[:]), -1.0, f2(u[:]), ALU.add, ALU.subtract, reverse1=True))
                if s == 10:
                    own.need(own.n)
                    v.wait_ge(s_ln, j + 1)
                    n = own.did(v.tensor_tensor(f2(ax[:]), f2(ax[:]), f2(lnw[:]), ALU.add))
                    own.need(n)
                    v.scalar_tensor_tensor(f2(dt[:, par]), f2(xd[:]), 0.0, f2(ax[:]), ALU.max, ALU.add).then_inc(s_dt, 1)
                if s == STATE - 1:
                    assert own.n == K_PRE, own.n

            def post(p, par, s, other):
                own = own_post
                if s == 3:
                    own.n, own.base = 0, p * K_POST
                    v.wait_ge(s_ys, p * PAIRS + PAIRS)
                    for h, m, a, b in ((0, 0, 0, N), (0, 1, N, HALF), (1, 1, HALF, 2 * N), (1, 2, 2 * N, 3 * N)):
                        n = v.scalar_tensor_tensor(y[:, a:b], z[:, par, a:b], vec[:, V_DSKIP + m:V_DSKIP + m + 1],
                                                   ps[:, BANK_Y + h, a - h * HALF:b - h * HALF], ALU.mult, ALU.add)
                    n.then_inc(s_y, 1)
                if s == 5:
                    for h in range(2):
                        v.wait_ge(s_o, p * 2 + (h + 1))
                        v.tensor_tensor(x1[:, 2 * h:2 * h + 2, :], xl[:, par, 2 * h:2 * h + 2, :],
                                        ps[0:S, bank(f"O{h}"), 0:2 * D].rearrange("p (j c) -> p j c", j=2), ALU.add).then_inc(s_x1, 1)
                    v.wait_ge(s_x1, p * 2 + 2)
                    for q in range(G):
                        n = own.did(v.bn_stats(st[:, q, :], x1[:, q, :]))
                    own.need(n)
                    v.sem_inc(s_step, 1)
                    for q in range(G):
                        n = own.did(v.bn_aggr(mg[:, q, :], st[:, q, :]))
                    own.need(n)
                    n = own.did(v.tensor_tensor(ms[:], mg[:, :, 0], mg[:, :, 0], ALU.mult))
                    own.need(n)
                    v.scalar_tensor_tensor(ms[:], ms[:], 1e-6, mg[:, :, 1], ALU.add, ALU.add).then_inc(s_st, 1)
                if s == 6:
                    v.wait_ge(s_rr, p + 1)
                    for q in range(G):
                        n = v.tensor_scalar(hf[:, q, :], x1[:, q, :], rr[:, q:q + 1], None, ALU.mult)
                    n.then_inc(s_hf, 1)
                if s in USE_AT:
                    m = USE_AT.index(s)
                    v.wait_ge(s_th, p * 4 + (m + 1))
                    n = own.did(v.scalar_tensor_tensor(th[:, m % 2, :], th[:, m % 2, :], 1.0, ps[:, bank(f"G{m}"), 0:N], ALU.add, ALU.mult))
                    own.need(n)
                    v.wait_ge(s_up, p * 4 + (m + 1))
                    v.scalar_tensor_tensor(av[:, m, :], th[:, m % 2, :], 0.5, ps[:, bank(f"U{m}"), 0:N], ALU.mult, ALU.mult).then_inc(s_av, 1)
                if s == 15:
                    v.wait_ge(s_add, p + 1)
                    for h in range(2):
                        v.wait_ge(s_dn, p * 2 + (h + 1))
                        v.tensor_tensor(H[:, bass.ds(p * G + 2 * h, 2), :], x1[:, 2 * h:2 * h + 2, :],
                                        ps[0:S, bank(f"N{h}"), 0:2 * D].rearrange("p (j c) -> p j c", j=2), ALU.add).then_inc(s_H, 1)
                if s == STATE - 1:
                    assert own.n == K_POST, own.n

            def scan(i, t):
                v.wait_ge(s_ab, i * STATE + (t + 1))
                v.wait_ge(s_bx, i * STATE + (t + 1))
                if t % 2 == 0:
                    at_least(v, s_ys, i * PAIRS + (t - LONG) // 2 + 1)
                v.tensor_tensor_scan(f2(hs[:, t % LONG]), abar[:, t % RING].rearrange("p m g t -> p (m g t)"), f2(Bx[:, t % RING]),
                                     0.0, ALU.mult, ALU.add).then_inc(s_scan, 1)

            def first():
                scan(0, 0)

            def step(i, par, s, last):
                v.wait_ge(s_scan, i * STATE + (s + 1))
                v.wait_ge(s_cb, i * STATE + (s + 1))
                v.tensor_tensor(hs[:, s % LONG], hs[:, s % LONG],
                                Cb[:, s % RING, :].rearrange("p (a n) -> p a n", a=1).broadcast_to([128, NI, N]),
                                ALU.mult).then_inc(s_hc, 1)
                if not last or s + 1 < STATE:
                    scan(i, s + 1)

            program(v, first, step, pre, post)
            v.wait_ge(s_H, 2 * ROUNDS)

        @block.gpsimd
        def _(g):
            g.wait_ge(s_cst, 2)
            late_roots(g, r1, r12, nh, s_r1)

            def pre(j, par, s, other):
                if s == 10:
                    g.wait_ge(s_dt, j + 1)
                    g.tensor_tensor(f2(dtz[:, par]), f2(dt[:, par]), z[:, par, :], ALU.mult).then_inc(s_dtz, 1)

            def post(p, par, s, other):
                if s == 5:
                    g.wait_ge(s_st, p + 1)
                    g.tensor_tensor(rr[:], ms[:], nh[:, 0:G], ALU.pow).then_inc(s_rr, 1)
                if s == 7:
                    g.wait_ge(s_hf, p + 1)
                    for k in range(2):
                        n = g.tensor_tensor(x1[:, 2 * k:2 * k + 2, :], x1[:, 2 * k:2 * k + 2, :],
                                            H[:, bass.ds(p * G + 2 * k, 2), :], ALU.add)
                    n.then_inc(s_add, 1)

            def inputs(i, par, t):
                g.wait_ge(s_bb, i * STATE + (t + 1))
                at_least(g, s_scan, i * STATE + t - (RING - 1))
                if t % STATE == 0:
                    g.wait_ge(s_dtz, i + t // STATE + 1)
                g.tensor_tensor(Bx[:, t % RING], dtz[:, (par + t // STATE) % 2],
                                Bb[:, t % RING, :].rearrange("p (a n) -> p a n", a=1).broadcast_to([128, NI, N]),
                                ALU.mult).then_inc(s_bx, 1)

            def first():
                inputs(0, 0, 0)
                inputs(0, 0, 1)
                inputs(0, 0, 2)

            def add_pair(i, k):
                g.wait_ge(s_hc, i * STATE + (2 * k + 2))
                a = f2(hs[:, 2 * k % LONG])
                g.tensor_tensor(a, a, f2(hs[:, (2 * k + 1) % LONG]), ALU.add).then_inc(s_pair, 1)

            def step(i, par, s, last):
                if s % 2 == 0 and s > 0:
                    add_pair(i, s // 2 - 1)
                elif s == 0 and (not isinstance(i, int) or i > 0):
                    add_pair(i - 1, PAIRS - 1)
                if not last or s + AHEAD < STATE:
                    inputs(i, par, s + AHEAD)

            program(g, first, step, pre, post, lambda last: add_pair(last, PAIRS - 1))


HEADS = 12
DH = 16
EXPERTS = 8
DFF = 768
KF = DFF // 128
U32 = mybir.dt.uint32


def attention(nc, H, XN, xs, w_qk, w_v, w_ao, rows_c, vecs, eye, W1, w1d):
    K_NORM = 8
    with ExitStack() as ctx:
        def sb(name, shape, dt=F32):
            return ctx.enter_context(nc.sbuf_tensor(name, shape, dt))

        def sem(name):
            return ctx.enter_context(nc.semaphore(name))

        mv = sb("c_mv", [S, B, 2]); r1 = sb("c_r1", [S, B]); r12 = sb("c_r12", [S, B])
        wqk = sb("wqk", [HD, 2, 6, 128]); wv = sb("wv", [HD, 2, D]); wao = sb("wao", [HD, 2, D])
        bro = sb("bro", [S, 2 * D + EXPERTS]); vec = sb("c_vec", [128, V_N]); ident = sb("c_id", [128, 128])
        qb = sb("qb", [128, 3]); nh = sb("c_nh", [S, B]); zero = sb("c_zero", [128, D])
        kB = sb("kB", [128, 2, 3, G, 4, S]); V = sb("V", [S, 2, G, HEADS, DH + 1])
        s_w = sem("c_w"); s_zero = sem("c_zs"); s_cst = sem("c_cst")

        def loads(sp):
            for dst, src in ((wqk, w_qk), (wv, w_v), (wao, w_ao), (vec, vecs), (ident, eye)):
                sp.dma_start(dst[:], src).then_inc(s_w, 16)
            sp.dma_start(bro[:], rows_c.rearrange("(a n) -> a n", a=1).broadcast_to([S, 2 * D + EXPERTS])).then_inc(s_w, 16)

        def fills(g):
            g.memset(zero[:], 0.0).then_inc(s_zero, 1)
            g.memset(V[:], 1.0).then_inc(s_cst, 1)
            g.memset(kB[:], 0.0).then_inc(s_cst, 1)

        row_stats(nc, "c", H, 1e-5, r1, r12, mv, nh, loads, fills)
        x2 = sb("c_x2", [S, G, D]); x2T = sb("x2T", [HD, 2, N])
        qT = sb("qT", [128, 2, 3, N])
        x = sb("c_x", [S, 2, D])
        st = sb("c_st", [S, G, 6]); mg = sb("c_mg", [S, G, 2]); ms = sb("c_ms", [S, G]); rr = sb("c_rr", [S, G])
        mx = sb("mx", [S, 2, HEADS]); E = sb("E", [S, 2, HEADS, S]); PT = sb("PT", [S, 2, HEADS, S])
        rc = sb("rc", [S, 2, HEADS]); ao = sb("ao", [S, 2, HEADS, DH]); aoT = sb("aoT", [HD, 2, 2, S])
        ps = ctx.enter_context(nc.psum_tensor("c_ps", [128, 8, BANK], F32))
        SCORES, FLIP, HEAD_OUT, SIDE0 = 0, 2, 4, 6

        s_e = sem("c_e"); s_qb = sem("c_qb"); s_x2 = sem("c_x2s"); s_tr = sem("c_tr")
        s_x2T = sem("c_x2T"); s_q = sem("c_q"); s_k = sem("c_k"); s_qT = sem("c_qT"); s_kT = sem("c_kT"); s_v = sem("c_v")
        s_V = sem("c_V"); s_s = sem("c_s"); s_mx = sem("c_mx"); s_E = sem("c_E"); s_P = sem("c_P"); s_pt = sem("c_pt"); s_PTa = sem("c_PTa")
        s_PTv = sem("c_PTv"); s_av = sem("c_av"); s_rc = sem("c_rc"); s_ao = sem("c_ao"); s_at = sem("c_at"); s_aoT = sem("c_aoT"); s_op = sem("c_op")
        s_r1 = sem("c_r1s"); s_x = sem("c_xs"); s_xb = sem("c_xb"); s_x3 = sem("c_x3"); s_add = sem("c_add"); s_mg = sem("c_mgs"); s_rr = sem("c_rrs"); s_xn = sem("c_xn")
        s_own = sem("c_own"); s_step = sem("c_step")
        block = ctx.enter_context(nc.Block())

        SIDE_TILES = [("RT0", s_x2T, 2, 1), ("RT1", s_x2T, 2, 2), ("Q0", s_qT, 3, 1), ("Q1", s_qT, 3, 2),
                      ("Q2", s_qT, 3, 3), ("K0", s_kT, 3, 1), ("K1", s_kT, 3, 2), ("K2", s_kT, 3, 3),
                      ("V0", s_V, 2, 1), ("V1", s_V, 2, 2)]
        PLACE = {t[0]: n for n, t in enumerate(SIDE_TILES)}

        def bank(name):
            return SIDE0 + PLACE[name] % 2

        def flat(a):
            return a.rearrange("p h s -> p (h s)")

        def behind(i, q, d):
            r, at = (i, q - d) if q >= d else (i - 1, q - d + G)
            return None if isinstance(r, int) and not 0 <= r < ROUNDS else (r, at)

        def program(engine, step, front, norm=lambda p, q: None):
            for q in range(G):
                front(0, 0, q)

            def round_(i, par, has_front):
                for q in range(G):
                    step(i, par, q)
                    if behind(i, 0, 1):
                        norm(i - 1, q)
                    if has_front:
                        front(i + 1, 1 - par, q)

            round_(0, 0, True)
            with engine.Fori(0, (ROUNDS - 2) // 2) as t:
                for par in (1, 0):
                    round_(t * 2 + (2 - par), par, True)
            round_(ROUNDS - 1, 1, False)
            round_(ROUNDS, 0, False)

        @block.sync
        def _(sp):
            sp.wait_ge(s_zero, 1)
            sp.dma_start(xs.rearrange("(n p) c -> p n c", p=128),
                         zero[:].rearrange("p (a c) -> p a c", a=1).broadcast_to([128, xs.shape[0] // 128, D])).then_inc(s_e, 16)
            for e in range(EXPERTS):
                sp.dma_start(W1[:, :, e, :], w1d[:, :, e, :]).then_inc(s_e, 16)
            sp.wait_ge(s_e, 16 * (1 + EXPERTS))

        @block.tensor
        def _(pe):
            pe.wait_ge(s_w, 96)
            pe.wait_ge(s_cst, 2)

            def free(name, j):
                k = PLACE[name] - 2
                if k >= 0:
                    _, s_free, per, at = SIDE_TILES[k]
                    pe.wait_ge(s_free, j * per + at)

            def turn(src, names, done, j):
                for k in range(2):
                    free(names[k], j)
                    for q in range(G):
                        mm = pe.transpose(ps[0:HD, bank(names[k]), q * S:(q + 1) * S], src[:, q, k * HD:(k + 1) * HD],
                                          ident[0:S, 0:S])
                    mm.then_inc(done, 1)

            def project(name, m, done, j):
                free(name, j)
                for k in range(2):
                    mm = pe.matmul(ps[:, bank(name), 0:N], wqk[:, k, m, :], x2T[:, k, :], start=k == 0, stop=k == 1)
                mm.then_inc(done, 1)

            def front(j, par, q):
                if q == 0:
                    pe.wait_ge(s_x2, j + 1)
                    turn(x2, ("RT0", "RT1"), s_tr, j)
                if q == 1:
                    pe.wait_ge(s_x2T, j * 2 + 2)
                    for m in range(3):
                        project(f"Q{m}", m, s_q, j)
                    project("K0", 3, s_k, j)
                if q == 2:
                    project("K1", 4, s_k, j)
                    project("K2", 5, s_k, j)
                if q == 3:
                    for h in range(2):
                        free(f"V{h}", j)
                        for c in range(2):
                            for k in range(2):
                                mm = pe.matmul(ps[0:S, bank(f"V{h}"), c * D:(c + 1) * D], x2T[:, k, (2 * h + c) * S:(2 * h + c + 1) * S],
                                               wv[:, k, :], start=k == 0, stop=k == 1)
                        mm.then_inc(s_v, 1)

            def step(i, par, q):
                g = i * G + q
                if behind(i, q, 0):
                    if q == 0:
                        pe.wait_ge(s_qT, i * 3 + 3)
                        pe.wait_ge(s_kT, i * 3 + 3)
                    at_least(pe, s_E, g)
                    for h0, h1 in ((0, 4), (4, 6), (6, 8), (8, 12)):
                        m, j = h0 // 4, h0 % 4
                        mm = pe.matmul(ps[0:S, SCORES + h0 // 6, (h0 % 6) * S:(h0 % 6 + h1 - h0) * S],
                                       qT[:, par, m, q * S:(q + 1) * S], kB[:, par, m, q, j:j + h1 - h0, :].rearrange("p h s -> p (h s)"),
                                       start=True, stop=True)
                    mm.then_inc(s_s, 1)
                if behind(i, q, 2):
                    r, c = behind(i, q, 2)
                    vpar = par if q >= 2 else 1 - par
                    pe.wait_ge(s_PTa, r * G + (c + 1))
                    pe.wait_ge(s_PTv, r * G + (c + 1))
                    if c == 0:
                        pe.wait_ge(s_V, r * 2 + 2)
                    at_least(pe, s_x3, i * G + (q - 3))
                    for h in range(HEADS):
                        mm = pe.matmul(ps[0:S, HEAD_OUT + c % 2, h * (DH + 1):(h + 1) * (DH + 1)], PT[:, c % 2, h, :], V[:, vpar, c, h, :],
                                       start=True, stop=True)
                    mm.then_inc(s_av, 1)
                if behind(i, q, 3):
                    r, c = behind(i, q, 3)
                    pe.wait_ge(s_ao, r * G + (c + 1))
                    for k in range(2):
                        mm = pe.transpose(ps[0:HD, HEAD_OUT + c % 2, 256 + k * S:256 + (k + 1) * S],
                                          ao[:, c % 2].rearrange("p h d -> p (h d)")[:, k * HD:(k + 1) * HD], ident[0:S, 0:S])
                    mm.then_inc(s_at, 1)
                if behind(i, q, 1):
                    r, c = behind(i, q, 1)
                    pe.wait_ge(s_P, r * G + (c + 1))
                    for h in range(HEADS):
                        mm = pe.transpose(ps[0:S, FLIP + h // 6, (h % 6) * S:(h % 6 + 1) * S], E[:, c % 2, h, :], ident[0:S, 0:S])
                    mm.then_inc(s_pt, 1)
                if behind(i, q, 3):
                    r, c = behind(i, q, 3)
                    pe.wait_ge(s_aoT, r * G + (c + 1))
                    for k in range(2):
                        mm = pe.matmul(ps[0:S, HEAD_OUT + c % 2, 0:D], aoT[:, c % 2, k, :], wao[:, k, :], start=k == 0, stop=k == 1)
                    mm.then_inc(s_op, 1)

            program(pe, step, front)

        @block.scalar
        def _(act):
            act.wait_ge(s_w, 96)
            act.wait_ge(s_cst, 2)
            act.activation(qb[:], vec[:, V_QB:V_QB + 3], ACT.Copy, scale=0.25).then_inc(s_qb, 1)
            act.wait_ge(s_qb, 1)

            def front(j, par, q):
                if q == 0:
                    for k in range(2):
                        act.wait_ge(s_tr, j * 2 + (k + 1))
                        act.activation(x2T[:, k, :], ps[0:HD, bank(f"RT{k}"), 0:N], ACT.Identity,
                                       bias=vec[0:HD, V_LN1_B + k:V_LN1_B + k + 1],
                                       scale=vec[0:HD, V_LN1_G + k:V_LN1_G + k + 1]).then_inc(s_x2T, 1)
                if q == 1:
                    for m in range(3):
                        act.wait_ge(s_q, j * 3 + (m + 1))
                        act.activation(qT[:, par, m, :], ps[:, bank(f"Q{m}"), 0:N], ACT.Identity, bias=qb[:, m:m + 1],
                                       scale=0.25).then_inc(s_qT, 1)
                for m in {1: (0,), 2: (1, 2)}.get(q, ()):
                    act.wait_ge(s_k, j * 3 + (m + 1))
                    for h in range(4):
                        c = slice(32 * h, 32 * h + 32)
                        a = act.activation(kB[c, par, m, :, h, :], ps[c, bank(f"K{m}"), 0:N].rearrange("p (g s) -> p g s", g=G),
                                           ACT.Identity, bias=vec[c, V_KB + m:V_KB + m + 1])
                    a.then_inc(s_kT, 1)

            def step(i, par, q):
                if behind(i, q, 3):
                    r, c = behind(i, q, 3)
                    act.wait_ge(s_at, r * G + (c + 1))
                    act.activation(aoT[:, c % 2].rearrange("p k s -> p (k s)"), ps[0:HD, HEAD_OUT + c % 2, 256:256 + 2 * S],
                                   ACT.Copy).then_inc(s_aoT, 1)
                if behind(i, q, 1):
                    r, c = behind(i, q, 1)
                    act.wait_ge(s_pt, r * G + (c + 1))
                    act.activation(flat(PT[:, c % 2, 0:6, :]), ps[0:S, FLIP, 0:6 * S], ACT.Copy).then_inc(s_PTa, 1)
                if behind(i, q, 0):
                    act.wait_ge(s_E, i * G + (q + 1))
                    act.activation(flat(E[:, q % 2]), flat(E[:, q % 2]), ACT.Exp).then_inc(s_P, 1)

            program(act, step, front)

        @block.vector
        def _(v):
            v.wait_ge(s_w, 96)
            v.wait_ge(s_cst, 2)

            def rows_of(j, q):
                b = bass.ds(j * G + q, 1)
                return H[:, b, :].rearrange("p a c -> p (a c)"), mv[:, b, 0:1].rearrange("p a c -> p (a c)"), b

            bv = bro[:, 0:D].rearrange("p (a h d) -> p a h d", a=1, h=HEADS)

            def front(j, par, q):
                if q == 3:
                    for h in range(2):
                        v.wait_ge(s_v, j * 2 + (h + 1))
                        for c in range(2):
                            n = v.tensor_tensor(V[:, par, 2 * h + c, :, 0:DH],
                                                ps[0:S, bank(f"V{h}"), c * D:(c + 1) * D].rearrange("p (h d) -> p h d", h=HEADS),
                                                bv[:, 0], ALU.add)
                        n.then_inc(s_V, 1)

            def rows_in(j):
                for c in range(G):
                    h_, m_, b = rows_of(j, c)
                    n = v.tensor_scalar(x2[:, c, :], h_, m_, r12[:, b], ALU.subtract, ALU.mult)
                n.then_inc(s_x2, 1)

            def step(i, par, q):
                if q == 0 and (not isinstance(i, int) or i + 1 < ROUNDS):
                    rows_in(i + 1)
                if behind(i, q, 0):
                    v.wait_ge(s_s, i * G + (q + 1))
                    sc = ps[0:S, SCORES:SCORES + 2, 0:6 * S].rearrange("p a (h s) -> p a h s", h=6)
                    v.tensor_reduce(mx[:, q % 2, :].rearrange("p (a h) -> p a h", a=2), sc, AX.X, ALU.max).then_inc(s_mx, 1)
                    v.wait_ge(s_mx, i * G + (q + 1))
                    at_least(v, s_pt, i * G + (q - 1))
                    for a in range(2):
                        n = v.tensor_tensor(E[:, q % 2, 6 * a:6 * a + 6, :], sc[:, a],
                                            mx[:, q % 2, 6 * a:6 * a + 6].rearrange("p (h a) -> p h a", a=1).broadcast_to([S, 6, S]),
                                            ALU.subtract)
                    n.then_inc(s_E, 1)
                if behind(i, q, 2):
                    r, c = behind(i, q, 2)
                    v.wait_ge(s_av, r * G + (c + 1))
                    o = ps[0:S, HEAD_OUT + c % 2, 0:HEADS * (DH + 1)].rearrange("p (h d) -> p h d", h=HEADS)
                    v.reciprocal(rc[:, c % 2].rearrange("p (h a) -> p h a", a=1), o[:, :, DH:DH + 1]).then_inc(s_rc, 1)
                    v.wait_ge(s_rc, r * G + (c + 1))
                    v.tensor_tensor(ao[:, c % 2], o[:, :, 0:DH], rc[:, c % 2].rearrange("p (h a) -> p h a", a=1).broadcast_to([S, HEADS, DH]),
                                    ALU.mult).then_inc(s_ao, 1)
                if behind(i, q, 1):
                    r, c = behind(i, q, 1)
                    v.wait_ge(s_pt, r * G + (c + 1))
                    v.tensor_copy(flat(PT[:, c % 2, 6:12, :]), ps[0:S, FLIP + 1, 0:6 * S]).then_inc(s_PTv, 1)
                if behind(i, q, 3):
                    r, c = behind(i, q, 3)
                    v.wait_ge(s_op, r * G + (c + 1))
                    v.wait_ge(s_xb, r * G + (c + 1))
                    v.tensor_tensor(XN[:, bass.ds(r * G + c, 1), :].rearrange("p a c -> p (a c)"), x[:, c % 2, :],
                                    ps[0:S, HEAD_OUT + c % 2, 0:D], ALU.add).then_inc(s_x3, 1)
                if behind(i, q, 2):
                    r, c = behind(i, q, 2)
                    h_, m_, b = rows_of(r, c)
                    if isinstance(r, int) and r == 0 and c == 0:
                        v.wait_ge(s_r1, 1)
                    v.tensor_scalar(x[:, c % 2, :], h_, m_, r1[:, b], ALU.subtract, ALU.mult).then_inc(s_x, 1)

            def norm(p, q):
                if q == 2:
                    own = Own(v, s_own, p * K_NORM)
                    v.wait_ge(s_x3, p * G + G)
                    v.sem_inc(s_step, 1)
                    for c in range(G):
                        b = bass.ds(p * G + c, 1)
                        n = own.did(v.bn_stats(st[:, c, :], XN[:, b, :].rearrange("p a c -> p (a c)")))
                    own.need(n)
                    v.sem_inc(s_step, 1)
                    for c in range(G):
                        n = own.did(v.bn_aggr(mg[:, c, :], st[:, c, :]))
                    own.need(n)
                    v.tensor_scalar(ms[:], mg[:, :, 1], 1e-5, None, ALU.add).then_inc(s_mg, 1)
                    assert n == K_NORM, n
                if q == 3:
                    v.wait_ge(s_add, p + 1)
                    v.wait_ge(s_rr, p + 1)
                    for c in range(G):
                        b = bass.ds(p * G + c, 1)
                        x_ = XN[:, b, :].rearrange("p a c -> p (a c)")
                        n = v.tensor_scalar(x_, x_, mg[:, c, 0:1], rr[:, c:c + 1], ALU.subtract, ALU.mult)
                    n.then_inc(s_xn, 1)
                    v.wait_ge(s_xn, p + 1)

            rows_in(0)
            program(v, step, front, norm)

        @block.gpsimd
        def _(g):
            g.wait_ge(s_w, 96)
            g.wait_ge(s_cst, 2)
            late_roots(g, r1, r12, nh, s_r1)

            def step(i, par, q):
                if behind(i, q, 2):
                    r, c = behind(i, q, 2)
                    g.wait_ge(s_x, r * G + (c + 1))
                    g.tensor_tensor(x[:, c % 2, :], x[:, c % 2, :], bro[:, D:2 * D], ALU.add).then_inc(s_xb, 1)

            def norm(p, q):
                if q == 2:
                    g.wait_ge(s_mg, p + 1)
                    g.tensor_tensor(rr[:], ms[:], nh[:, 0:G], ALU.pow).then_inc(s_rr, 1)
                    hb = H[:, bass.ds(p * G, G), :]
                    g.tensor_tensor(hb, hb, XN[:, bass.ds(p * G, G), :], ALU.add).then_inc(s_add, 1)

            program(g, step, lambda j, par, q: None, norm)
            g.wait_ge(s_add, ROUNDS)



NR = -(-B * S // 128)
LAST = B * S - (NR - 1) * 128


def packed(rows, dst):
    full = (NR - 1) * 128
    return ((dst[:, 0:NR - 1, :], rows[0:full, :].rearrange("(n p) c -> p n c", p=128)),
            (dst[0:LAST, NR - 1, :], rows[full:, :]))


def route_logits(nc, XN, XR, L, xn_d, q_d, w_r, rows_c, vecs, eye):
    with ExitStack() as ctx:
        def sb(name, shape, dt=F32):
            return ctx.enter_context(nc.sbuf_tensor(name, shape, dt))

        def sem(name):
            return ctx.enter_context(nc.semaphore(name))

        wr = sb("wr", [HD, 2, EXPERTS]); vec = sb("r_vec", [128, V_N]); ident = sb("r_id", [128, 128]); br = sb("br", [S, EXPERTS])
        xnT = sb("xnT", [HD, 2, 2, N]); zq = sb("zq", [4 * NR, 128])
        s_zq = sem("r_zq"); s_q = sem("r_q"); s_pk = sem("r_pk"); s_xr = sem("r_xr")
        s_w = sem("r_w"); s_tr = sem("r_tr"); s_xnT = sem("r_xnT"); s_lg = sem("r_lg")
        ps = ctx.enter_context(nc.psum_tensor("r_ps", [128, 8, BANK], F32))
        LG = 4
        block = ctx.enter_context(nc.Block())

        @block.sync
        def _(sp):
            for dst, src in ((wr, w_r), (vec, vecs), (ident, eye)):
                sp.dma_start(dst[:], src).then_inc(s_w, 16)
            sp.dma_start(br[:], rows_c[2 * D:].rearrange("(a n) -> a n", a=1).broadcast_to([S, EXPERTS])).then_inc(s_w, 16)
            sp.dma_start(xn_d.rearrange("(b s) c -> s b c", b=B), XN[:]).then_inc(s_pk, 16)
            sp.wait_ge(s_zq, 1)
            sp.dma_start(q_d.rearrange("q (n p) -> (q n) p", p=128), zq[:]).then_inc(s_q, 16)
            sp.wait_ge(s_pk, 16)
            for dst, src in packed(xn_d, XR):
                sp.dma_start(dst, src).then_inc(s_xr, 16)
            sp.wait_ge(s_q, 16)
            sp.wait_ge(s_xr, 32)

        @block.vector
        def _(v):
            v.memset(zq[:], 0.0).then_inc(s_zq, 1)
            v.wait_ge(s_w, 64)
            v.wait_ge(s_lg, 1)
            v.tensor_tensor(L[:], ps[0:S, LG, 0:B * EXPERTS].rearrange("p (b e) -> p b e", b=B),
                            br[:].rearrange("p (a e) -> p a e", a=1).broadcast_to([S, B, EXPERTS]), ALU.add)

        @block.tensor
        def _(pe):
            pe.wait_ge(s_w, 64)

            def turn(i):
                if i >= 2:
                    pe.wait_ge(s_xnT, i - 1)
                for k in range(2):
                    for q in range(G):
                        mm = pe.transpose(ps[0:HD, 2 * (i % 2) + k, q * S:(q + 1) * S], XN[:, i * G + q, k * HD:(k + 1) * HD],
                                          ident[0:S, 0:S])
                mm.then_inc(s_tr, 1)

            turn(0)
            for i in range(ROUNDS):
                if i + 1 < ROUNDS:
                    turn(i + 1)
                pe.wait_ge(s_xnT, i + 1)
                for q in range(G):
                    for k in range(2):
                        mm = pe.matmul(ps[0:S, LG, (i * G + q) * EXPERTS:(i * G + q + 1) * EXPERTS], xnT[:, i % 2, k, q * S:(q + 1) * S],
                                       wr[:, k, :], start=k == 0, stop=k == 1)
            mm.then_inc(s_lg, 1)

        @block.scalar
        def _(act):
            act.wait_ge(s_w, 64)
            for i in range(ROUNDS):
                act.wait_ge(s_tr, i + 1)
                for k in range(2):
                    a = act.activation(xnT[:, i % 2, k, :], ps[0:HD, 2 * (i % 2) + k, 0:N], ACT.Identity,
                                       bias=vec[0:HD, V_LN2_B + k:V_LN2_B + k + 1], scale=vec[0:HD, V_LN2_G + k:V_LN2_G + k + 1])
                a.then_inc(s_xnT, 1)


TILES = B * S * 2 // 128 + EXPERTS - 1


def experts(nc, H, XR, L, W1, w2d, xs, ys, h_d, q_d, b2d, cst, vecs, eye, out):
    with ExitStack() as ctx:
        def sb(name, shape, dt=F32):
            return ctx.enter_context(nc.sbuf_tensor(name, shape, dt))

        def sem(name):
            return ctx.enter_context(nc.semaphore(name))

        BE = B * EXPERTS
        W = [S, B, EXPERTS]
        HR = sb("HR", [128, NR, D])
        slot = sb("slot", [128, 2, NR], U32); gw = sb("gw", [128, 2, NR])
        W2 = sb("W2", [128, KF, EXPERTS, D])
        te = sb("te", [1, TILES + 1], I32)
        ident = sb("d_id", [128, 128]); vec = sb("d_vec", [128, V_N]); b2 = sb("b2", [1, EXPERTS, D]); one = sb("one", [1, 128])
        with ExitStack() as inner:
            def tb(name, shape, dt=F32):
                return inner.enter_context(nc.sbuf_tensor(name, shape, dt))

            c = tb("d_cst", [S, cst.shape[1]])
            m = [tb(f"d_m{k}", [S, B]) for k in range(2)]
            eq = tb("d_eq", W); t = tb("d_t", W); l2 = tb("d_l2", W)
            it = tb("d_it", [S, B]); sel = [tb(f"d_sel{k}", W) for k in range(2)]
            d_ = tb("d_d", [S, B]); e2 = tb("d_e2", [S, B]); M = tb("d_M", W)
            tot = tb("d_tot", [S, EXPERTS, B]); inc = tb("d_inc", [S, EXPERTS, B])
            nf = tb("d_nf", [S, EXPERTS]); ni = tb("d_ni", [S, EXPERTS], I32); nt = tb("d_nt", [S, EXPERTS]); ct = tb("d_ct", [S, EXPERTS])
            sl = tb("d_sl", W); q4 = tb("d_q4", [S, 4, B]); qt = tb("d_qt", [128, S]); qr = tb("d_qr", [4 * NR, 128]); le = tb("d_le", [1, TILES + 1, EXPERTS]); tf = tb("d_tf", [1, TILES + 1])
            ps = inner.enter_context(nc.psum_tensor("d_ps", [128, 4, BANK], F32))
            s_w = sem("d_w"); s_W2 = sem("d_W2"); s_own = sem("d_own"); s_d = sem("d_ds"); s_e2 = sem("d_e2s"); s_M = sem("d_Ms"); s_pe = sem("d_pe")
            s_slot = sem("d_slot"); s_sc = sem("d_sc"); s_h = sem("d_h"); s_hr = sem("d_hr")
            s_q4 = sem("d_q4s"); s_qp = sem("d_qp"); s_qt = sem("d_qt"); s_qd = sem("d_qd"); s_qr = sem("d_qr"); s_rp = sem("d_rp")
            tri, ones, iota_e, keep, iota_t = (c[:, a:b] for a, b in ((0, S), (S, 2 * S), (2 * S, 2 * S + 8),
                                                                      (2 * S + 8, 2 * S + 8 + BE), (2 * S + 8 + BE, 2 * S + 8 + BE + TILES + 1)))
            block = inner.enter_context(nc.Block())

            @block.sync
            def _(sp):
                sp.dma_start(c[:], cst).then_inc(s_w, 16)
                sp.dma_start(ident[:], eye).then_inc(s_w, 16)
                sp.dma_start(vec[:], vecs).then_inc(s_w, 16)
                sp.dma_start(b2[:], b2d.rearrange("(a e) d -> a e d", a=1)).then_inc(s_w, 16)
                sp.dma_start(h_d.rearrange("(b s) c -> s b c", b=B), H[:]).then_inc(s_h, 16)
                sp.wait_ge(s_qt, 1)
                for q in range(4):
                    sp.dma_start(q_d[q, 0:B * S].rearrange("(b s) -> b s", s=S), qt[q * B:(q + 1) * B, :]).then_inc(s_qd, 16)
                sp.wait_ge(s_qd, 64)
                sp.dma_start(qr[:], q_d.rearrange("q (n p) -> (q n) p", p=128)).then_inc(s_qr, 16)
                sp.wait_ge(s_h, 16)
                for dst, src in packed(h_d, HR):
                    sp.dma_start(dst, src).then_inc(s_hr, 16)
                for e in range(EXPERTS):
                    sp.dma_start(W2[:, :, e, :], w2d[:, :, e, :]).then_inc(s_W2, 16)
                sp.wait_ge(s_w, 64)
                sp.wait_ge(s_W2, 16 * EXPERTS)
                sp.wait_ge(s_hr, 32)
                sp.wait_ge(s_qr, 16)

            @block.tensor
            def _(pe):
                pe.wait_ge(s_w, 64)
                pe.wait_ge(s_M, 1)
                mm_ = M[:].rearrange("p b e -> p (b e)")
                pe.matmul(ps[0:S, 0, 0:BE], tri, mm_, start=True, stop=True)
                pe.matmul(ps[0:S, 1, 0:BE], ones, mm_, start=True, stop=True).then_inc(s_pe, 1)
                pe.wait_ge(s_q4, 1)
                pe.transpose(ps[:, 2, 0:S], q4[:].rearrange("p q b -> p (q b)"), ident[0:S, 0:S]).then_inc(s_qp, 1)
                pe.wait_ge(s_qr, 16)
                pe.transpose(ps[:, 3, 0:4 * NR], qr[:], ident[0:4 * NR, 0:4 * NR]).then_inc(s_rp, 1)

            @block.scalar
            def _(act):
                act.wait_ge(s_d, 1)
                act.activation(e2[:], d_[:], ACT.Exp).then_inc(s_e2, 1)

            @block.vector
            def _(v):
                own = Own(v, s_own)

                def do(ins):
                    own.need(own.did(ins))

                def col(a):
                    return a.rearrange("p (b a) -> p b a", a=1).broadcast_to(W)

                ie = iota_e.rearrange("p (a e) -> p a e", a=1).broadcast_to(W)
                v.wait_ge(s_w, 64)
                src = L
                for k in range(2):
                    do(v.tensor_reduce(m[k][:], src[:], AX.X, ALU.max))
                    do(v.tensor_tensor(eq[:], src[:], col(m[k][:]), ALU.is_equal))
                    do(v.scalar_tensor_tensor(t[:], eq[:], -float(EXPERTS), ie, ALU.mult, ALU.add))
                    do(v.tensor_reduce(it[:], t[:], AX.X, ALU.min))
                    do(v.tensor_tensor(sel[k][:], t[:], col(it[:]), ALU.is_equal))
                    if k == 0:
                        do(v.scalar_tensor_tensor(l2[:], sel[0][:], -3.0e38, L[:], ALU.mult, ALU.add))
                        src = l2
                do(v.tensor_tensor(M[:], sel[0][:], sel[1][:], ALU.add))
                v.sem_inc(s_M, 1)
                do(v.tensor_tensor(d_[:], m[1][:], m[0][:], ALU.subtract))
                v.sem_inc(s_d, 1)
                v.wait_ge(s_e2, 1)
                do(v.tensor_scalar(d_[:], e2[:], 1.0, None, ALU.add))
                do(v.reciprocal(q4[:, 2, :], d_[:]))
                do(v.tensor_tensor(q4[:, 3, :], e2[:], q4[:, 2, :], ALU.mult))
                v.wait_ge(s_pe, 1)
                do(v.tensor_copy(tot[:], ps[0:S, 1, 0:BE].rearrange("p (b e) -> p e b", e=EXPERTS)))
                do(v.tensor_tensor_scan(inc[:].rearrange("p e b -> p (e b)"), keep, tot[:].rearrange("p e b -> p (e b)"),
                                        0.0, ALU.mult, ALU.add))
                do(v.tensor_scalar(ni[:], inc[:, :, B - 1], 127.0, None, ALU.add))
                do(v.tensor_scalar(ni[:], ni[:], 7, None, ALU.arith_shift_right))
                do(v.tensor_copy(nt[:], ni[:]))
                do(v.tensor_tensor_scan(ct[:], ones[:, 0:EXPERTS], nt[:], 0.0, ALU.mult, ALU.add))
                do(v.tensor_tensor(inc[:], inc[:], tot[:], ALU.subtract))
                do(v.tensor_tensor(nf[:], ct[:], nt[:], ALU.subtract))
                do(v.tensor_scalar(nf[:], nf[:], 128.0, None, ALU.mult))
                do(v.tensor_tensor(inc[:], inc[:], nf[:].rearrange("p (e a) -> p e a", a=1).broadcast_to([S, EXPERTS, B]), ALU.add))
                do(v.tensor_tensor(sl[:], ps[0:S, 0, 0:BE].rearrange("p (b e) -> p b e", e=EXPERTS), inc[:].rearrange("p e b -> p b e"), ALU.add))
                for k in range(2):
                    do(v.tensor_tensor(t[:], sel[k][:], sl[:], ALU.mult))
                    do(v.tensor_reduce(q4[:, k, :], t[:], AX.X, ALU.add))
                v.sem_inc(s_q4, 1)
                v.wait_ge(s_qp, 1)
                v.tensor_copy(qt[:], ps[:, 2, 0:S]).then_inc(s_qt, 1)
                TW = [1, TILES + 1, EXPERTS]
                do(v.tensor_tensor(le[:], ct[0:1].rearrange("p (a e) -> p a e", a=1).broadcast_to(TW),
                                   iota_t[0:1].rearrange("p (t a) -> p t a", a=1).broadcast_to(TW), ALU.is_le))
                do(v.tensor_reduce(tf[:], le[:], AX.X, ALU.add))
                do(v.tensor_scalar(te[:], tf[:], float(EXPERTS - 1), None, ALU.min))
                v.wait_ge(s_rp, 1)
                r_ = ps[:, 3, 0:4 * NR].rearrange("p (q n) -> p q n", q=4)
                do(v.tensor_copy(slot[:], r_[:, 0:2]))
                v.sem_inc(s_slot, 1)
                do(v.tensor_copy(gw[:], r_[:, 2:4]))

            @block.gpsimd
            def _(g):
                g.wait_ge(s_slot, 1)
                for n in range(NR):
                    p = LAST if n == NR - 1 else 128
                    for k in range(2):
                        g.indirect_dma_start(out=xs, out_offset=bass.IndirectOffsetOnAxis(ap=slot[0:p, k, n:n + 1], axis=0),
                                             in_=XR[0:p, n, :], in_offset=None).then_inc(s_sc, 16)
                g.wait_ge(s_sc, 16 * 2 * NR)

        with ExitStack() as inner:
            def tb(name, shape, dt=F32):
                return inner.enter_context(nc.sbuf_tensor(name, shape, dt))

            xg = tb("xg", [128, 2, D]); xT = tb("xT", [HD + 1, 2, 2, 128]); hb = tb("hb", [128, 2, DFF])
            hT = tb("hT_", [128, 2, KF, 128]); yt = tb("yt", [128, 2, D])
            ps = inner.enter_context(nc.psum_tensor("e_ps", [128, 8, BANK], F32))
            s_xg = [sem("e_xg0"), sem("e_xg1")]; s_st = [sem("e_st0"), sem("e_st1")]
            s_cst = sem("e_cst"); s_tx = sem("e_tx"); s_xT = sem("e_xT"); s_h = sem("e_h"); s_ge = sem("e_ge")
            s_ht = sem("e_ht"); s_hT = sem("e_hT"); s_y = sem("e_y"); s_yt = sem("e_yt")
            block = inner.enter_context(nc.Block())

            def program(engine, step):
                for j in range(2):
                    step(j, j)
                with engine.Fori(1, TILES // 2 - 1) as i:
                    for p in range(2):
                        step(i * 2 + p, p)
                for j in range(TILES - 2, TILES + 1):
                    step(j, j % 2)

            def is_tile(j):
                return not isinstance(j, int) or 0 <= j < TILES

            def per_slot(j, p):
                return (j // 2 + 1) * 16 if isinstance(j, int) else (j - p) * 8 + 16

            @block.sync
            def _(sp):
                def load(j, p):
                    sp.dma_start(xg[:, p, :], xs[bass.ds(j * 128, 128), :]).then_inc(s_xg[p], 16)

                def step(j, p):
                    if is_tile(j):
                        sp.wait_ge(s_yt, j + 1)
                        sp.dma_start(ys[bass.ds(j * 128, 128), :], yt[:, p, :]).then_inc(s_st[p], 16)
                    if is_tile(j + 4):
                        sp.wait_ge(s_tx, j + 3)
                        load(j + 4, p)

                load(0, 0)
                load(1, 1)
                for j in (2, 3):
                    sp.wait_ge(s_tx, j - 1)
                    load(j, j % 2)
                for j in range(2):
                    step(j, j)
                with sp.Fori(1, TILES // 2 - 2) as i:
                    for p in range(2):
                        step(i * 2 + p, p)
                for j in range(TILES - 4, TILES):
                    step(j, j % 2)
                for p in range(2):
                    sp.wait_ge(s_st[p], 16 * (TILES // 2))

            @block.tensor
            def _(pe):
                pe.wait_ge(s_cst, 2)

                def expert(j):
                    return pe.value_load(te[0:1, bass.ds(j, 1)] if not isinstance(j, int) else te[0:1, j:j + 1],
                                         min_val=0, max_val=EXPERTS - 1)

                def turn(j, p):
                    pe.wait_ge(s_xg[p], per_slot(j, p))
                    at_least(pe, s_xT, j)
                    for k in range(2):
                        mm = pe.transpose(ps[0:HD, 0, k * 128:(k + 1) * 128], xg[:, p, k * HD:(k + 1) * HD], ident[:])
                    mm.then_inc(s_tx, 1)

                def up(j, p, e):
                    pe.wait_ge(s_xT, j + 1)
                    at_least(pe, s_ge, j - 1)
                    for h in range(2):
                        for k in range(2):
                            c_ = slice(0, HD + k)
                            mm = pe.matmul(ps[:, 1 + 2 * p + h, 0:384], xT[c_, p, k, :],
                                           W1[c_, k, bass.ds(e, 1), h * 384:(h + 1) * 384].rearrange("p a n -> p (a n)"),
                                           start=k == 0, stop=k == 1)
                    mm.then_inc(s_h, 1)

                def flip(j, p):
                    pe.wait_ge(s_ge, j + 1)
                    at_least(pe, s_hT, j)
                    for k in range(KF):
                        mm = pe.transpose(ps[:, 5 + k // 3, (k % 3) * 128:(k % 3 + 1) * 128], hb[:, p, k * 128:(k + 1) * 128], ident[:])
                    mm.then_inc(s_ht, 1)

                def down(j, p, e, between):
                    pe.wait_ge(s_hT, j + 1)
                    at_least(pe, s_yt, j)
                    pe.matmul(ps[:, 7, 0:D], one[:], b2[:, bass.ds(e, 1), :].rearrange("p a n -> p (a n)"), start=True, stop=False)
                    for k in range(KF):
                        if k == KF // 2:
                            between()
                        mm = pe.matmul(ps[:, 7, 0:D], hT[:, p, k, :], W2[:, k, bass.ds(e, 1), :].rearrange("p a n -> p (a n)"),
                                       start=False, stop=k == KF - 1)
                    mm.then_inc(s_y, 1)

                def step(j, p):
                    e_up = expert(j + 1) if is_tile(j + 1) else None
                    e_down = expert(j - 1) if is_tile(j - 1) else None
                    if is_tile(j + 1):
                        up(j + 1, 1 - p, e_up)
                    if is_tile(j):
                        flip(j, p)

                    def next_turn():
                        if is_tile(j + 2):
                            turn(j + 2, p)

                    if is_tile(j - 1):
                        down(j - 1, 1 - p, e_down, next_turn)
                    else:
                        next_turn()

                turn(0, 0)
                turn(1, 1)
                up(0, 0, expert(0))
                program(pe, step)

            @block.scalar
            def _(act):
                act.wait_ge(s_cst, 2)

                def affine(j, p):
                    act.wait_ge(s_tx, j + 1)
                    for k in range(2):
                        a = act.activation(xT[0:HD, p, k, :], ps[0:HD, 0, k * 128:(k + 1) * 128], ACT.Identity,
                                           bias=vec[0:HD, V_LN2_B + k:V_LN2_B + k + 1], scale=vec[0:HD, V_LN2_G + k:V_LN2_G + k + 1])
                    a.then_inc(s_xT, 1)

                def hidden(j, p):
                    act.wait_ge(s_h, j + 1)
                    act.activation(hb[:, p, :].rearrange("p (a n) -> p a n", a=2), ps[:, 1 + 2 * p:3 + 2 * p, 0:384], ACT.Gelu).then_inc(s_ge, 1)

                def step(j, p):
                    if is_tile(j + 1):
                        hidden(j + 1, 1 - p)
                    if is_tile(j + 2):
                        affine(j + 2, p)

                affine(0, 0)
                affine(1, 1)
                hidden(0, 0)
                program(act, step)

            @block.vector
            def _(v):
                v.memset(xT[HD:HD + 1], 1.0).then_inc(s_cst, 1)
                v.memset(one[:], 1.0).then_inc(s_cst, 1)

                def step(j, p):
                    if is_tile(j):
                        v.wait_ge(s_ht, j + 1)
                        v.tensor_copy(hT[:, p].rearrange("p (a k) n -> p a (k n)", a=2), ps[:, 5:7, 0:384]).then_inc(s_hT, 1)
                    if is_tile(j - 1):
                        v.wait_ge(s_y, j)
                        if not isinstance(j, int) or j >= 3:
                            v.wait_ge(s_st[1 - p], per_slot(j - 1, 1 - p) - 16)
                        v.tensor_copy(yt[:, 1 - p, :], ps[:, 7, 0:D]).then_inc(s_yt, 1)

                program(v, step)

        with ExitStack() as inner:
            def tb(name, shape, dt=F32):
                return inner.enter_context(nc.sbuf_tensor(name, shape, dt))

            gy = tb("gy", [128, G, 2, D]); o = tb("o_", [128, G, D])
            used = [len(range(q, NR, G)) for q in range(G)]
            s_g = [sem(f"g_g{q}") for q in range(G)]; s_acc = sem("g_acc"); s_o = sem("g_o"); s_out = [sem(f"g_out{q}") for q in range(G)]
            block = inner.enter_context(nc.Block())

            def tile(n):
                return LAST if n == NR - 1 else 128, n % G

            @block.gpsimd
            def _(g):
                for n in range(NR):
                    p, q = tile(n)
                    if n >= G:
                        g.wait_ge(s_o, n - G + 1)
                    for k in range(2):
                        g.indirect_dma_start(out=gy[0:p, q, k, :], out_offset=None, in_=ys,
                                             in_offset=bass.IndirectOffsetOnAxis(ap=slot[0:p, k, n:n + 1], axis=0)).then_inc(s_g[q], 16)

            @block.vector
            def _(v):
                for n in range(NR):
                    p, q = tile(n)
                    v.wait_ge(s_g[q], 32 * (n // G + 1))
                    v.scalar_tensor_tensor(gy[0:p, q, 0, :], gy[0:p, q, 0, :], gw[0:p, 0, n:n + 1], HR[0:p, n, :], ALU.mult, ALU.add).then_inc(s_acc, 1)
                    v.wait_ge(s_acc, n + 1)
                    if n >= G:
                        v.wait_ge(s_out[q], 16 * (n // G))
                    v.scalar_tensor_tensor(o[0:p, q, :], gy[0:p, q, 1, :], gw[0:p, 1, n:n + 1], gy[0:p, q, 0, :], ALU.mult, ALU.add).then_inc(s_o, 1)

            @block.sync
            def _(sp):
                flat = out.rearrange("b s c -> (b s) c")
                for n in range(NR):
                    p, q = tile(n)
                    sp.wait_ge(s_o, n + 1)
                    sp.dma_start(flat[n * 128:n * 128 + p, :], o[0:p, q, :]).then_inc(s_out[q], 16)
                for q in range(G):
                    sp.wait_ge(s_out[q], 16 * used[q])
def _halves(a):
    import numpy as np
    a = np.asarray(a).reshape(192, -1)
    out = np.zeros((128, 2 * a.shape[1]), a.dtype)
    out[0:96, 0:a.shape[1]] = a[0:96]
    out[0:96, a.shape[1]:] = a[96:192]
    return out


def _mixed(loc, g):
    import numpy as np
    loc, g = np.asarray(loc).reshape(192, -1), np.asarray(g).reshape(192, -1)
    return np.stack([loc[0:128], np.concatenate([loc[128:192], g[128:192]]), g[0:128]], axis=1)


def _haar():
    import numpy as np
    bands, pixels = np.arange(256), np.arange(256)
    odd = np.zeros((256, 256), np.int64)
    for level in range(4):
        pair = (bands >> (2 * (3 - level))) & 3
        wide, high = pair >> 1, pair & 1
        row, col = (pixels // 16 >> level) & 1, (pixels % 16 >> level) & 1
        odd = odd + high[:, None] * row[None, :] + wide[:, None] * col[None, :]
    return np.where(odd % 2 == 1, -0.0625, 0.0625).astype(np.float32)


def _heads(a):
    import numpy as np
    a = np.asarray(a).reshape(12, 16, -1)
    out = np.zeros((12, 32, a.shape[2]), a.dtype)
    out[:, 0:16] = a
    return out.reshape(384, -1)


def _layout(x):
    import numpy as np
    t = {k.replace("L0_", ""): np.asarray(v) for k, v in x.items()}
    f32 = np.float32
    a = {}
    a["xcol"] = t["x"].reshape(32, 3, 7, 16, 7, 16).transpose(1, 3, 5, 0, 2, 4).reshape(768, 1568)
    a["w_pl"] = t["tok_pl_w"].reshape(192, 768).T
    a["w_pg"] = t["tok_pg_w1"].reshape(192, 256, 3).transpose(1, 2, 0)
    a["had"] = _haar()
    a["pw_mix"] = _mixed(t["tok_pl_pw"].reshape(192, 192).T, t["tok_pg_pw"].reshape(192, 192).T)
    a["w96"] = np.stack([t[n].reshape(192, 192).T.reshape(2, 96, 192)
                         for n in ("tok_pg_w2", "tok_f1_pw", "tok_f2_pw", "tok_f3_pw")]).transpose(2, 0, 1, 3)
    thirds = lambda v: v.reshape(3, 128).T
    bq, bk, bv = t["ffn_in_proj_b"].reshape(3, 192)
    cols = [_mixed(t["tok_pl_b"], t["tok_pg_b1"])[:, :, 0], _mixed(t["tok_pl_dw"], t["tok_pg_dw"]).reshape(128, 27)]
    cols += [_halves(t[n]) for n in ("tok_f1_dw", "tok_f2_dw", "tok_f3_dw", "tok_pl_pwb", "tok_pg_pwb", "tok_pg_b2",
                                     "tok_f1_pwb", "tok_f2_pwb", "tok_alpha", "attn_w_norm1", "attn_w_ffn_norm",
                                     "ffn_ln1_g", "ffn_ln1_b", "ffn_ln2_g", "ffn_ln2_b")]
    cols += [thirds(t["attn_b_dt"]), thirds(t["attn_D_skip"]), thirds(_heads(bq)), thirds(_heads(bk))]
    a["vecs"] = np.concatenate(cols, axis=1)
    a["pwb_row"], a["lng_row"], a["lnb_row"] = t["tok_f3_pwb"], t["tok_ln_g"], t["tok_ln_b"]
    a["cls_row"] = np.broadcast_to(t["tok_cls"].reshape(1, 192), (32, 192))
    a["txt"] = t["txt"]
    rows = lambda w, p: w.T.reshape(-1, p, w.shape[0]).transpose(1, 0, 2)
    a["w_zg"] = np.stack([rows(t["attn_W_in"], 96), rows(t["attn_W_gate"], 96)], axis=2)
    wx = t["attn_W_xproj"]
    a["w_x"] = rows(np.concatenate([wx[0:96]] + [wx[96:128]] * 3), 128)
    a["w_dt"] = t["attn_W_dt"].T
    a["a_log"] = t["attn_A_log"].reshape(3, 128, 16).transpose(1, 0, 2)
    a["w_o"] = rows(t["attn_W_out"], 128)
    a["w_ug"] = np.stack([rows(t["attn_W_gate_ffn"], 96), rows(t["attn_W_up"], 96)], axis=2)
    a["w_dn"] = rows(t["attn_W_down"], 128)
    a["onehot"] = np.tile(np.eye(32, dtype=f32), (3, 1))
    a["eye"] = np.eye(128, dtype=f32)
    wq, wk, wv = t["ffn_in_proj_w"].reshape(3, 192, 192)
    a["w_qk"] = rows(np.concatenate([_heads(wq), _heads(wk)]), 96).reshape(96, 2, 6, 128)
    a["w_v"], a["w_ao"], a["w_r"] = rows(wv, 96), rows(t["ffn_out_proj_w"], 96), rows(t["ffn_router_w"], 96)
    a["rows_c"] = np.concatenate([bv, t["ffn_out_proj_b"], t["ffn_router_b"]])
    w1 = np.zeros((97, 2, 8, 768), f32)
    w1[0:96] = t["ffn_w1"].reshape(8, 2, 96, 768).transpose(2, 1, 0, 3)
    w1[96, 1] = t["ffn_b1"]
    a["w1d"] = w1
    a["w2d"] = t["ffn_w2"].reshape(8, 6, 128, 192).transpose(2, 1, 0, 3)
    a["b2d"] = t["ffn_b2"]
    s = 82
    before = np.triu(np.ones((s, s), f32), 1)
    first = np.ones((8, 32), f32)
    first[:, 0] = 0
    wide = lambda v: np.broadcast_to(v.reshape(1, -1), (s, v.size))
    a["cst"] = np.concatenate([before, np.ones((s, s), f32), wide(np.arange(8, dtype=f32)), wide(first),
                               wide(np.arange(49, dtype=f32))], axis=1)
    return {k: np.ascontiguousarray(v) for k, v in a.items()}


def program(nc, io):
    xs = nc.dram_tensor("expert_in", (TILES * 128, D), F32, kind="Internal").ap()
    ys = nc.dram_tensor("expert_out", (TILES * 128, D), F32, kind="Internal").ap()
    xn_d = nc.dram_tensor("packed_normed", (B * S, D), F32, kind="Internal").ap()
    h_d = nc.dram_tensor("packed_rows", (B * S, D), F32, kind="Internal").ap()
    q_d = nc.dram_tensor("packed_slots", (4, NR * 128), F32, kind="Internal").ap()
    with nc.sbuf_tensor("H", [S, B, D], F32) as H:
        tokenizer(nc, H, io["xcol"], io["w_pl"], io["w_pg"], io["had"], io["pw_mix"], io["w96"], io["vecs"],
                  io["pwb_row"], io["lng_row"], io["lnb_row"], io["cls_row"], io["txt"])
        mamba(nc, H, io["w_zg"], io["w_x"], io["w_dt"], io["a_log"], io["w_o"], io["w_ug"], io["w_dn"], io["vecs"],
              io["onehot"], io["eye"])
        with (nc.sbuf_tensor("XN", [S, B, D], F32) as XN, nc.sbuf_tensor("L", [S, B, EXPERTS], F32) as L,
              nc.sbuf_tensor("W1", [HD + 1, 2, EXPERTS, DFF], F32) as W1):
            attention(nc, H, XN, xs, io["w_qk"], io["w_v"], io["w_ao"], io["rows_c"], io["vecs"], io["eye"],
                      W1, io["w1d"])
            with nc.sbuf_tensor("XR", [128, NR, D], F32) as XR:
                route_logits(nc, XN, XR, L, xn_d, q_d, io["w_r"], io["rows_c"], io["vecs"], io["eye"])
                experts(nc, H, XR, L, W1, io["w2d"], xs, ys, h_d, q_d, io["b2d"], io["cst"], io["vecs"], io["eye"], io["out"])


def kernel(**inputs):
    import concourse.bacc as _bacc
    from concourse.bass_utils import run_bass_kernel_spmd as _run

    nc = _bacc.Bacc("TRN2", target_bir_lowering=False, num_devices=1)
    arrays = _layout(inputs)
    io = {name: nc.dram_tensor(f"in_{name}", a.shape, mybir.dt.from_np(a.dtype), kind="ExternalInput").ap()
          for name, a in arrays.items()}
    io["out"] = nc.dram_tensor("out_0", (B, S, D), F32, kind="ExternalOutput").ap()
    program(nc, io)
    r = _run(nc, [{f"in_{name}": a for name, a in arrays.items()}], core_ids=[0])
    return r.results[0]["out_0"]
```
